# Optimizing a Trainium2 kernel written in Bass

```python
import numpy as np
import jax
import jax.numpy as jnp

def _softmax(x, axis=-1):
    return jax.nn.softmax(x, axis=axis)

def _gelu(x):
    return jax.nn.gelu(x, approximate=True)

def _silu(x):
    return jax.nn.silu(x)

def _sigmoid(x):
    return jax.nn.sigmoid(x)

def _layernorm(x, axis=-1, eps=1e-05):
    m = jnp.mean(x, axis=axis, keepdims=True)
    v = jnp.var(x, axis=axis, keepdims=True)
    return (x - m) / jnp.sqrt(v + eps)

def _scatter_add(tgt, idx, src, axis=0):
    return tgt.at[idx].add(src)

def _segment_sum(src, seg, n):
    return jax.ops.segment_sum(src, seg, n)
kernel_name = 'mk_hybrid_d2_jaxref_r8_a19d69'

def setup_inputs(seed: int=0):
    np.random.seed(seed)
    _w = jnp.asarray

    def _L0_attn_a_setup():
        import jax, jax.numpy as jnp
        import numpy as np
        B, SEQ, DIM = (2, 256, 128)
        H = 16
        DH = DIM // H
        LAT = 64
        CTX = SEQ - LAT
        SCALE = DH ** (-0.5)
        LN_EPS = 1e-05

        def _rotary_cos_sin(n):
            inv_freq = 1.0 / 10000.0 ** (jnp.arange(0, DH, 2, dtype=jnp.float32) / DH)
            freqs = jnp.arange(n, dtype=jnp.float32)[:, None] * inv_freq[None, :]
            emb = jnp.concatenate([freqs, freqs], axis=-1)
            return (jnp.cos(emb), jnp.sin(emb))

        def _rotate_half(t):
            t1, t2 = jnp.split(t, 2, axis=-1)
            return jnp.concatenate([-t2, t1], axis=-1)

        def _layernorm(t, g, b):
            m = jnp.mean(t, axis=-1, keepdims=True)
            v = jnp.var(t, axis=-1, keepdims=True)
            return (t - m) / jnp.sqrt(v + LN_EPS) * g + b
        key = jax.random.key(seed)
        ks = jax.random.split(key, 4)
        x = jax.random.normal(ks[0], (B, SEQ, DIM), dtype=jnp.float32)
        Wq = jax.random.normal(ks[1], (DIM, DIM), dtype=jnp.float32) * 0.02
        Wkv = jax.random.normal(ks[2], (DIM, DIM), dtype=jnp.float32) * 0.02
        Wo = jax.random.normal(ks[3], (DIM, DIM), dtype=jnp.float32) * 0.02
        bo = jnp.zeros((DIM,), dtype=jnp.float32)
        ln_g = jnp.ones((DH,), dtype=jnp.float32)
        ln_b = jnp.zeros((DH,), dtype=jnp.float32)
        return {'x': x, 'Wq': Wq, 'Wkv': Wkv, 'Wo': Wo, 'bo': bo, 'ln_g': ln_g, 'ln_b': ln_b}
    _L0_attn_a_in = _L0_attn_a_setup()

    def _L0_attn_b_setup():
        import jax, jax.numpy as jnp
        import numpy as np
        SEQ, BATCH, HIDDEN = (256, 2, 128)
        NUM_HEADS, HEAD_DIM = (16, 64)
        LN_EPS = 1e-06
        NEG_INF = -10000000000.0
        key = jax.random.key(seed)
        k1, k2, k3 = jax.random.split(key, 3)
        inputs_q = jax.random.normal(k1, (SEQ, BATCH, HIDDEN), dtype=jnp.float32)
        ln_scale = jnp.ones((HIDDEN,), dtype=jnp.float32)
        ln_bias = jnp.zeros((HIDDEN,), dtype=jnp.float32)
        qkv_kernel = jax.random.normal(k2, (HIDDEN, 3, NUM_HEADS * HEAD_DIM), dtype=jnp.float32) / np.sqrt(HIDDEN).astype(np.float32)
        out_kernel = jax.random.normal(k3, (NUM_HEADS * HEAD_DIM, HIDDEN), dtype=jnp.float32) / np.sqrt(NUM_HEADS * HEAD_DIM).astype(np.float32)
        return {'inputs_q': inputs_q, 'ln_scale': ln_scale, 'ln_bias': ln_bias, 'qkv_kernel': qkv_kernel, 'out_kernel': out_kernel}
    _L0_attn_b_in = _L0_attn_b_setup()

    def _L0_ffn_setup():
        import jax, jax.numpy as jnp
        import numpy as np
        N_EMBD = 128
        EXPERT_SIZES = [(4, 128), (4, 256)]
        TOP_K = 2
        B, S = (1, 256)
        WIDTHS = []
        for count, size in EXPERT_SIZES:
            WIDTHS += [size] * count
        OFFSETS = np.concatenate([[0], np.cumsum(WIDTHS)]).astype(np.int64)
        E = len(WIDTHS)
        TOTAL_W = int(OFFSETS[-1])
        MAX_W = max(WIDTHS)

        def _stack_experts(w1, w2):
            W1e, W2e = ([], [])
            for e in range(E):
                off, wd = (int(OFFSETS[e]), WIDTHS[e])
                pad = MAX_W - wd
                W1e.append(jnp.pad(w1[:, off:off + wd], ((0, 0), (0, pad))))
                W2e.append(jnp.pad(w2[off:off + wd, :], ((0, pad), (0, 0))))
            return (jnp.stack(W1e), jnp.stack(W2e))
        key = jax.random.key(seed)
        k1, k2, k3, k4 = jax.random.split(key, 4)
        x = jax.random.normal(k1, (B, S, N_EMBD), jnp.float32)
        router_w = jax.random.normal(k2, (E, N_EMBD), jnp.float32) * 0.02
        w1 = jax.random.truncated_normal(k3, -3.0, 3.0, (N_EMBD, TOTAL_W), jnp.float32) * 0.02
        w2 = jax.random.truncated_normal(k4, -3.0, 3.0, (TOTAL_W, N_EMBD), jnp.float32) * 0.02
        return {'x': x, 'router_w': router_w, 'w1': w1, 'w2': w2}
    _L0_ffn_in = _L0_ffn_setup()

    def _L1_attn_a_setup():
        import jax, jax.numpy as jnp
        import numpy as np
        EXPAND = 2
        key = jax.random.key(seed)
        k1, k2, k3 = jax.random.split(key, 3)
        n, b, d = (512, 8, 128)
        x = jax.random.normal(k1, (n, b, d), dtype=jnp.float32)
        lower_bound = jnp.zeros((d,), dtype=jnp.float32)
        W_in = jax.random.normal(k2, (d, 3 * d), dtype=jnp.float32) / np.sqrt(d)
        W_out = jax.random.normal(k3, (d, d), dtype=jnp.float32) / np.sqrt(d)
        return {'x': x, 'lower_bound': lower_bound, 'W_in': W_in, 'W_out': W_out}
    _L1_attn_a_in = _L1_attn_a_setup()

    def _L1_attn_b_setup():
        import math
        import jax, jax.numpy as jnp
        import numpy as np
        N_EMBD = 128
        N_HEAD = 16
        HEAD_DIM = N_EMBD // N_HEAD

        def alibi_slopes(n_heads):
            start = 2.0 ** (-2.0 ** (-(math.log2(n_heads) - 3)))
            return np.array([start * start ** i for i in range(n_heads)], dtype=np.float32)
        key = jax.random.key(seed)
        k1, k2, k3 = jax.random.split(key, 3)
        B, T, C = (2, 256, N_EMBD)
        x = jax.random.normal(k1, (B, T, C), dtype=jnp.float32)
        w_attn = jax.random.normal(k2, (3 * C, C), dtype=jnp.float32) * (1.0 / math.sqrt(C))
        w_proj = jax.random.normal(k3, (C, C), dtype=jnp.float32) * (1.0 / math.sqrt(C))
        return {'x': x, 'w_attn': w_attn, 'w_proj': w_proj}
    _L1_attn_b_in = _L1_attn_b_setup()

    def _L1_ffn_setup():
        import jax, jax.numpy as jnp
        import numpy as np
        B, S, D_MODEL, D_FF, E, R, TOP_K = (4, 256, 128, 512, 8, 16, 2)
        key = jax.random.key(seed)
        ks = jax.random.split(key, 9)
        sd = 1.0 / np.sqrt(D_MODEL)
        return {'hidden_states': jax.random.normal(ks[0], (B, S, D_MODEL), jnp.float32), 'wi': jax.random.normal(ks[1], (D_FF, D_MODEL), jnp.float32) * sd, 'bi': jax.random.normal(ks[2], (D_FF,), jnp.float32) * 0.01, 'wo': jax.random.normal(ks[3], (D_MODEL, D_FF), jnp.float32) * (1.0 / np.sqrt(D_FF)), 'bo': jax.random.normal(ks[4], (D_MODEL,), jnp.float32) * 0.01, 'lora_A': jax.random.normal(ks[5], (E, R, D_MODEL), jnp.float32) * sd, 'lora_B': jax.random.normal(ks[6], (E, D_FF, R), jnp.float32) * 0.02, 'gate_w': jax.random.normal(ks[7], (E, D_MODEL), jnp.float32) * sd, 'gate_b': jax.random.normal(ks[8], (E,), jnp.float32) * 0.01}
    _L1_ffn_in = _L1_ffn_setup()
    _d = {'L0_attn_a_x': _L0_attn_a_in['x'], 'L0_attn_a_Wq': _L0_attn_a_in['Wq'], 'L0_attn_a_Wkv': _L0_attn_a_in['Wkv'], 'L0_attn_a_Wo': _L0_attn_a_in['Wo'], 'L0_attn_a_bo': _L0_attn_a_in['bo'], 'L0_attn_a_ln_g': _L0_attn_a_in['ln_g'], 'L0_attn_a_ln_b': _L0_attn_a_in['ln_b'], 'L0_attn_b_ln_scale': _L0_attn_b_in['ln_scale'], 'L0_attn_b_ln_bias': _L0_attn_b_in['ln_bias'], 'L0_attn_b_qkv_kernel': _L0_attn_b_in['qkv_kernel'], 'L0_attn_b_out_kernel': _L0_attn_b_in['out_kernel'], 'L0_ffn_router_w': _L0_ffn_in['router_w'], 'L0_ffn_w1': _L0_ffn_in['w1'], 'L0_ffn_w2': _L0_ffn_in['w2'], 'L1_attn_a_lower_bound': _L1_attn_a_in['lower_bound'], 'L1_attn_a_W_in': _L1_attn_a_in['W_in'], 'L1_attn_a_W_out': _L1_attn_a_in['W_out'], 'L1_attn_b_w_attn': _L1_attn_b_in['w_attn'], 'L1_attn_b_w_proj': _L1_attn_b_in['w_proj'], 'L1_ffn_wi': _L1_ffn_in['wi'], 'L1_ffn_bi': _L1_ffn_in['bi'], 'L1_ffn_wo': _L1_ffn_in['wo'], 'L1_ffn_bo': _L1_ffn_in['bo'], 'L1_ffn_lora_A': _L1_ffn_in['lora_A'], 'L1_ffn_lora_B': _L1_ffn_in['lora_B'], 'L1_ffn_gate_w': _L1_ffn_in['gate_w'], 'L1_ffn_gate_b': _L1_ffn_in['gate_b']}
    _x0 = _d['L0_attn_a_x']
    _d['L0_attn_a_x'] = jax.random.normal(jax.random.fold_in(jax.random.key(seed), 1), (2, 1024, 128), dtype=_x0.dtype)
    del _x0
    return _d

def reference(L0_attn_a_x, L0_attn_a_Wq, L0_attn_a_Wkv, L0_attn_a_Wo, L0_attn_a_bo, L0_attn_a_ln_g, L0_attn_a_ln_b, L0_attn_b_ln_scale, L0_attn_b_ln_bias, L0_attn_b_qkv_kernel, L0_attn_b_out_kernel, L0_ffn_router_w, L0_ffn_w1, L0_ffn_w2, L1_attn_a_lower_bound, L1_attn_a_W_in, L1_attn_a_W_out, L1_attn_b_w_attn, L1_attn_b_w_proj, L1_ffn_wi, L1_ffn_bi, L1_ffn_wo, L1_ffn_bo, L1_ffn_lora_A, L1_ffn_lora_B, L1_ffn_gate_w, L1_ffn_gate_b):

    def _L0_attn_a_ref(x, Wq, Wkv, Wo, bo, ln_g, ln_b):
        import jax, jax.numpy as jnp
        import numpy as np
        B, SEQ, DIM = (2, 256, 128)
        H = 16
        DH = DIM // H
        LAT = 64
        CTX = SEQ - LAT
        SCALE = DH ** (-0.5)
        LN_EPS = 1e-05

        def _rotary_cos_sin(n):
            inv_freq = 1.0 / 10000.0 ** (jnp.arange(0, DH, 2, dtype=jnp.float32) / DH)
            freqs = jnp.arange(n, dtype=jnp.float32)[:, None] * inv_freq[None, :]
            emb = jnp.concatenate([freqs, freqs], axis=-1)
            return (jnp.cos(emb), jnp.sin(emb))

        def _rotate_half(t):
            t1, t2 = jnp.split(t, 2, axis=-1)
            return jnp.concatenate([-t2, t1], axis=-1)

        def _layernorm(t, g, b):
            m = jnp.mean(t, axis=-1, keepdims=True)
            v = jnp.var(t, axis=-1, keepdims=True)
            return (t - m) / jnp.sqrt(v + LN_EPS) * g + b
        b, n, d = x.shape
        neg = -jnp.finfo(x.dtype).max
        q = x @ Wq.T
        kv = x @ Wkv.T

        def split_heads(t):
            return t.reshape(b, n, H, DH).transpose(0, 2, 1, 3).reshape(b * H, n, DH)
        q = split_heads(q)
        kv = split_heads(kv)
        cos, sin = _rotary_cos_sin(n)
        q = q * cos + _rotate_half(q) * sin
        kv = kv * cos + _rotate_half(kv) * sin
        q_lat = q[:, CTX:] * SCALE
        q_ctx = q[:, :CTX] * SCALE
        lkv = _layernorm(kv, ln_g, ln_b)
        lkv_ctx = lkv[:, :CTX]
        lsim = jnp.einsum('bid,bjd->bij', q_lat, lkv)
        lat = n - CTX
        causal = jnp.triu(jnp.ones((lat, lat), dtype=bool), 1)
        mask = jnp.concatenate([jnp.zeros((lat, CTX), dtype=bool), causal], axis=-1)
        lsim = jnp.where(mask, neg, lsim)
        attn = jax.nn.softmax(lsim, axis=-1)
        out = jnp.einsum('bij,bjd->bid', attn, lkv)
        lsim_ctx = jnp.einsum('bid,bjd->bij', q_ctx, lkv_ctx)
        attn_ctx = jax.nn.softmax(lsim_ctx, axis=-1)
        out_ctx = jnp.einsum('bij,bjd->bid', attn_ctx, lkv_ctx)

        def merge_heads(t):
            m = t.shape[1]
            return t.reshape(b, H, m, DH).transpose(0, 2, 1, 3).reshape(b, m, H * DH)
        out_all = jnp.concatenate([merge_heads(out), merge_heads(out_ctx)], axis=1)
        return out_all @ Wo.T + bo

    def _L0_attn_b_ref(inputs_q, ln_scale, ln_bias, qkv_kernel, out_kernel):
        import jax, jax.numpy as jnp
        import numpy as np
        SEQ, BATCH, HIDDEN = (256, 2, 128)
        NUM_HEADS, HEAD_DIM = (16, 64)
        LN_EPS = 1e-06
        NEG_INF = -10000000000.0
        s, b, h = inputs_q.shape
        mu = jnp.mean(inputs_q, axis=-1, keepdims=True)
        var = jnp.mean(jnp.square(inputs_q - mu), axis=-1, keepdims=True)
        ln_out = (inputs_q - mu) * jax.lax.rsqrt(var + LN_EPS) * ln_scale + ln_bias
        qkv = jnp.einsum('sbh,htk->stbk', ln_out, qkv_kernel)
        q = qkv[:, 0].reshape(s, b, NUM_HEADS, HEAD_DIM)
        k = qkv[:, 1].reshape(s, b, NUM_HEADS, HEAD_DIM)
        v = qkv[:, 2].reshape(s, b, NUM_HEADS, HEAD_DIM)
        scale = 1.0 / np.sqrt(HEAD_DIM).astype(np.float32)
        logits = jnp.einsum('qbhd,kbhd->bhqk', q, k) * scale
        causal = jnp.tril(jnp.ones((s, s), dtype=bool))
        logits = jnp.where(causal[None, None], logits, jnp.asarray(NEG_INF, logits.dtype))
        attn = jax.nn.softmax(logits, axis=-1)
        ctx = jnp.einsum('bhqk,kbhd->qbhd', attn, v).reshape(s, b, NUM_HEADS * HEAD_DIM)
        return jnp.einsum('sbk,kh->sbh', ctx, out_kernel)

    def _L0_ffn_ref(x, router_w, w1, w2):
        import jax, jax.numpy as jnp
        import numpy as np
        N_EMBD = 128
        EXPERT_SIZES = [(4, 128), (4, 256)]
        TOP_K = 2
        B, S = (1, 256)
        WIDTHS = []
        for count, size in EXPERT_SIZES:
            WIDTHS += [size] * count
        OFFSETS = np.concatenate([[0], np.cumsum(WIDTHS)]).astype(np.int64)
        E = len(WIDTHS)
        TOTAL_W = int(OFFSETS[-1])
        MAX_W = max(WIDTHS)

        def _stack_experts(w1, w2):
            W1e, W2e = ([], [])
            for e in range(E):
                off, wd = (int(OFFSETS[e]), WIDTHS[e])
                pad = MAX_W - wd
                W1e.append(jnp.pad(w1[:, off:off + wd], ((0, 0), (0, pad))))
                W2e.append(jnp.pad(w2[off:off + wd, :], ((0, pad), (0, 0))))
            return (jnp.stack(W1e), jnp.stack(W2e))
        b, s, d = x.shape
        xf = x.reshape(-1, d)
        logits = xf @ router_w.T
        probs = jax.nn.sigmoid(logits.astype(jnp.float32))
        topw, sel = jax.lax.top_k(probs, TOP_K)
        topw = topw / (topw.sum(-1, keepdims=True) + 1e-20)
        topw = topw.astype(x.dtype)
        onehot = sel[:, :, None] == jnp.arange(E)[None, None, :]
        combine = jnp.sum(topw[:, :, None] * onehot, axis=1)
        W1e, W2e = _stack_experts(w1, w2)
        h = jnp.einsum('td,edw->tew', xf, W1e)
        h = jnp.square(jax.nn.relu(h))
        y = jnp.einsum('tew,ewd->ted', h, W2e)
        out = jnp.einsum('ted,te->td', y, combine)
        return out.reshape(b, s, d)

    def _L1_attn_a_ref(x, lower_bound, W_in, W_out):
        import jax, jax.numpy as jnp
        import numpy as np
        EXPAND = 2
        n, b, d = x.shape
        e = EXPAND
        h = d // e
        feat = x @ W_in
        V, Q, Fg = jnp.split(feat, 3, axis=-1)
        V = jax.nn.gelu(V, approximate=False)
        Q = jax.nn.gelu(Q, approximate=False)
        Fg = jax.nn.sigmoid(Fg)
        V = V.reshape(n, b, h, e)
        Q = Q.reshape(n, b, h, e)
        Fg = Fg.reshape(n, b, h, e)
        lb = lower_bound.reshape(h, e)
        lam = lb + (1.0 - lb) * Fg
        K = 1.0 - lam

        def step(S, inp):
            lam_t, k_t, v_t, q_t = inp
            S = lam_t[..., :, None] * S + k_t[..., :, None] * v_t[..., None, :]
            o_t = jnp.einsum('bhk,bhkv->bhv', q_t, S)
            return (S, o_t)
        S0 = jnp.zeros((b, h, e, e), dtype=x.dtype)
        _, o = jax.lax.scan(step, S0, (lam, K, V, Q))
        o = o.reshape(n, b, d)
        return o @ W_out

    def _L1_attn_b_ref(x, w_attn, w_proj):
        import math
        import jax, jax.numpy as jnp
        import numpy as np
        N_EMBD = 128
        N_HEAD = 16
        HEAD_DIM = N_EMBD // N_HEAD

        def alibi_slopes(n_heads):
            start = 2.0 ** (-2.0 ** (-(math.log2(n_heads) - 3)))
            return np.array([start * start ** i for i in range(n_heads)], dtype=np.float32)
        B, T, C = x.shape
        H, D = (N_HEAD, HEAD_DIM)
        qkv = x @ w_attn.T
        q, k, v = jnp.split(qkv, 3, axis=-1)
        q = q.reshape(B, T, H, D).transpose(0, 2, 1, 3)
        k = k.reshape(B, T, H, D).transpose(0, 2, 1, 3)
        v = v.reshape(B, T, H, D).transpose(0, 2, 1, 3)
        att = jnp.einsum('bhqd,bhkd->bhqk', q, k) * (1.0 / math.sqrt(D))
        pos = jnp.arange(T)
        rel = pos[None, :] - pos[:, None]
        slopes = jnp.asarray(alibi_slopes(H))[:, None, None]
        causal = rel <= 0
        bias = jnp.where(causal, slopes * rel, -jnp.inf)
        att = att + bias[None]
        att = jax.nn.softmax(att, axis=-1)
        y = jnp.einsum('bhqk,bhkd->bhqd', att, v)
        y = y.transpose(0, 2, 1, 3).reshape(B, T, C)
        return y @ w_proj.T

    def _L1_ffn_ref(hidden_states, wi, bi, wo, bo, lora_A, lora_B, gate_w, gate_b):
        import jax, jax.numpy as jnp
        import numpy as np
        B, S, D_MODEL, D_FF, E, R, TOP_K = (4, 256, 128, 512, 8, 16, 2)
        logits = jnp.einsum('bsd,ed->bse', hidden_states, gate_w) + gate_b
        scores = jax.nn.softmax(logits, axis=-1)
        top_v, top_i = jax.lax.top_k(scores, TOP_K)
        val_sum = top_v.sum(axis=-1)
        out = jnp.zeros_like(hidden_states)
        for e in range(E):
            count = (top_i == e).sum(axis=-1).astype(hidden_states.dtype)
            gate = count * val_sum
            inter = jnp.einsum('bsd,fd->bsf', hidden_states, wi) + bi + jnp.einsum('bsr,fr->bsf', jnp.einsum('bsd,rd->bsr', hidden_states, lora_A[e]), lora_B[e])
            h = jax.nn.relu(inter)
            expert_out = jnp.einsum('bsf,df->bsd', h, wo) + bo
            out = out + gate[..., None] * expert_out
        return out
    x = L0_attn_a_x
    x = x + _L0_attn_a_ref(_layernorm(x, axis=-1), L0_attn_a_Wq, L0_attn_a_Wkv, L0_attn_a_Wo, L0_attn_a_bo, L0_attn_a_ln_g, L0_attn_a_ln_b)
    x = x + _L0_ffn_ref(_layernorm(x, axis=-1), L0_ffn_router_w, L0_ffn_w1, L0_ffn_w2)
    x = x + _L0_attn_b_ref(_layernorm(x, axis=-1), L0_attn_b_ln_scale, L0_attn_b_ln_bias, L0_attn_b_qkv_kernel, L0_attn_b_out_kernel)
    x = x + _L0_ffn_ref(_layernorm(x, axis=-1), L0_ffn_router_w, L0_ffn_w1, L0_ffn_w2)
    x = x + _L1_attn_a_ref(_layernorm(x, axis=-1), L1_attn_a_lower_bound, L1_attn_a_W_in, L1_attn_a_W_out)
    x = x + _L1_ffn_ref(_layernorm(x, axis=-1), L1_ffn_wi, L1_ffn_bi, L1_ffn_wo, L1_ffn_bo, L1_ffn_lora_A, L1_ffn_lora_B, L1_ffn_gate_w, L1_ffn_gate_b)
    x = x + _L1_attn_b_ref(_layernorm(x, axis=-1), L1_attn_b_w_attn, L1_attn_b_w_proj)
    x = x + _L1_ffn_ref(_layernorm(x, axis=-1), L1_ffn_wi, L1_ffn_bi, L1_ffn_wo, L1_ffn_bo, L1_ffn_lora_A, L1_ffn_lora_B, L1_ffn_gate_w, L1_ffn_gate_b)
    return x

_drawn_inputs = setup_inputs


def setup_inputs(seed=0):
    import zlib

    import numpy as np

    out = dict(_drawn_inputs(seed))
    spreads = {'L0_attn_a_bo': (0.0, 0.1),
     'L0_attn_a_ln_g': (1.0, 0.6),
     'L0_attn_a_ln_b': (0.0, 0.5),
     'L0_attn_b_ln_scale': (1.0, 0.2),
     'L0_attn_b_ln_bias': (0.0, 0.1),
     'L1_attn_a_lower_bound': (0.0, 0.339)}
    factors = {'L0_attn_a_Wq': 2.763,
     'L0_attn_a_Wkv': 4.564,
     'L0_ffn_router_w': 3.753,
     'L0_ffn_w1': 3.581,
     'L0_ffn_w2': 3.274,
     'L1_ffn_bi': 7.755,
     'L1_ffn_bo': 4.885,
     'L1_ffn_gate_b': 8.0}
    for name, (base, spread) in spreads.items():
        noise = np.random.default_rng([zlib.crc32(name.encode()), seed]).standard_normal(out[name].shape)
        drawn = base * np.exp(spread * noise) if base else spread * noise
        out[name] = jnp.asarray(drawn.astype(out[name].dtype))
    for name, factor in factors.items():
        out[name] = (out[name] * factor).astype(out[name].dtype)
    return out
```

```python
from contextlib import ExitStack

import concourse.bass as bass
from concourse import mybir

F32 = mybir.dt.float32
BF16 = mybir.dt.bfloat16
ALU = mybir.AluOpType
ACT = mybir.ActivationFunctionType
AX = mybir.AxisListType

P = 128
BATCH, SEQ = 2, 1024
SEQ_TILES = SEQ // P
TILES = BATCH * SEQ_TILES
CHUNK = 4
CHUNKS = TILES // CHUNK
CW = CHUNK * P
TOKENS = TILES * P
HEADS, DH = 16, 8
ALL_HEADS = BATCH * HEADS
CTX = 192
EXPERTS = 8

Q_PARTS = (0, 0, 1, 1, 0, 2)
K_PARTS = (0, 1, 0, 1, 2, 0)
ROW_BIAS = len(Q_PARTS) * DH
ROW_MAX = ROW_BIAS + 3
ROWS = ROW_MAX + 3

PAIR_HEADS, PAIR_DH = 16, 64
PAIR_W = PAIR_HEADS * PAIR_DH
PAIR_BLOCKS = PAIR_W // P

EXPERT_BLOCKS = (1, 1, 1, 1, 2, 2, 2, 2)
HIDDEN_BLOCKS = sum(EXPERT_BLOCKS)

FF = 512
FF_BLOCKS = FF // P
RANK = 16

STAGES = 8


def columns(*fields):
    at, out = 0, {}
    for name, n in fields:
        out[name] = (at, n)
        at += n
    return out, at


CONST, CONST_W = columns(("ident", P), ("cos", SEQ_TILES * DH), ("sin", SEQ_TILES * DH), ("rank", EXPERTS))
MASKS, MASKS_W = columns(("ident", P), ("rot_01", P), ("rot_11", P), ("diag", P),
                         ("rot_T", 2 * P), ("diag_T", P))
W_ROT, W_ROT_W = columns(("qkv", 2 * P), ("out", P), ("bo", P), ("ln_g", DH), ("ln_b", DH))
W_MOE, W_MOE_W = columns(("router", EXPERTS), ("w1", HIDDEN_BLOCKS * P), ("w2", HIDDEN_BLOCKS * P))
W_PAIR, W_PAIR_W = columns(("q", PAIR_W), ("k", PAIR_W), ("v", PAIR_W), ("v_T", PAIR_W), ("out", PAIR_W),
                           ("ln_scale", 1), ("ln_bias", 1))
W_REC, W_REC_W = columns(("in", 3 * P), ("out", P), ("lower", P))
W_ALI, W_ALI_W = columns(("q", P), ("k", P), ("v", P), ("out", P))
W_LORA, W_LORA_W = columns(("wi", FF), ("wo", FF), ("a_gate", P + EXPERTS), ("b", FF), ("bi", FF_BLOCKS),
                           ("gate_b", EXPERTS), ("bo", P))


class Count:

    def __init__(self, handle):
        self.sem = handle
        self.before = 0

    def at(self, n):
        return self.before + n

    def passed(self, n):
        self.before += n


class Core:

    def __init__(self, nc, ctx):
        self.nc = nc
        self.ctx = ctx
        self.counts = {}
        self.names = 0

    def name(self, name):
        self.names += 1
        return f"{name}_{self.names}"

    def sbuf(self, ctx, name, shape, dt=F32):
        return ctx.enter_context(self.nc.sbuf_tensor(self.name(name), shape, dt))

    def psum(self, ctx, name, shape, dt=F32):
        return ctx.enter_context(self.nc.psum_tensor(self.name(name), shape, dt))

    def semaphore(self, name):
        if name not in self.counts:
            self.counts[name] = Count(self.ctx.enter_context(self.nc.semaphore(name)))
        return self.counts[name]


def field(tile, places, name):
    at, n = places[name]
    return tile[:, at:at + n]


def stage_load(core, loads):
    nc = core.nc
    loaded = core.semaphore("loaded")
    with nc.Block() as block:

        @block.sync
        def _(sp):
            for dst, src in loads:
                sp.dma_start(dst, src).then_inc(loaded.sem, 16)
            sp.wait_ge(loaded.sem, loaded.at(16 * len(loads)))
    loaded.passed(16 * len(loads))


ROOT_STEPS = 5


def inverse_root(dve, done, step, root_ready, var, eps, shifted, root, out, spare, scale=1.0):
    dve.tensor_scalar(shifted, var, scale, eps, ALU.mult, ALU.add).then_inc(step.sem, 1)
    dve.wait_ge(root_ready.sem, root_ready.at(1))
    dve.reciprocal(out, root).then_inc(step.sem, 1)
    dve.wait_ge(step.sem, step.at(2))
    dve.tensor_tensor(spare, out, out, ALU.mult).then_inc(step.sem, 1)
    dve.wait_ge(step.sem, step.at(3))
    dve.tensor_tensor(spare, spare, shifted, ALU.mult).then_inc(step.sem, 1)
    dve.wait_ge(step.sem, step.at(4))
    dve.tensor_scalar(spare, spare, -0.5, 1.5, ALU.mult, ALU.add).then_inc(step.sem, 1)
    dve.wait_ge(step.sem, step.at(5))
    dve.tensor_tensor(out, out, spare, ALU.mult).then_inc(done.sem, 1)
    dve.wait_ge(done.sem, done.at(1))


def stage_norm(core, src, eps, xT=None, token_major=None, affine=None, loads=()):
    nc = core.nc
    stats_ready = core.semaphore("norm_stats_ready")
    moments_ready = core.semaphore("norm_moments_ready")
    variance_step = core.semaphore("norm_variance_step")
    root_ready = core.semaphore("norm_root_ready")
    rstd_ready = core.semaphore("norm_rstd_ready")
    tile_ready = core.semaphore("norm_chunk_ready")
    turned = core.semaphore("norm_chunk_turned")
    xT_ready = core.semaphore("norm_xT_ready")
    with ExitStack() as ctx:
        stats = core.sbuf(ctx, "stats", [P, TILES, 6], F32)
        moments = core.sbuf(ctx, "moments", [P, TILES, 2], F32)
        variance = core.sbuf(ctx, "variance", [P, TILES], F32)
        root = core.sbuf(ctx, "root", [P, TILES], F32)
        spare = core.sbuf(ctx, "spare", [P, TILES], F32)
        rstd = core.sbuf(ctx, "rstd", [P, TILES], F32)
        normed = token_major
        if token_major is None:
            normed = core.sbuf(ctx, "normed", [P, TILES, P], F32)
            turned_ps = core.psum(ctx, "turned_ps", [P, 2, CW], F32)
        loaded = core.semaphore("loaded")
        block = ctx.enter_context(nc.Block())

        if loads:
            @block.sync
            def _(sp):
                for dst, source in loads:
                    sp.dma_start(dst, source).then_inc(loaded.sem, 16)
                sp.wait_ge(loaded.sem, loaded.at(16 * len(loads)))

        @block.vector
        def _(dve):
            for t in range(TILES):
                last = dve.bn_stats(stats[:, t, :], src[:, t, :])
            last.then_inc(stats_ready.sem, 1)
            dve.wait_ge(stats_ready.sem, stats_ready.at(1))
            for t in range(TILES):
                last = dve.bn_aggr(moments[:, t, :], stats[:, t, :])
            last.then_inc(moments_ready.sem, 1)
            dve.wait_ge(moments_ready.sem, moments_ready.at(1))
            inverse_root(dve, rstd_ready, variance_step, root_ready, moments[:, :, 1], eps, variance[:, :],
                         root[:, :], rstd[:, :], spare[:, :])
            for c in range(CHUNKS):
                for t in range(CHUNK * c, CHUNK * (c + 1)):
                    last = dve.tensor_scalar(normed[:, t, :], src[:, t, :], moments[:, t, 0:1],
                                             rstd[:, t:t + 1], ALU.subtract, ALU.mult)
                last.then_inc(tile_ready.sem, 1)

        if token_major is None:
            @block.tensor
            def _(pe):
                for c in range(CHUNKS):
                    pe.wait_ge(tile_ready.sem, tile_ready.at(c + 1))
                    if c >= 2:
                        pe.wait_ge(xT_ready.sem, xT_ready.at(c - 1))
                    for j in range(CHUNK):
                        last = pe.transpose(turned_ps[:, c % 2, j * P:(j + 1) * P],
                                            normed[:, CHUNK * c + j, :], core.ident)
                    last.then_inc(turned.sem, 1)

        @block.scalar
        def _(act):
            act.wait_ge(variance_step.sem, variance_step.at(1))
            act.activation(root[:, :], variance[:, :], ACT.Sqrt).then_inc(root_ready.sem, 1)
            if token_major is None:
                for c in range(CHUNKS):
                    act.wait_ge(turned.sem, turned.at(c + 1))
                    out = xT[:, c * CW:(c + 1) * CW]
                    if affine:
                        ins = act.activation(out, turned_ps[:, c % 2, :], ACT.Identity,
                                             bias=affine[1], scale=affine[0])
                    else:
                        ins = act.copy(out, turned_ps[:, c % 2, :])
                    ins.then_inc(xT_ready.sem, 1)

    stats_ready.passed(1)
    moments_ready.passed(1)
    variance_step.passed(ROOT_STEPS)
    root_ready.passed(1)
    rstd_ready.passed(1)
    loaded.passed(16 * len(loads))
    tile_ready.passed(CHUNKS)
    if token_major is None:
        turned.passed(CHUNKS)
        xT_ready.passed(CHUNKS)


def stage_operands(core, xT, weights, rotary, scale, q_stack, k_stack, v_tok, q_rows, k_rows):
    nc = core.nc
    proj_ready = core.semaphore("op_projection_ready")
    step_done = core.semaphore("op_vector_step_done")
    middle_ready = core.semaphore("op_middle_part_ready")
    var_step = core.semaphore("op_variance_step")
    root_ready = core.semaphore("op_root_ready")
    sq_ready = core.semaphore("op_k_variance_ready")
    rstd_ready = core.semaphore("op_k_rstd_ready")
    qk_ready = core.semaphore("op_qk_token_major_ready")
    turned = core.semaphore("op_qk_turned")
    v_ready = core.semaphore("op_v_ready")
    vps_ready = core.semaphore("op_v_product_ready")
    high_ready = core.semaphore("op_high_part_ready")
    rest_ready = core.semaphore("op_rest_ready")
    low_ready = core.semaphore("op_low_parts_ready")
    stored = [core.semaphore(f"op_parts_stored_{i}") for i in range(2)]
    stacked = core.semaphore("op_stacks_loaded")
    ones_set = core.semaphore("op_v_ones_set")
    G = CHUNK * HEADS
    with ExitStack() as ctx:
        def sb(name, shape, dt=F32):
            return core.sbuf(ctx, name, shape, dt)

        parts = sb("parts", [P, 2, 6, CW], BF16)
        rest = sb("rest", [P, 2, CW])
        turned_ps = core.psum(ctx, "turned_ps", [P, 2, 2, CW], F32)
        parts_dram = nc.dram_tensor("parts_rot" if rotary else "parts_ali", [6, P, TOKENS], BF16, kind="Internal")
        if rotary:
            proj_ps = core.psum(ctx, "proj_ps", [P, 2, CHUNK, 2 * P], F32)
            by_cos = sb("by_cos", [P, CHUNK, 2 * P])
            by_sin = sb("by_sin", [P, CHUNK, 2 * P])
            rotated = sb("rotated", [P, CHUNK, 2 * P])
            q_tok = rotated[:, :, 0:P]
            k_tok = sb("k_tok", [P, CHUNK, P])
            mean = sb("mean", [P, G])
            var = sb("var", [P, G])
            shifted = sb("shifted", [P, G])
            root = sb("root", [P, G])
            spare = sb("spare", [P, G])
            rstd = sb("rstd", [P, G])
            square = by_sin[:, :, 0:P]
        else:
            v_ps = core.psum(ctx, "v_ps", [P, 2, CW], F32)
        block = ctx.enter_context(nc.Block())

        def v_of_chunk(c):
            b, t0 = divmod(CHUNK * c, SEQ_TILES)
            return v_tok[:, b * HEADS:(b + 1) * HEADS, t0:t0 + CHUNK, 0:DH].rearrange("p h j d -> p j h d")

        @block.tensor
        def _(pe):
            def project(c):
                if rotary:
                    if c >= 2:
                        pe.wait_ge(step_done.sem, step_done.at(2 * (c - 1)))
                    for j in range(CHUNK):
                        t = CHUNK * c + j
                        last = pe.matmul(proj_ps[:, c % 2, j, :], xT[:, t * P:(t + 1) * P],
                                         field(weights, W_ROT, "qkv"), start=True, stop=True)
                    last.then_inc(proj_ready.sem, 1)
                    return
                if c >= 2:
                    pe.wait_ge(rest_ready.sem, rest_ready.at(2 * (c - 1)))
                    pe.wait_ge(high_ready.sem, high_ready.at(2 * (c - 1)))
                    pe.wait_ge(v_ready.sem, v_ready.at(c - 1))
                for i, name in enumerate("qk"):
                    last = pe.matmul(turned_ps[:, c % 2, i, :], field(weights, W_ALI, name),
                                     xT[:, c * CW:(c + 1) * CW], start=True, stop=True)
                last.then_inc(turned.sem, 1)
                for j in range(CHUNK):
                    t = CHUNK * c + j
                    last = pe.matmul(v_ps[:, c % 2, j * P:(j + 1) * P], xT[:, t * P:(t + 1) * P],
                                     field(weights, W_ALI, "v"), start=True, stop=True)
                last.then_inc(vps_ready.sem, 1)

            def turn(c):
                pe.wait_ge(qk_ready.sem, qk_ready.at(c + 1))
                if c >= 2:
                    pe.wait_ge(rest_ready.sem, rest_ready.at(2 * (c - 1)))
                    pe.wait_ge(high_ready.sem, high_ready.at(2 * (c - 1)))
                for i, tok in enumerate((q_tok, k_tok)):
                    for j in range(CHUNK):
                        last = pe.transpose(turned_ps[:, c % 2, i, j * P:(j + 1) * P], tok[:, j, :], core.ident)
                last.then_inc(turned.sem, 1)

            for c in range(CHUNKS):
                project(c)
                if rotary and c >= 1:
                    turn(c - 1)
            if rotary:
                turn(CHUNKS - 1)

        @block.vector
        def _(dve):
            dve.memset(v_tok[:, :, :, DH:DH + 1], 1.0).then_inc(ones_set.sem, 1)

            def rotate(c):
                t0 = (CHUNK * c) % SEQ_TILES
                both = proj_ps[:, c % 2, :, :].rearrange("p j (g d) -> p j g d", d=DH)
                cos = field(core.const, CONST, "cos").rearrange("p (t d) -> p t d", d=DH)[:, t0:t0 + CHUNK, :]
                sin = field(core.const, CONST, "sin").rearrange("p (t d) -> p t d", d=DH)[:, t0:t0 + CHUNK, :]
                wide = [P, CHUNK, 2 * HEADS, DH]
                half = [P, CHUNK, 2 * HEADS, DH // 2]
                dve.wait_ge(proj_ready.sem, proj_ready.at(c + 1))
                dve.tensor_tensor(by_cos[:, :, :].rearrange("p j (g d) -> p j g d", d=DH), both,
                                  cos[:, :, None, :].to_broadcast(wide), ALU.mult)
                sines = by_sin[:, :, :].rearrange("p j (g d) -> p j g d", d=DH)
                dve.tensor_tensor(sines[:, :, :, 0:4], both[:, :, :, 4:8],
                                  sin[:, :, None, 0:4].to_broadcast(half), ALU.mult)
                dve.tensor_tensor(sines[:, :, :, 4:8], both[:, :, :, 0:4],
                                  sin[:, :, None, 4:8].to_broadcast(half), ALU.mult).then_inc(step_done.sem, 1)
                dve.wait_ge(step_done.sem, step_done.at(2 * c + 1))
                if c >= 1:
                    dve.wait_ge(turned.sem, turned.at(c))
                    dve.wait_ge(v_ready.sem, v_ready.at(c))
                dve.tensor_tensor(rotated[:, :, :], by_cos[:, :, :], by_sin[:, :, :],
                                  ALU.add).then_inc(step_done.sem, 1)
                dve.wait_ge(step_done.sem, step_done.at(2 * c + 2))

            def norm_k(c):
                k = rotated[:, :, P:2 * P].rearrange("p j (g d) -> p j g d", d=DH)
                kn = k_tok[:, :, :].rearrange("p j (g d) -> p j g d", d=DH)
                sq = square.rearrange("p j (g d) -> p j g d", d=DH)
                shape = [P, CHUNK, HEADS, DH]

                def wide(s):
                    return s[:, :].rearrange("p (j g) -> p j g", j=CHUNK)[:, :, :, None].to_broadcast(shape)

                n = 5 * c
                dve.tensor_reduce(mean[:, :].rearrange("p (j g) -> p j g", j=CHUNK), k, AX.X,
                                  ALU.add).then_inc(sq_ready.sem, 1)
                dve.wait_ge(sq_ready.sem, sq_ready.at(n + 1))
                dve.tensor_scalar(mean[:, :], mean[:, :], 1.0 / DH, None, ALU.mult).then_inc(sq_ready.sem, 1)
                dve.wait_ge(sq_ready.sem, sq_ready.at(n + 2))
                dve.tensor_tensor(kn, k, wide(mean), ALU.subtract).then_inc(sq_ready.sem, 1)
                dve.wait_ge(sq_ready.sem, sq_ready.at(n + 3))
                dve.tensor_tensor(sq, kn, kn, ALU.mult).then_inc(sq_ready.sem, 1)
                dve.wait_ge(sq_ready.sem, sq_ready.at(n + 4))
                dve.tensor_reduce(var[:, :].rearrange("p (j g) -> p j g", j=CHUNK), sq, AX.X,
                                  ALU.add).then_inc(sq_ready.sem, 1)
                dve.wait_ge(sq_ready.sem, sq_ready.at(n + 5))
                inverse_root(dve, rstd_ready, var_step, root_ready, var[:, :], 1e-5, shifted[:, :], root[:, :],
                             rstd[:, :], spare[:, :], scale=1.0 / DH)
                var_step.before += ROOT_STEPS
                root_ready.before += 1
                rstd_ready.before += 1
                g = field(weights, W_ROT, "ln_g")[:, None, None, :].to_broadcast(shape)
                b = field(weights, W_ROT, "ln_b")[:, None, None, :].to_broadcast(shape)
                dve.tensor_tensor(kn, kn, wide(rstd), ALU.mult).then_inc(qk_step.sem, 1)
                dve.wait_ge(qk_step.sem, qk_step.at(2 * c + 1))
                dve.tensor_tensor(kn, kn, g, ALU.mult).then_inc(qk_step.sem, 1)
                dve.wait_ge(qk_step.sem, qk_step.at(2 * c + 2))
                dve.tensor_tensor(kn, kn, b, ALU.add).then_inc(qk_ready.sem, 1)

            def rest_of(c):
                for i in range(2):
                    dve.wait_ge(high_ready.sem, high_ready.at(2 * c + i + 1))
                    if c >= 1:
                        dve.wait_ge(low_ready.sem, low_ready.at(2 * (c - 1) + i + 1))
                    dve.scalar_tensor_tensor(rest[:, i, :], turned_ps[:, c % 2, i, :],
                                             scale if i == 0 else 1.0, parts[:, c % 2, 3 * i, :],
                                             ALU.mult, ALU.subtract).then_inc(rest_ready.sem, 1)

            qk_step = core.semaphore("op_k_affine_step")
            at_start = var_step.before, root_ready.before, rstd_ready.before
            for c in range(CHUNKS):
                if rotary:
                    rotate(c)
                    norm_k(c)
                rest_of(c)
            if rotary:
                qk_step.passed(2 * CHUNKS)
                var_step.before, root_ready.before, rstd_ready.before = at_start

        @block.scalar
        def _(act):
            act.wait_ge(ones_set.sem, ones_set.at(1))
            for c in range(CHUNKS):
                if rotary:
                    act.wait_ge(var_step.sem, var_step.at(ROOT_STEPS * c + 1))
                    act.activation(root[:, :], shifted[:, :], ACT.Sqrt).then_inc(root_ready.sem, 1)
                    act.wait_ge(qk_ready.sem, qk_ready.at(c + 1))
                    act.copy(v_of_chunk(c), k_tok[:, :, :].rearrange("p j (g d) -> p j g d", d=DH)
                             ).then_inc(v_ready.sem, 1)
                act.wait_ge(turned.sem, turned.at(c + 1))
                if c >= 2:
                    act.wait_ge(stored[c % 2].sem, stored[c % 2].at(16 * (c // 2)))
                for i in range(2):
                    act.mul(parts[:, c % 2, 3 * i, :], turned_ps[:, c % 2, i, :],
                            scale if i == 0 else 1.0).then_inc(high_ready.sem, 1)
                for i in range(2):
                    act.wait_ge(rest_ready.sem, rest_ready.at(2 * c + i + 1))
                    act.copy(parts[:, c % 2, 3 * i + 1, :], rest[:, i, :]).then_inc(middle_ready.sem, 1)
                if not rotary:
                    act.wait_ge(vps_ready.sem, vps_ready.at(c + 1))
                    act.copy(v_of_chunk(c), v_ps[:, c % 2, :].rearrange("p (j g d) -> p j g d", j=CHUNK, d=DH)
                             ).then_inc(v_ready.sem, 1)

        @block.gpsimd
        def _(pool):
            for c in range(CHUNKS):
                for i in range(2):
                    pool.wait_ge(middle_ready.sem, middle_ready.at(2 * c + i + 1))
                    pool.tensor_tensor(parts[:, c % 2, 3 * i + 2, :], rest[:, i, :],
                                       parts[:, c % 2, 3 * i + 1, :], ALU.subtract).then_inc(low_ready.sem, 1)

        @block.sync
        def _(sp):
            wide = slice(0, ALL_HEADS * SEQ)
            sp.dma_start(q_stack[ROW_BIAS:ROW_MAX, wide], q_rows).then_inc(stacked.sem, 16)
            sp.dma_start(k_stack[ROW_BIAS:ROWS, wide], k_rows).then_inc(stacked.sem, 16)
            for c in range(CHUNKS):
                sp.wait_ge(high_ready.sem, high_ready.at(2 * c + 2))
                sp.wait_ge(low_ready.sem, low_ready.at(2 * c + 2))
                sp.dma_start(parts_dram[:, :, c * CW:(c + 1) * CW].rearrange("a p n -> p a n"),
                             parts[:, c % 2, :, :]).then_inc(stored[c % 2].sem, 16)
                if c % 2 == 1:
                    b = c // 2
                    for s in stored:
                        sp.wait_ge(s.sem, s.at(16 * (b + 1)))
                    for stack, order, first in ((q_stack, Q_PARTS, 0), (k_stack, K_PARTS, 3)):
                        for a, part in enumerate(order):
                            src = parts_dram[first + part, :, b * SEQ:(b + 1) * SEQ].rearrange("(h d) n -> d h n", d=DH)
                            dst = stack[a * DH:(a + 1) * DH, b * HEADS * SEQ:(b + 1) * HEADS * SEQ]
                            sp.dma_start(dst.rearrange("d (h n) -> d h n", h=HEADS), src).then_inc(stacked.sem, 16)
            sp.wait_ge(stacked.sem, stacked.at(16 * (2 + 2 * len(Q_PARTS) * BATCH)))

    ones_set.passed(1)
    for s in (high_ready, rest_ready, middle_ready, low_ready):
        s.passed(2 * CHUNKS)
    turned.passed(CHUNKS)
    v_ready.passed(CHUNKS)
    for s in stored:
        s.passed(16 * CHUNKS // 2)
    stacked.passed(16 * (2 + 2 * len(Q_PARTS) * BATCH))
    if rotary:
        proj_ready.passed(CHUNKS)
        step_done.passed(2 * CHUNKS)
        sq_ready.passed(5 * CHUNKS)
        rstd_ready.passed(CHUNKS)
        qk_ready.passed(CHUNKS)
        var_step.passed(ROOT_STEPS * CHUNKS)
        root_ready.passed(CHUNKS)
    else:
        vps_ready.passed(CHUNKS)


def key_tiles(qt, rotary):
    if rotary and qt == 0:
        return 2, 1, "rot_01"
    if rotary and qt == 1:
        return 2, 1, "rot_11"
    return qt + 1, qt, "diag"


GROUP = 4
GROUPS = ALL_HEADS // GROUP
AHEAD = 6
SLOT = P // GROUP
UNITS = GROUP * SEQ_TILES


def max_units(heads, whole=0):
    out = []
    for i, head in enumerate(heads):
        merged = i < len(heads) - whole
        if merged:
            out.append((head, ((0, 0), (1, 0))))
        else:
            out += [(head, ((0, 0),)), (head, ((1, 0),))]
        for qt in range(2, SEQ_TILES):
            out.append((head, ((qt, 0),)))
            if qt >= CHUNK:
                out.append((head, ((qt, CHUNK),)))
    return out


def plan_side(heads, settle_after, rows_after, turns, whole=0):
    out = [("max", *u) for u in max_units([h for h in heads], whole)]
    if settle_after is not None:
        at = len(max_units(heads[:settle_after]))
        out[at - 1] = ("settle", *out[at - 1][1:])
        out.insert(min(at + rows_after, len(out)), ("rows",))
    if turns:
        at = min(6, len(out))
        out[at:at] = [("turn", 0)]
        at = min(9, len(out))
        out[at:at] = [("turn", 1)]
    return out


def first_query_tile(kt, rotary):
    return 0 if rotary and kt == 1 else kt


def width(kt, rotary):
    return SEQ - first_query_tile(kt, rotary) * P


def query_spans(kt, rotary):
    q0 = first_query_tile(kt, rotary) * P
    return [(max(q0, s), s + CW) for s in range(0, SEQ, CW) if q0 < s + CW]


def interleave(side, rotary):
    clock, busy, done, out = 0.0, 0.0, [], []
    k = 0

    def fill(turns):
        nonlocal clock, busy, k
        while k < len(side) and (k < 2 or done[k - 2] <= clock):
            work = side[k]
            if work[0] == "turn" and not turns:
                break
            cols = 400 if work[0] in ("turn", "rows") else sum(
                (min(CHUNK, qt + 1 - k0)) * P for qt, k0 in work[2])
            clock += cols / 2.4
            busy = max(busy, clock) + cols / 0.96 + 70
            done.append(busy)
            out.append(("side", k))
            k += 1

    for kt in range(SEQ_TILES + 1):
        spans = query_spans(kt - 1, rotary) if kt else []
        for j in range(GROUP):
            if kt < SEQ_TILES:
                out.append(("score", kt, j))
                clock += width(kt, rotary) / 2.4
                fill(kt > 0)
            if j % 2 == 0 and spans:
                a, b = spans.pop(0)
                out.append(("weigh", kt - 1, a, b, not spans))
                clock += GROUP * (b - a) * 0.45
                fill(True)
    out += [("side", i) for i in range(k, len(side))]
    return out


def stage_attend(core, rotary, q_stack, k_stack, v_tok, o_tok):
    nc = core.nc
    side_ready = core.semaphore("att_side_ready")
    side_free = core.semaphore("att_side_bank_free")
    split = core.semaphore("att_max_split_step")
    rows_stacked = core.semaphore("att_max_rows_stacked")
    scores_ready = core.semaphore("att_scores_ready")
    exp_done = core.semaphore("att_exp_done")
    weighed = core.semaphore("att_probs_used")
    v_staged = core.semaphore("att_v_staged")
    sums_copied = core.semaphore("att_sums_copied")
    inv_ready = core.semaphore("att_inverse_ready")
    pad_set = core.semaphore("att_v_pad_set")

    PROLOGUE = plan_side(list(range(GROUP)), GROUP, 0, False)
    FIRST = plan_side(list(range(GROUP, GROUP + AHEAD)), GROUP, 10, False)
    STEADY = plan_side([AHEAD + i for i in range(GROUP)], 2, 10, True, whole=1)
    LATE = plan_side([AHEAD, AHEAD + 1], 2, 2, True)
    LAST = plan_side([], None, 0, True)
    assert len(STEADY) % 2 == 0
    STEADY_GROUPS = (1, GROUPS - 2)
    before = {0: len(PROLOGUE)}
    before[1] = before[0] + len(FIRST)
    for g in range(2, GROUPS - 1):
        before[g] = before[g - 1] + len(STEADY)
    before[GROUPS - 1] = before[GROUPS - 2] + len(LATE)
    SIDE = before[GROUPS - 1] + 2 * len(LAST)
    SPLIT = 7
    with ExitStack() as ctx:
        def sb(name, shape, dt=F32):
            return core.sbuf(ctx, name, shape, dt)

        side_ps = core.psum(ctx, "side_ps", [P, 2, CW])
        score_ps = core.psum(ctx, "score_ps", [P, 2, SEQ])
        sums_ps = core.psum(ctx, "sums_ps", [P, SEQ])
        probs = sb("probs", [P, 2, GROUP, SEQ])
        v_group = sb("v_group", [P, GROUP, SEQ_TILES, SLOT])
        sums = sb("sums", [P, SEQ])
        negmax = sb("negmax", [P, ALL_HEADS * (SEQ_TILES + CHUNK)])
        group_max = sb("group_max", [P, GROUP, SEQ_TILES])
        parts = sb("parts", [P, 3, UNITS], BF16)
        rows = sb("rows", [P, P], BF16)
        inverse = sb("inverse", [P, 2, CHUNK, GROUP])
        block = ctx.enter_context(nc.Block())
        COLS = SEQ_TILES + CHUNK
        eye = field(core.masks, MASKS, "ident")

        def column(qt, k0):
            return qt if k0 == 0 else SEQ_TILES + qt - CHUNK

        def seen(qt, k0):
            n, m, mask = key_tiles(qt, rotary)
            return min(n - k0, CHUNK), m, mask

        @block.tensor
        def _(pe):
            def side(work, g, n, n0, base):
                pe.wait_ge(side_free.sem, n + side_free.at(n0 + 1))
                bank = side_ps[:, (base + n0) % 2, :]
                if work[0] == "rows":
                    pe.wait_ge(split.sem, (g + 1) * SPLIT + split.at(SPLIT))
                    pe.transpose(bank.bitcast(BF16)[0:3 * UNITS, 0:P], parts[:, :, :].rearrange("p a u -> p (a u)"),
                                 eye).then_inc(side_ready.sem, 1)
                    return
                if work[0] == "turn":
                    if work[1] == 0:
                        pe.wait_ge(sums_copied.sem, g + sums_copied.at(0))
                    for i in range(CHUNK):
                        t = work[1] * CHUNK + i
                        last = pe.transpose(bank[:, i * P:(i + 1) * P], sums[:, t * P:(t + 1) * P], core.ident)
                    last.then_inc(side_ready.sem, 1)
                    return
                head = g * GROUP + work[1]
                at = 0
                for qt, k0 in work[2]:
                    n_keys, m, mask = seen(qt, k0)
                    out = bank[:, at:at + n_keys * P]
                    here = k0 <= m < k0 + n_keys
                    if here:
                        pe.matmul(out[:, (m - k0) * P:(m - k0 + 1) * P], eye, field(core.masks, MASKS, mask),
                                  start=True, stop=False, skip_group_check=True)
                    last = pe.matmul(out, q_stack[0:ROW_MAX, bass.ds(head * SEQ + qt * P, P)],
                                     k_stack[0:ROW_MAX, bass.ds(head * SEQ + k0 * P, n_keys * P)],
                                     start=not here, stop=True, skip_group_check=here)
                    at += n_keys * P
                last.then_inc(side_ready.sem, 1)

            def score(g, kt, j):
                n = kt * GROUP + j
                if n == 0:
                    pe.wait_ge(rows_stacked.sem, g * 48 + rows_stacked.at(48))
                pe.wait_ge(exp_done.sem, g * UNITS + exp_done.at(n + 1))
                head = g * GROUP + j
                w = width(kt, rotary)
                q0 = SEQ - w
                mask = None if rotary and kt == 0 else "rot_T" if rotary and kt == 1 else "diag_T"
                for s in range(0, w, CW):
                    e = min(s + CW, w)
                    here = mask is not None and s == 0
                    if here:
                        at = MASKS[mask][1]
                        pe.matmul(score_ps[:, n % 2, 0:at], eye, field(core.masks, MASKS, mask), start=True,
                                  stop=False, skip_group_check=True)
                    last = pe.matmul(score_ps[:, n % 2, s:e], k_stack[0:ROWS, bass.ds(head * SEQ + kt * P, P)],
                                     q_stack[0:ROWS, bass.ds(head * SEQ + q0 + s, e - s)], start=not here,
                                     stop=True, skip_group_check=here)
                last.then_inc(scores_ready.sem, 1)

            def weigh(g, kt, a, b, is_last, first_group):
                if kt == 0 and a == 0:
                    pe.wait_ge(v_staged.sem, g + v_staged.at(1))
                    if not first_group:
                        pe.wait_ge(sums_copied.sem, g + sums_copied.at(0))
                if a == max(query_spans(kt, rotary)[0][0], 0):
                    pe.wait_ge(exp_done.sem, g * UNITS + exp_done.at(2 + GROUP * (kt + 1)))
                q0 = first_query_tile(kt, rotary) * P
                for j in range(GROUP):
                    last = pe.matmul(sums_ps[j * SLOT:(j + 1) * SLOT, a:b], v_group[:, j, kt, :],
                                     probs[:, kt % 2, j, a - q0:b - q0], start=kt == 0,
                                     stop=kt == SEQ_TILES - 1, skip_group_check=True)
                if is_last:
                    last.then_inc(weighed.sem, 1)

            def step(g, plan, n, base, first_group=False):
                for what in interleave(plan, rotary):
                    if what[0] == "side":
                        side(plan[what[1]], g, n, what[1], base)
                    elif what[0] == "score":
                        score(g, *what[1:])
                    else:
                        weigh(g, *what[1:], first_group)

            for i, work in enumerate(PROLOGUE):
                side(work, 0 if work[0] != "rows" else -1, 0, i, 0)
            step(0, FIRST, before[0], before[0], True)
            with pe.Fori(*STEADY_GROUPS) as g:
                step(g, STEADY, (g - 1) * len(STEADY) + before[1], before[1])
            step(GROUPS - 2, LATE, before[GROUPS - 2], before[GROUPS - 2])
            step(GROUPS - 1, LAST, before[GROUPS - 1], before[GROUPS - 1])
            for i, work in enumerate(LAST):
                n = before[GROUPS - 1] + len(LAST)
                side(work, GROUPS, n, i, n)

        @block.vector
        def _(dve):
            dve.sem_inc(side_free.sem, 2)

            def side(work, g, n, n0, base):
                dve.wait_ge(side_ready.sem, n + side_ready.at(n0 + 1))
                bank = side_ps[:, (base + n0) % 2, :]
                if work[0] == "rows":
                    dve.tensor_copy(rows[0:3 * UNITS, :], bank.bitcast(BF16)[0:3 * UNITS, 0:P]).then_inc(side_free.sem, 1)
                    return
                if work[0] == "turn":
                    tiles = bank.rearrange("p (t j d) -> p t j d", t=CHUNK, j=GROUP)
                    dve.reciprocal(inverse[:, work[1], :, :], tiles[:, :, :, DH]).then_inc(inv_ready.sem, 1)
                    dve.wait_ge(inv_ready.sem, (g - 1) * 2 + inv_ready.at(work[1] + 1))
                    out = o_tok[:, work[1] * CHUNK:(work[1] + 1) * CHUNK, bass.ds(g - 1, 1), :]
                    dve.tensor_tensor(out.rearrange("p t o (j d) -> p t (o j) d", j=GROUP), tiles[:, :, :, 0:DH],
                                      inverse[:, work[1], :, :, None].to_broadcast([P, CHUNK, GROUP, DH]),
                                      ALU.mult).then_inc(side_free.sem, 1)
                    return
                head = g * GROUP + work[1]
                at = 0
                for qt, k0 in work[2]:
                    n_keys = seen(qt, k0)[0]
                    last = dve.tensor_reduce(negmax[:, bass.ds(head * COLS + column(qt, k0), 1)],
                                             bank[:, at:at + n_keys * P], AX.X, ALU.max, negate=True)
                    at += n_keys * P
                last.then_inc(side_free.sem, 1)
                if work[0] == "settle":
                    dve.wait_ge(side_free.sem, n + side_free.at(n0 + 3))
                    settle(g + 1 if base else 0)

            def settle(g):
                own = negmax[:, bass.ds(g * (GROUP * COLS), GROUP * COLS)].rearrange("p (j c) -> p j c", c=COLS)
                flat = group_max[:, :, :].rearrange("p j t -> p (j t)")
                dve.tensor_copy(group_max[:, :, 0:CHUNK], own[:, :, 0:CHUNK]).then_inc(split.sem, 1)
                dve.tensor_tensor(group_max[:, :, CHUNK:SEQ_TILES], own[:, :, CHUNK:SEQ_TILES],
                                  own[:, :, SEQ_TILES:COLS], ALU.min).then_inc(split.sem, 1)
                dve.wait_ge(split.sem, g * SPLIT + split.at(2))
                dve.tensor_copy(parts[:, 0, :], flat).then_inc(split.sem, 1)
                dve.wait_ge(split.sem, g * SPLIT + split.at(3))
                dve.tensor_tensor(flat, flat, parts[:, 0, :], ALU.subtract).then_inc(split.sem, 1)
                dve.wait_ge(split.sem, g * SPLIT + split.at(4))
                dve.tensor_copy(parts[:, 1, :], flat).then_inc(split.sem, 1)
                dve.wait_ge(split.sem, g * SPLIT + split.at(5))
                dve.tensor_tensor(flat, flat, parts[:, 1, :], ALU.subtract).then_inc(split.sem, 1)
                dve.wait_ge(split.sem, g * SPLIT + split.at(6))
                dve.tensor_copy(parts[:, 2, :], flat).then_inc(split.sem, 1)

            for i, work in enumerate(PROLOGUE):
                side(work, 0, 0, i, 0)
            for i, work in enumerate(FIRST):
                side(work, 0, before[0], i, before[0])
            with dve.Fori(*STEADY_GROUPS) as g:
                for i, work in enumerate(STEADY):
                    side(work, g, (g - 1) * len(STEADY) + before[1], i, before[1])
            for g, plan in ((GROUPS - 2, LATE), (GROUPS - 1, LAST)):
                for i, work in enumerate(plan):
                    side(work, g, before[g], i, before[g])
            n = before[GROUPS - 1] + len(LAST)
            for i, work in enumerate(LAST):
                side(work, GROUPS, n, i, n)

        @block.scalar
        def _(act):
            act.sem_inc(exp_done.sem, 2)

            def copy_sums(g):
                act.wait_ge(weighed.sem, g * SEQ_TILES + weighed.at(2))
                act.copy(sums[:, :], sums_ps[:, :]).then_inc(sums_copied.sem, 1)

            def group(g, first_group):
                for n in range(UNITS):
                    kt, j = divmod(n, GROUP)
                    act.wait_ge(scores_ready.sem, g * UNITS + scores_ready.at(n + 1))
                    if j == 0:
                        act.wait_ge(weighed.sem, g * SEQ_TILES + weighed.at(kt + 1))
                    w = width(kt, rotary)
                    act.activation(probs[:, kt % 2, j, 0:w], score_ps[:, n % 2, 0:w],
                                   ACT.Exp).then_inc(exp_done.sem, 1)
                    if n == 1 and not first_group:
                        copy_sums(g)

            group(0, True)
            with act.Fori(1, GROUPS) as g:
                group(g, False)
            copy_sums(GROUPS)

        @block.gpsimd
        def _(pool):
            pool.sem_inc(weighed.sem, 2)
            pool.memset(v_group[:, :, :, :], 0.0).then_inc(pad_set.sem, 1)
            pool.wait_ge(pad_set.sem, pad_set.at(1))
            with pool.Fori(0, GROUPS) as g:
                pool.wait_ge(weighed.sem, g * SEQ_TILES + weighed.at(2))
                pool.tensor_copy(v_group[:, :, :, 0:DH + 1], v_tok[:, bass.ds(g * GROUP, GROUP), :, :]
                                 ).then_inc(v_staged.sem, 1)

        @block.sync
        def _(sp):
            def stack(g, n):
                sp.wait_ge(side_free.sem, n)
                for a in range(3):
                    dst = q_stack[ROW_MAX + a:ROW_MAX + a + 1, bass.ds(g * GROUP * SEQ, GROUP * SEQ)]
                    sp.dma_start(dst.rearrange("o (u n) -> o u n", n=P), rows[a * UNITS:(a + 1) * UNITS, :]
                                 ).then_inc(rows_stacked.sem, 16)

            stack(0, side_free.at(2 + PROLOGUE.index(("rows",)) + 1))
            stack(1, side_free.at(2 + before[0] + FIRST.index(("rows",)) + 1))
            with sp.Fori(*STEADY_GROUPS) as g:
                stack(g + 1, (g - 1) * len(STEADY) + side_free.at(2 + before[1] + STEADY.index(("rows",)) + 1))
            stack(GROUPS - 1, side_free.at(2 + before[GROUPS - 2] + LATE.index(("rows",)) + 1))
            sp.wait_ge(rows_stacked.sem, rows_stacked.at(48 * GROUPS))

    side_ready.passed(SIDE)
    side_free.passed(SIDE + 2)
    split.passed(SPLIT * GROUPS)
    rows_stacked.passed(48 * GROUPS)
    scores_ready.passed(UNITS * GROUPS)
    exp_done.passed(UNITS * GROUPS + 2)
    weighed.passed(SEQ_TILES * GROUPS + 2)
    v_staged.passed(GROUPS)
    sums_copied.passed(GROUPS)
    inv_ready.passed(2 * GROUPS)
    pad_set.passed(1)


def stage_project(core, x, w_out, o_tok=None, o_all=None, bo=None, shift=0):
    nc = core.nc
    turned = core.semaphore("prj_turned")
    oT_ready = core.semaphore("prj_oT_ready")
    product = core.semaphore("prj_product_ready")
    added = core.semaphore("prj_added")

    def rows_of(t):
        if o_all is not None:
            return o_all[:, t, :]
        b, t = divmod(t, SEQ_TILES)
        own = o_tok[:, t, b * (GROUPS // BATCH):(b + 1) * (GROUPS // BATCH), :]
        return own.rearrange("p g f -> p (g f)")

    HALVES = 2
    with ExitStack() as ctx:
        oT = core.sbuf(ctx, "oT", [P, BATCH, SEQ], F32)
        turned_ps = core.psum(ctx, "turned_ps", [P, 2, CW], F32)
        prod_ps = core.psum(ctx, "prod_ps", [P, 2, CW], F32)
        block = ctx.enter_context(nc.Block())

        @block.tensor
        def _(pe):
            for c in range(CHUNKS):
                if c >= 2:
                    pe.wait_ge(oT_ready.sem, oT_ready.at(c - 1))
                for j in range(CHUNK):
                    last = pe.transpose(turned_ps[:, c % 2, j * P:(j + 1) * P], rows_of(CHUNK * c + j),
                                        core.ident)
                last.then_inc(turned.sem, 1)
                if c % HALVES != HALVES - 1:
                    continue
                b = c // HALVES
                pe.wait_ge(oT_ready.sem, oT_ready.at(c + 1))
                for half in range(HALVES):
                    if b >= 1:
                        pe.wait_ge(added.sem, added.at(HALVES * (b - 1) + half + 1))
                    for j in range(CHUNK):
                        t = half * CHUNK + j
                        out = prod_ps[:, half, j * P:(j + 1) * P]
                        last = pe.matmul(out, oT[:, b, t * P:(t + 1) * P], w_out, start=True, stop=bo is None)
                        if bo is not None:
                            last = pe.matmul(out, core.ones[0:1, :], bo[0:1, :], start=False, stop=True)
                    last.then_inc(product.sem, 1)

        @block.scalar
        def _(act):
            for c in range(CHUNKS):
                b, half = divmod(c, HALVES)
                act.wait_ge(turned.sem, turned.at(c + 1))
                first = (half * CW - shift) % SEQ
                w = min(CW, SEQ - first)
                last = act.copy(oT[:, b, first:first + w], turned_ps[:, c % 2, 0:w])
                if w < CW:
                    last = act.copy(oT[:, b, 0:CW - w], turned_ps[:, c % 2, w:CW])
                last.then_inc(oT_ready.sem, 1)

        @block.vector
        def _(dve):
            for c in range(CHUNKS):
                dve.wait_ge(product.sem, product.at(c + 1))
                xc = x[:, CHUNK * c:CHUNK * (c + 1), :].rearrange("p t d -> p (t d)")
                dve.tensor_tensor(xc, prod_ps[:, c % HALVES, :], xc, ALU.add).then_inc(added.sem, 1)

    for s in (turned, oT_ready, product, added):
        s.passed(CHUNKS)


def top_two(dve, step, scores, rank, picks, best, work):
    wide = [P, TILES, EXPERTS]
    left, equal, order = work
    n = [0]

    def then(ins, wait=True):
        ins.then_inc(step.sem, 1)
        n[0] += 1
        if wait:
            dve.wait_ge(step.sem, step.at(n[0]))

    here = scores
    for i in range(2):
        top = best[:, i, :]
        then(dve.tensor_reduce(top, here, AX.X, ALU.max))
        then(dve.tensor_tensor(equal, here, top[:, :, None].to_broadcast(wide), ALU.is_equal))
        then(dve.tensor_tensor(equal, equal, rank[:, None, :].to_broadcast(wide), ALU.mult))
        then(dve.tensor_reduce(order, equal, AX.X, ALU.max))
        then(dve.tensor_tensor(picks[:, i, :, :], equal, order[:, :, None].to_broadcast(wide), ALU.is_equal))
        if i == 0:
            then(dve.scalar_tensor_tensor(left, picks[:, 0, :, :], -4.0, scores, ALU.mult, ALU.add))
            here = left
    return n[0]


TOP_TWO_STEPS = 11


def stage_experts(core, x, xT, weights):
    nc = core.nc
    logits_ready = core.semaphore("moe_logits_ready")
    probs_ready = core.semaphore("moe_probs_ready")
    step = core.semaphore("moe_route_step")
    hidden_ready = core.semaphore("moe_hidden_ready")
    relu_ready = core.semaphore("moe_relu_ready")
    square_ready = core.semaphore("moe_square_ready")
    out_ready = core.semaphore("moe_out_ready")
    added = core.semaphore("moe_added")
    blocks_done = core.semaphore("moe_block_used")
    rank = field(core.const, CONST, "rank")
    BUF = 4
    firsts = [sum(EXPERT_BLOCKS[:e]) for e in range(EXPERTS)]
    with ExitStack() as ctx:
        def sb(name, shape, dt=F32):
            return core.sbuf(ctx, name, shape, dt)

        logits_ps = core.psum(ctx, "logits_ps", [P, CW], F32)
        hidden_ps = core.psum(ctx, "hidden_ps", [P, BUF, CW], F32)
        out_ps = core.psum(ctx, "out_ps", [P, 2, CW], F32)
        probs = sb("probs", [P, TILES, EXPERTS])
        left = sb("left", [P, TILES, EXPERTS])
        equal = sb("equal", [P, TILES, EXPERTS])
        order = sb("order", [P, TILES])
        picks = sb("picks", [P, 2, TILES, EXPERTS])
        best = sb("best", [P, 2, TILES])
        total = sb("total", [P, TILES])
        share = sb("share", [P, TILES, EXPERTS])
        relu = sb("relu", [P, BUF, CW])
        square = sb("square", [P, BUF, CW])
        block = ctx.enter_context(nc.Block())
        ROUTE = TOP_TWO_STEPS + 6

        @block.tensor
        def _(pe):
            for t in range(TILES):
                last = pe.matmul(logits_ps[:, t * EXPERTS:(t + 1) * EXPERTS], xT[:, t * P:(t + 1) * P],
                                 field(weights, W_MOE, "router"), start=True, stop=True)
            last.then_inc(logits_ready.sem, 1)
            w1, w2 = field(weights, W_MOE, "w1"), field(weights, W_MOE, "w2")

            def up(c, m):
                pe.wait_ge(square_ready.sem, c * HIDDEN_BLOCKS + square_ready.at(m + 1))
                pe.matmul(hidden_ps[:, m % BUF, :], w1[:, m * P:(m + 1) * P], xT[:, bass.ds(c * CW, CW)],
                          start=True, stop=True).then_inc(hidden_ready.sem, 1)

            def down(c, e):
                m0, n = firsts[e], EXPERT_BLOCKS[e]
                pe.wait_ge(square_ready.sem, c * HIDDEN_BLOCKS + square_ready.at(BUF + m0 + n))
                pe.wait_ge(added.sem, c * EXPERTS + added.at(e + 1))
                for j in range(CHUNK):
                    for i in range(n):
                        m = m0 + i
                        last = pe.matmul(out_ps[:, e % 2, j * P:(j + 1) * P],
                                         square[:, m % BUF, j * P:(j + 1) * P], w2[:, m * P:(m + 1) * P],
                                         start=i == 0, stop=i == n - 1)
                last.then_inc(out_ready.sem, 1)

            with pe.Fori(0, CHUNKS) as c:
                for e in range(EXPERTS + 1):
                    if e < EXPERTS:
                        for i in range(EXPERT_BLOCKS[e]):
                            up(c, firsts[e] + i)
                    if e >= 1:
                        down(c, e - 1)

        @block.scalar
        def _(act):
            act.wait_ge(logits_ready.sem, logits_ready.at(1))
            act.activation(probs[:, :, :].rearrange("p t e -> p (t e)"), logits_ps[:, 0:TILES * EXPERTS],
                           ACT.Sigmoid).then_inc(probs_ready.sem, 1)
            with act.Fori(0, CHUNKS) as c:
                for m in range(HIDDEN_BLOCKS):
                    act.wait_ge(hidden_ready.sem, c * HIDDEN_BLOCKS + hidden_ready.at(m + 1))
                    act.wait_ge(square_ready.sem, c * HIDDEN_BLOCKS + square_ready.at(m + 1))
                    act.activation(relu[:, m % BUF, :], hidden_ps[:, m % BUF, :], ACT.Relu).then_inc(relu_ready.sem, 1)

        @block.vector
        def _(dve):
            dve.sem_inc(square_ready.sem, BUF)
            dve.sem_inc(added.sem, 2)
            dve.wait_ge(probs_ready.sem, probs_ready.at(1))
            n = top_two(dve, step, probs[:, :, :], rank, picks, best, (left[:, :, :], equal[:, :, :], order[:, :]))
            dve.tensor_tensor(total[:, :], best[:, 0, :], best[:, 1, :], ALU.add).then_inc(step.sem, 1)
            dve.wait_ge(step.sem, step.at(n + 1))
            dve.tensor_scalar(total[:, :], total[:, :], 1e-20, None, ALU.add).then_inc(step.sem, 1)
            dve.wait_ge(step.sem, step.at(n + 2))
            dve.reciprocal(total[:, :], total[:, :]).then_inc(step.sem, 1)
            dve.wait_ge(step.sem, step.at(n + 3))
            dve.tensor_tensor(share[:, :, :], picks[:, 0, :, :], picks[:, 1, :, :], ALU.add).then_inc(step.sem, 1)
            dve.wait_ge(step.sem, step.at(n + 4))
            dve.tensor_tensor(share[:, :, :], share[:, :, :], probs[:, :, :], ALU.mult).then_inc(step.sem, 1)
            dve.wait_ge(step.sem, step.at(n + 5))
            dve.tensor_tensor(share[:, :, :], share[:, :, :],
                              total[:, :, None].to_broadcast([P, TILES, EXPERTS]), ALU.mult).then_inc(step.sem, 1)
            dve.wait_ge(step.sem, step.at(n + 6))

            def square_of(c, m):
                dve.wait_ge(relu_ready.sem, c * HIDDEN_BLOCKS + relu_ready.at(m + 1))
                dve.wait_ge(out_ready.sem, used(c, m))
                dve.scalar_tensor_tensor(square[:, m % BUF, :], hidden_ps[:, m % BUF, :], 0.0, relu[:, m % BUF, :],
                                         ALU.max, ALU.mult).then_inc(square_ready.sem, 1)

            def used(c, m):
                before = m - BUF
                e = [i for i in range(EXPERTS) for _ in range(EXPERT_BLOCKS[i])]
                if before < 0:
                    return c * EXPERTS + out_ready.at(e[before + HIDDEN_BLOCKS] + 1 - EXPERTS)
                return c * EXPERTS + out_ready.at(e[before] + 1)

            def add(c, e):
                dve.wait_ge(out_ready.sem, c * EXPERTS + out_ready.at(e + 1))
                dve.wait_ge(added.sem, c * EXPERTS + added.at(e + 2))
                for j in range(CHUNK):
                    t = c * CHUNK + j
                    xt = x[:, bass.ds(t, 1), :].rearrange("p o d -> p (o d)")
                    s = share[:, bass.ds(t, 1), e]
                    last = dve.scalar_tensor_tensor(xt, out_ps[:, e % 2, j * P:(j + 1) * P], s, xt,
                                                    ALU.mult, ALU.add)
                last.then_inc(added.sem, 1)

            def chunk(c, first):
                m = 0
                for e in range(EXPERTS + 2):
                    if e < EXPERTS:
                        for _ in range(EXPERT_BLOCKS[e]):
                            if first and m < BUF:
                                dve.wait_ge(relu_ready.sem, relu_ready.at(m + 1))
                                dve.scalar_tensor_tensor(square[:, m % BUF, :], hidden_ps[:, m % BUF, :], 0.0,
                                                         relu[:, m % BUF, :], ALU.max,
                                                         ALU.mult).then_inc(square_ready.sem, 1)
                            else:
                                square_of(c, m)
                            m += 1
                    if e >= 2:
                        add(c, e - 2)

            chunk(0, True)
            with dve.Fori(1, CHUNKS) as c:
                chunk(c, False)

    logits_ready.passed(1)
    probs_ready.passed(1)
    step.passed(ROUTE)
    for s in (hidden_ready, relu_ready):
        s.passed(CHUNKS * HIDDEN_BLOCKS)
    square_ready.passed(BUF + CHUNKS * HIDDEN_BLOCKS)
    out_ready.passed(CHUNKS * EXPERTS)
    added.passed(2 + CHUNKS * EXPERTS)


def stage_pair(core, x, xT, weights):
    nc = core.nc
    vo_ready = core.semaphore("pair_vo_product")
    vo_copied = core.semaphore("pair_vo_copied")
    staged = core.semaphore("pair_tiles_staged")
    step = core.semaphore("pair_stage_step")
    q_ready = core.semaphore("pair_q_ready")
    k_ready = core.semaphore("pair_k_ready")
    v_ready = core.semaphore("pair_v_ready")
    q_copied = core.semaphore("pair_q_copied")
    prod_ready = core.semaphore("pair_qk_ready")
    chain = core.semaphore("pair_softmax_step")
    exp_ready = core.semaphore("pair_exp_ready")
    ctx_ready = core.semaphore("pair_context_ready")
    turned = core.semaphore("pair_half_turned")
    copied = core.semaphore("pair_half_copied")
    out_ready = core.semaphore("pair_out_ready")
    added = core.semaphore("pair_added")
    HALF = PAIR_BLOCKS // 2
    CHAIN = 8
    with ExitStack() as ctx:
        def sb(name, shape, dt=F32):
            return core.sbuf(ctx, name, shape, dt)

        q_ps = core.psum(ctx, "q_ps", [P, PAIR_W])
        k_ps = core.psum(ctx, "k_ps", [P, PAIR_W])
        v_ps = core.psum(ctx, "v_ps", [P, PAIR_W])
        turned_ps = core.psum(ctx, "turned_ps", [P, CW])
        out_ps = core.psum(ctx, "out_ps", [P, CW])
        vo = sb("vo", [P, P])
        y0 = sb("y0", [P, 2, P])
        y1 = sb("y1", [P, 2, P])
        dy = sb("dy", [P, 2, P])
        q = sb("q", [P, PAIR_W])
        prod = sb("prod", [P, PAIR_W])
        d = sb("d", [P, PAIR_HEADS])
        top = sb("top", [P, PAIR_HEADS])
        shifted = sb("shifted", [P, 2, PAIR_HEADS])
        e = sb("e", [P, 2, PAIR_HEADS])
        total = sb("total", [P, PAIR_HEADS])
        p1 = sb("p1", [P, PAIR_HEADS])
        context = sb("context", [P, PAIR_W])
        contextT = sb("contextT", [P, PAIR_W])
        block = ctx.enter_context(nc.Block())

        @block.gpsimd
        def _(pool):
            def stage(t, buf, used):
                if used:
                    pool.wait_ge(out_ready.sem, t + out_ready.at(0))
                a0 = xT[:, bass.ds(t * P, P)]
                a1 = xT[:, bass.ds(SEQ + t * P, P)]
                pool.tensor_copy(y0[:, buf, :], a0)
                pool.tensor_copy(y1[:, buf, :], a1)
                pool.tensor_tensor(dy[:, buf, :], a1, a0, ALU.subtract).then_inc(staged.sem, 1)

            stage(0, 0, False)
            stage(1, 1, False)
            with pool.Fori(1, SEQ_TILES // 2) as i:
                for buf in range(2):
                    stage(i * 2 + buf, buf, True)

        @block.tensor
        def _(pe):
            pe.sem_inc(turned.sem, 2)
            pe.sem_inc(out_ready.sem, 1)
            for m in range(PAIR_BLOCKS):
                last = pe.matmul(out_ps[:, 0:P], field(weights, W_PAIR, "v_T")[:, m * P:(m + 1) * P],
                                 field(weights, W_PAIR, "out")[:, m * P:(m + 1) * P],
                                 start=m == 0, stop=m == PAIR_BLOCKS - 1)
            last.then_inc(vo_ready.sem, 1)
            pe.wait_ge(vo_copied.sem, vo_copied.at(1))

            def product(out, lhs, name, ready):
                for k0 in range(0, PAIR_W, CW):
                    last = pe.matmul(out[:, k0:k0 + CW], lhs, field(weights, W_PAIR, name)[:, k0:k0 + CW],
                                     start=True, stop=True)
                last.then_inc(ready.sem, 1)

            def turn(t, half):
                pe.wait_ge(ctx_ready.sem, t + ctx_ready.at(2))
                pe.wait_ge(copied.sem, t * 2 + copied.at(half + 1))
                for m in range(HALF):
                    at = (half * HALF + m) * P
                    last = pe.transpose(turned_ps[:, m * P:(m + 1) * P], context[:, at:at + P], core.ident)
                last.then_inc(turned.sem, 1)

            def out(t, buf):
                pe.wait_ge(copied.sem, t * 2 + copied.at(3))
                pe.wait_ge(added.sem, t + added.at(1))
                pe.matmul(out_ps[:, 0:P], y0[:, buf, :], vo[:, :], start=True, stop=True)
                pe.matmul(out_ps[:, P:2 * P], y0[:, buf, :], vo[:, :], start=True, stop=False)
                for m in range(PAIR_BLOCKS):
                    last = pe.matmul(out_ps[:, P:2 * P], contextT[:, m * P:(m + 1) * P],
                                     field(weights, W_PAIR, "out")[:, m * P:(m + 1) * P],
                                     start=False, stop=m == PAIR_BLOCKS - 1)
                last.then_inc(out_ready.sem, 1)

            def tile(t, buf, back):
                pe.wait_ge(staged.sem, t + staged.at(1))
                pe.wait_ge(q_copied.sem, t + q_copied.at(1))
                product(q_ps, y1[:, buf, :], "q", q_ready)
                if back:
                    turn(t - 1, 0)
                pe.wait_ge(prod_ready.sem, t + prod_ready.at(1))
                product(k_ps, dy[:, buf, :], "k", k_ready)
                if back:
                    turn(t - 1, 1)
                pe.wait_ge(ctx_ready.sem, t + ctx_ready.at(1))
                product(v_ps, dy[:, buf, :], "v", v_ready)
                if back:
                    out(t - 1, 1 - buf)

            tile(0, 0, False)
            with pe.Fori(0, SEQ_TILES // 2 - 1) as i:
                tile(i * 2 + 1, 1, True)
                tile(i * 2 + 2, 0, True)
            tile(SEQ_TILES - 1, 1, True)
            turn(SEQ_TILES - 1, 0)
            turn(SEQ_TILES - 1, 1)
            out(SEQ_TILES - 1, 1)

        @block.scalar
        def _(act):
            act.sem_inc(q_copied.sem, 1)
            act.sem_inc(copied.sem, 1)
            act.wait_ge(vo_ready.sem, vo_ready.at(1))
            act.copy(vo[:, :], out_ps[:, 0:P]).then_inc(vo_copied.sem, 1)

            def halves(t):
                for half in range(2):
                    act.wait_ge(turned.sem, t * 2 + turned.at(half + 3))
                    if half == 0:
                        act.wait_ge(out_ready.sem, t + out_ready.at(1))
                    act.copy(contextT[:, half * CW:(half + 1) * CW], turned_ps[:, :]).then_inc(copied.sem, 1)

            def tile(t, back):
                act.wait_ge(q_ready.sem, t + q_ready.at(1))
                act.wait_ge(prod_ready.sem, t + prod_ready.at(1))
                act.copy(q[:, :], q_ps[:, :]).then_inc(q_copied.sem, 1)
                if back:
                    halves(t - 1)
                act.wait_ge(chain.sem, t * CHAIN + chain.at(5))
                act.activation(e[:, :, :], shifted[:, :, :], ACT.Exp).then_inc(exp_ready.sem, 1)

            tile(0, False)
            with act.Fori(1, SEQ_TILES) as t:
                tile(t, True)
            halves(SEQ_TILES - 1)

        @block.vector
        def _(dve):
            dve.sem_inc(prod_ready.sem, 1)
            dve.sem_inc(ctx_ready.sem, 1)
            dve.sem_inc(added.sem, 1)

            def tile(t, back):
                def then(ins, n):
                    ins.then_inc(chain.sem, 1)
                    dve.wait_ge(chain.sem, t * CHAIN + chain.at(n))

                dve.wait_ge(q_copied.sem, t + q_copied.at(2))
                dve.wait_ge(k_ready.sem, t + k_ready.at(1))
                dve.tensor_tensor(prod[:, :], k_ps[:, :], q[:, :], ALU.mult).then_inc(prod_ready.sem, 1)
                dve.wait_ge(prod_ready.sem, t + prod_ready.at(2))
                then(dve.tensor_reduce(d[:, :], prod[:, :].rearrange("p (h d) -> p h d", d=PAIR_DH), AX.X, ALU.add), 1)
                then(dve.tensor_scalar(d[:, :], d[:, :], PAIR_DH ** -0.5, None, ALU.mult), 2)
                then(dve.tensor_scalar(top[:, :], d[:, :], 0.0, None, ALU.max), 3)
                then(dve.tensor_scalar(shifted[:, 0, :], top[:, :], -1.0, None, ALU.mult), 4)
                dve.tensor_tensor(shifted[:, 1, :], d[:, :], top[:, :], ALU.subtract).then_inc(chain.sem, 1)
                dve.wait_ge(exp_ready.sem, t + exp_ready.at(1))
                then(dve.tensor_tensor(total[:, :], e[:, 0, :], e[:, 1, :], ALU.add), 6)
                then(dve.reciprocal(total[:, :], total[:, :]), 7)
                then(dve.tensor_tensor(p1[:, :], e[:, 1, :], total[:, :], ALU.mult), 8)
                dve.wait_ge(v_ready.sem, t + v_ready.at(1))
                dve.wait_ge(turned.sem, t * 2 + turned.at(2))
                dve.tensor_tensor(context[:, :].rearrange("p (h d) -> p h d", d=PAIR_DH),
                                  v_ps[:, :].rearrange("p (h d) -> p h d", d=PAIR_DH),
                                  p1[:, :, None].to_broadcast([P, PAIR_HEADS, PAIR_DH]),
                                  ALU.mult).then_inc(ctx_ready.sem, 1)
                if back:
                    add(t - 1)

            def add(t):
                dve.wait_ge(out_ready.sem, t + out_ready.at(2))
                for b in range(BATCH):
                    xt = x[:, bass.ds(b * SEQ_TILES + t, 1), :].rearrange("p o d -> p (o d)")
                    last = dve.tensor_tensor(xt, out_ps[:, b * P:(b + 1) * P], xt, ALU.add)
                last.then_inc(added.sem, 1)

            tile(0, False)
            with dve.Fori(1, SEQ_TILES) as t:
                tile(t, True)
            add(SEQ_TILES - 1)

    for s in (vo_ready, vo_copied):
        s.passed(1)
    for s in (staged, q_ready, k_ready, v_ready, exp_ready):
        s.passed(SEQ_TILES)
    for s in (q_copied, prod_ready, ctx_ready, added, out_ready):
        s.passed(SEQ_TILES + 1)
    chain.passed(CHAIN * SEQ_TILES)
    turned.passed(2 * SEQ_TILES + 2)
    copied.passed(2 * SEQ_TILES + 1)


def stage_recurrence(core, xT, weights, o_all):
    nc = core.nc
    feat_ready = core.semaphore("rec_features_ready")
    vq_ready = core.semaphore("rec_gelu_ready")
    f_copied = core.semaphore("rec_gates_copied")
    f_ready = core.semaphore("rec_sigmoid_ready")
    chain = core.semaphore("rec_step")
    BANKS = 8
    E = 2
    with ExitStack() as ctx:
        def sb(name, shape, dt=F32):
            return core.sbuf(ctx, name, shape, dt)

        feat_ps = core.psum(ctx, "feat_ps", [P, BANKS, CW])
        vq = sb("vq", [P, TILES, 2 * P])
        gates = sb("gates", [P, TILES, P])
        keys = sb("keys", [P, TILES, P])
        spare = sb("spare", [P, SEQ_TILES, P])
        dots = sb("dots", [P, 3, SEQ_TILES, P // E])
        rest = sb("rest", [P, P])
        block = ctx.enter_context(nc.Block())
        lower = field(weights, W_REC, "lower")
        N0, N1 = slice(0, SEQ_TILES), slice(SEQ_TILES, TILES)

        @block.tensor
        def _(pe):
            for t in range(TILES):
                if t >= BANKS:
                    pe.wait_ge(vq_ready.sem, vq_ready.at(t - BANKS + 1))
                pe.matmul(feat_ps[:, t % BANKS, 0:3 * P], xT[:, t * P:(t + 1) * P], field(weights, W_REC, "in"),
                          start=True, stop=True).then_inc(feat_ready.sem, 1)

        @block.scalar
        def _(act):
            for t in range(TILES):
                act.wait_ge(f_copied.sem, f_copied.at(t + 1))
                act.activation(vq[:, t, :], feat_ps[:, t % BANKS, 0:2 * P], ACT.Gelu).then_inc(vq_ready.sem, 1)
            for half in (N0, N1):
                act.wait_ge(f_copied.sem, f_copied.at(half.stop))
                act.activation(gates[:, half, :], gates[:, half, :], ACT.Sigmoid).then_inc(f_ready.sem, 1)

        @block.vector
        def _(dve):
            wide = [P, SEQ_TILES, P]
            n = [0]

            def then(ins):
                ins.then_inc(chain.sem, 1)
                n[0] += 1

            def settle():
                dve.wait_ge(chain.sem, chain.at(n[0]))

            then(dve.tensor_scalar(rest[:, :], lower, -1.0, 1.0, ALU.mult, ALU.add))
            for t in range(TILES):
                dve.wait_ge(feat_ready.sem, feat_ready.at(t + 1))
                dve.tensor_copy(gates[:, t, :], feat_ps[:, t % BANKS, 2 * P:3 * P]).then_inc(f_copied.sem, 1)
            settle()
            for i, half in enumerate((N0, N1)):
                dve.wait_ge(f_ready.sem, f_ready.at(i + 1))
                then(dve.tensor_tensor(gates[:, half, :], gates[:, half, :],
                                       rest[:, None, :].to_broadcast(wide), ALU.mult))
                settle()
                then(dve.tensor_tensor(gates[:, half, :], gates[:, half, :],
                                       lower[:, None, :].to_broadcast(wide), ALU.add))
                settle()
                then(dve.tensor_scalar(keys[:, half, :], gates[:, half, :], -1.0, 1.0, ALU.mult, ALU.add))
                settle()
            dve.wait_ge(vq_ready.sem, vq_ready.at(TILES))

            def dot(i, qn, k):
                then(dve.tensor_tensor(k, k, vq[:, qn, P:2 * P], ALU.mult))
                settle()
                pairs = k.rearrange("p t (h e) -> p t h e", e=E)
                then(dve.tensor_tensor(dots[:, i, :, :], pairs[:, :, :, 0], pairs[:, :, :, 1], ALU.add))
                settle()

            then(dve.tensor_tensor(spare[:, :, :], keys[:, N0, :], gates[:, N1, :], ALU.mult))
            settle()
            dot(1, N1, spare[:, :, :])
            dot(0, N0, keys[:, N0, :])
            dot(2, N1, keys[:, N1, :])
            four = [P, SEQ_TILES, P // E, E]

            def values(half):
                return vq[:, half, 0:P].rearrange("p t (h e) -> p t h e", e=E)

            def times(i):
                return dots[:, i, :, :, None].to_broadcast(four)

            def heads(tile, half):
                return tile[:, half, :].rearrange("p t (h e) -> p t h e", e=E)

            then(dve.tensor_tensor(heads(o_all, N0), values(N0), times(0), ALU.mult))
            then(dve.tensor_tensor(heads(spare, slice(0, SEQ_TILES)), values(N0), times(1), ALU.mult))
            then(dve.tensor_tensor(heads(o_all, N1), values(N1), times(2), ALU.mult))
            settle()
            then(dve.tensor_tensor(o_all[:, N1, :], o_all[:, N1, :], spare[:, :, :], ALU.add))
            settle()

    for s in (feat_ready, vq_ready, f_copied):
        s.passed(TILES)
    f_ready.passed(2)
    chain.passed(1 + 2 * 3 + 1 + 3 * 2 + 4)


def stage_lora_route(core, xT, weights, chosenT, gate):
    nc = core.nc
    low_ready = core.semaphore("lora_low_rank_ready")
    low_copied = core.semaphore("lora_low_rank_copied")
    logits_ready = core.semaphore("lora_logits_ready")
    step = core.semaphore("lora_route_step")
    exp_ready = core.semaphore("lora_exp_ready")
    picked = core.semaphore("lora_picked")
    masked = core.semaphore("lora_masked")
    turned = core.semaphore("lora_turned")
    copied = core.semaphore("lora_turned_copied")
    PER_BANK = 3
    W = P + EXPERTS
    BANKS = -(-TILES // PER_BANK)
    rank = field(core.const, CONST, "rank")
    with ExitStack() as ctx:
        def sb(name, shape, dt=F32):
            return core.sbuf(ctx, name, shape, dt)

        low_ps = core.psum(ctx, "low_ps", [P, BANKS, CW])
        turned_ps = core.psum(ctx, "turned_ps", [P, 2, CW])
        low = sb("low", [P, TILES, P])
        chosen = sb("chosen", [P, 2, TILES, P])
        scores = sb("scores", [P, TILES, EXPERTS])
        top = sb("top", [P, TILES])
        left = sb("left", [P, TILES, EXPERTS])
        equal = sb("equal", [P, TILES, EXPERTS])
        order = sb("order", [P, TILES])
        picks = sb("picks", [P, 2, TILES, EXPERTS])
        best = sb("best", [P, 2, TILES])
        block = ctx.enter_context(nc.Block())
        wide = [P, TILES, EXPERTS]

        def bank(i):
            n = min(PER_BANK, TILES - i * PER_BANK)
            tiles = slice(i * PER_BANK, i * PER_BANK + n)
            return tiles, low_ps[:, i, 0:n * W].rearrange("p (t w) -> p t w", w=W)

        @block.tensor
        def _(pe):
            for t in range(TILES):
                at = (t % PER_BANK) * W
                last = pe.matmul(low_ps[:, t // PER_BANK, at:at + W], xT[:, t * P:(t + 1) * P],
                                 field(weights, W_LORA, "a_gate"), start=True, stop=True)
                if t % PER_BANK == PER_BANK - 1 or t == TILES - 1:
                    last.then_inc(low_ready.sem, 1)
            for i in range(2):
                pe.wait_ge(masked.sem, masked.at(i + 1))
                for c in range(CHUNKS):
                    n = i * CHUNKS + c
                    if n >= 2:
                        pe.wait_ge(copied.sem, copied.at(n - 1))
                    for j in range(CHUNK):
                        last = pe.transpose(turned_ps[:, n % 2, j * P:(j + 1) * P],
                                            chosen[:, i, CHUNK * c + j, :], core.ident)
                    last.then_inc(turned.sem, 1)

        @block.scalar
        def _(act):
            for i in range(BANKS):
                act.wait_ge(low_ready.sem, low_ready.at(i + 1))
                tiles, src = bank(i)
                act.copy(low[:, tiles, :], src[:, :, 0:P]).then_inc(low_copied.sem, 1)
            act.wait_ge(logits_ready.sem, logits_ready.at(1))
            act.activation(scores[:, :, :], scores[:, :, :], ACT.Exp).then_inc(exp_ready.sem, 1)
            for n in range(2 * CHUNKS):
                i, c = divmod(n, CHUNKS)
                act.wait_ge(turned.sem, turned.at(n + 1))
                act.copy(chosenT[:, i, c * CW:(c + 1) * CW], turned_ps[:, n % 2, :]).then_inc(copied.sem, 1)

        @block.vector
        def _(dve):
            n = [0]

            def then(ins):
                ins.then_inc(step.sem, 1)
                n[0] += 1
                dve.wait_ge(step.sem, step.at(n[0]))

            for i in range(BANKS):
                dve.wait_ge(low_copied.sem, low_copied.at(i + 1))
                tiles, src = bank(i)
                m = tiles.stop - tiles.start
                ins = dve.tensor_tensor(scores[:, tiles, :], src[:, :, P:W],
                                        field(weights, W_LORA, "gate_b")[:, None, :].to_broadcast([P, m, EXPERTS]),
                                        ALU.add)
            then(ins)
            then(dve.tensor_reduce(top[:, :], scores[:, :, :], AX.X, ALU.max))
            dve.tensor_tensor(scores[:, :, :], scores[:, :, :], top[:, :, None].to_broadcast(wide),
                              ALU.subtract).then_inc(logits_ready.sem, 1)
            dve.wait_ge(exp_ready.sem, exp_ready.at(1))
            then(dve.tensor_reduce(top[:, :], scores[:, :, :], AX.X, ALU.add))
            then(dve.reciprocal(top[:, :], top[:, :]))
            then(dve.tensor_tensor(scores[:, :, :], scores[:, :, :], top[:, :, None].to_broadcast(wide), ALU.mult))
            step.before += n[0]
            top_two(dve, step, scores[:, :, :], rank, picks, best, (left[:, :, :], equal[:, :, :], order[:, :]))
            step.before -= n[0]
            n[0] += TOP_TWO_STEPS
            picks_ready = dve.tensor_tensor(gate[:, :], best[:, 0, :], best[:, 1, :], ALU.add)
            picks_ready.then_inc(picked.sem, 1)
            for i in range(2):
                four = [P, TILES, EXPERTS, RANK]
                dve.tensor_tensor(chosen[:, i, :, :].rearrange("p t (e r) -> p t e r", r=RANK),
                                  low[:, :, :].rearrange("p t (e r) -> p t e r", r=RANK),
                                  picks[:, i, :, :, None].to_broadcast(four), ALU.mult).then_inc(masked.sem, 1)

    low_ready.passed(BANKS)
    low_copied.passed(BANKS)
    step.passed(5 + TOP_TWO_STEPS)
    for s in (logits_ready, exp_ready, picked):
        s.passed(1)
    masked.passed(2)
    turned.passed(2 * CHUNKS)
    copied.passed(2 * CHUNKS)


def stage_lora(core, x, xT, weights, chosenT, gate):
    nc = core.nc
    hidden_ready = core.semaphore("lora_hidden_ready")
    relu_ready = core.semaphore("lora_relu_ready")
    sum_ready = core.semaphore("lora_relu_sum_ready")
    out_ready = core.semaphore("lora_out_ready")
    added = core.semaphore("lora_added")
    with ExitStack() as ctx:
        hidden_ps = core.psum(ctx, "hidden_ps", [P, 2, 2, CW])
        out_ps = core.psum(ctx, "out_ps", [P, 2, CW])
        relu = core.sbuf(ctx, "relu", [P, 2, 2, CW])
        both = core.sbuf(ctx, "both", [P, 2, CW])
        block = ctx.enter_context(nc.Block())
        F = FF_BLOCKS

        @block.tensor
        def _(pe):
            def up(c, m, buf):
                pe.wait_ge(relu_ready.sem, c * F + relu_ready.at(m + 1))
                at = slice(m * P, (m + 1) * P)
                for i in range(2):
                    pe.matmul(hidden_ps[:, buf, i, :], field(weights, W_LORA, "wi")[:, at],
                              xT[:, bass.ds(c * CW, CW)], start=True, stop=False)
                    last = pe.matmul(hidden_ps[:, buf, i, :], field(weights, W_LORA, "b")[:, at],
                                     chosenT[:, i, bass.ds(c * CW, CW)], start=False, stop=True)
                last.then_inc(hidden_ready.sem, 1)

            def down(c, m, buf, obuf):
                pe.wait_ge(sum_ready.sem, c * F + sum_ready.at(m + 3))
                if m == 0:
                    pe.wait_ge(added.sem, c + added.at(1))
                    pe.matmul(out_ps[:, obuf, :], core.twos[0:1, :],
                              field(weights, W_LORA, "bo")[0:1, None, :].to_broadcast([1, CHUNK, P]),
                              start=True, stop=False, skip_group_check=True)
                for j in range(CHUNK):
                    last = pe.matmul(out_ps[:, obuf, j * P:(j + 1) * P], both[:, buf, j * P:(j + 1) * P],
                                     field(weights, W_LORA, "wo")[:, m * P:(m + 1) * P],
                                     start=False, stop=m == F - 1, skip_group_check=True)
                last.then_inc(out_ready.sem, 1)

            with pe.Fori(0, CHUNKS // 2) as pair:
                for obuf in range(2):
                    c = pair * 2 + obuf
                    for m in range(F + 1):
                        if m < F:
                            up(c, m, m % 2)
                        if m >= 1:
                            down(c, m - 1, (m - 1) % 2, obuf)

        @block.scalar
        def _(act):
            act.sem_inc(relu_ready.sem, 2)
            with act.Fori(0, CHUNKS) as c:
                for m in range(F):
                    buf = m % 2
                    act.wait_ge(hidden_ready.sem, c * F + hidden_ready.at(m + 1))
                    act.wait_ge(sum_ready.sem, c * F + sum_ready.at(m + 1))
                    for i in range(2):
                        last = act.activation(relu[:, buf, i, :], hidden_ps[:, buf, i, :], ACT.Relu,
                                              bias=field(weights, W_LORA, "bi")[:, m:m + 1])
                    last.then_inc(relu_ready.sem, 1)

        @block.vector
        def _(dve):
            dve.sem_inc(sum_ready.sem, 2)
            dve.sem_inc(added.sem, 2)

            def chunk(c, obuf, first):
                for m in range(F):
                    buf = m % 2
                    dve.wait_ge(relu_ready.sem, c * F + relu_ready.at(m + 3))
                    if not (first and m < 2):
                        dve.wait_ge(out_ready.sem, c * F + out_ready.at(m - 1))
                    dve.tensor_tensor(both[:, buf, :], relu[:, buf, 0, :], relu[:, buf, 1, :],
                                      ALU.add).then_inc(sum_ready.sem, 1)
                dve.wait_ge(out_ready.sem, c * F + out_ready.at(F))
                for j in range(CHUNK):
                    t = c * CHUNK + j
                    xt = x[:, bass.ds(t, 1), :].rearrange("p o d -> p (o d)")
                    last = dve.scalar_tensor_tensor(xt, out_ps[:, obuf, j * P:(j + 1) * P],
                                                    gate[:, bass.ds(t, 1)], xt, ALU.mult, ALU.add)
                last.then_inc(added.sem, 1)

            chunk(0, 0, True)
            chunk(1, 1, False)
            with dve.Fori(1, CHUNKS // 2) as pair:
                for obuf in range(2):
                    chunk(pair * 2 + obuf, obuf, False)

    hidden_ready.passed(CHUNKS * F)
    relu_ready.passed(2 + CHUNKS * F)
    sum_ready.passed(2 + CHUNKS * F)
    out_ready.passed(CHUNKS * F)
    added.passed(2 + CHUNKS)


def program(nc, x_in, const_in, masks_in, rows_q, rows_rot, rows_ali, w_rot, w_moe, w_pair, w_rec, w_ali,
            w_lora, out):
    with ExitStack() as ctx:
        core = Core(nc, ctx)

        def sb(name, shape, dt=F32):
            return core.sbuf(ctx, name, shape, dt)

        x = sb("x", [P, TILES, P])
        core.const = sb("const", [P, CONST_W])
        core.masks = sb("masks", [P, MASKS_W], BF16)
        core.ident = field(core.const, CONST, "ident")
        core.ones = sb("ones", [P, P])
        core.twos = sb("twos", [P, P])
        x_view = x_in.rearrange("b (t p) d -> p (b t) d", p=P)
        out_view = out.rearrange("b (t p) d -> p (b t) d", p=P)

        def long_attention(weights, places, rotary, scale, k_rows, bo, shift, loads=()):
            with ExitStack() as outer:
                xT = core.sbuf(outer, "xT", [P, TOKENS])
                o_tok = xT[:, :].rearrange("p (t g f) -> p t g f", g=GROUPS, t=SEQ_TILES)
                with ExitStack() as stacks:
                    q_stack = core.sbuf(stacks, "q_stack", [P, ALL_HEADS * SEQ], BF16)
                    k_stack = core.sbuf(stacks, "k_stack", [P, ALL_HEADS * SEQ], BF16)
                    v_tok = core.sbuf(stacks, "v_tok", [P, ALL_HEADS, SEQ_TILES, DH + 1])
                    stage_norm(core, x, 1e-5, xT=xT, loads=loads)
                    stage_operands(core, xT, weights, rotary, scale, q_stack, k_stack, v_tok, rows_q, k_rows)
                    stage_attend(core, rotary, q_stack, k_stack, v_tok, o_tok)
                stage_project(core, x, field(weights, places, "out"), o_tok=o_tok, bo=bo, shift=shift)

        def experts():
            with ExitStack() as inner:
                moe = core.sbuf(inner, "moe", [P, W_MOE_W])
                xT = core.sbuf(inner, "xT", [P, TOKENS])
                stage_norm(core, x, 1e-5, xT=xT, loads=[(moe[:, :], w_moe)])
                stage_experts(core, x, xT, moe)

        def pair():
            with ExitStack() as inner:
                weights = core.sbuf(inner, "w_pair", [P, W_PAIR_W])
                once = core.sbuf(inner, "normed_once", [P, TILES, P])
                xT = core.sbuf(inner, "xT", [P, TOKENS])
                stage_norm(core, x, 1e-5, token_major=once, loads=[(weights[:, :], w_pair)])
                stage_norm(core, once, 1e-6, xT=xT, affine=(field(weights, W_PAIR, "ln_scale"),
                                                            field(weights, W_PAIR, "ln_bias")))
                stage_pair(core, x, xT, weights)

        def recurrence():
            with ExitStack() as inner:
                xT = core.sbuf(inner, "xT", [P, TOKENS])
                o_all = core.sbuf(inner, "o_all", [P, TILES, P])
                rec = core.sbuf(inner, "rec", [P, W_REC_W])
                stage_norm(core, x, 1e-5, xT=xT, loads=[(rec[:, :], w_rec)])
                stage_recurrence(core, xT, rec, o_all)
                stage_project(core, x, field(rec, W_REC, "out"), o_all=o_all)

        def lora():
            with ExitStack() as inner:
                weights = core.sbuf(inner, "w_lora", [P, W_LORA_W])
                xT = core.sbuf(inner, "xT", [P, TOKENS])
                chosenT = core.sbuf(inner, "chosenT", [P, 2, TOKENS])
                gate = core.sbuf(inner, "gate", [P, TILES])
                stage_norm(core, x, 1e-5, xT=xT, loads=[(weights[:, :], w_lora)])
                stage_lora_route(core, xT, weights, chosenT, gate)
                stage_lora(core, x, xT, weights, chosenT, gate)

        with ExitStack() as first:
            rot = core.sbuf(first, "rot", [P, W_ROT_W])
            stage_load(core, [(x[:, :, :], x_view), (core.const[:, :], const_in), (core.masks[:, :], masks_in),
                              (rot[:, :], w_rot)])
            ones_set = core.semaphore("ones_set")
            with nc.Block() as block:
                @block.vector
                def _(dve):
                    dve.memset(core.ones[:, :], 1.0)
                    dve.memset(core.twos[:, :], 2.0).then_inc(ones_set.sem, 1)
            if STAGES >= 1:
                long_attention(rot, W_ROT, True, DH ** -0.5, rows_rot, field(rot, W_ROT, "bo"), CTX)
        if STAGES >= 2:
            experts()
        if STAGES >= 3:
            pair()
        if STAGES >= 4:
            experts()
        if STAGES >= 5:
            recurrence()
        if STAGES >= 6:
            lora()
        if STAGES >= 7:
            with ExitStack() as inner:
                ali = core.sbuf(inner, "ali", [P, W_ALI_W])
                long_attention(ali, W_ALI, False, DH ** -0.5, rows_ali, None, 0, loads=[(ali[:, :], w_ali)])
        if STAGES >= 8:
            lora()
        stored = core.semaphore("x_stored")
        with nc.Block() as block:
            @block.sync
            def _(sp):
                sp.dma_start(out_view, x[:, :, :]).then_inc(stored.sem, 16)
                sp.wait_ge(stored.sem, 16)



def _pack(np, places, width, **arrays):
    out = np.zeros((P, width), np.float32)
    for name, a in arrays.items():
        at, n = places[name]
        out[:, at:at + n] = a
    return out


def kernel(**inputs):
    import numpy as np
    import concourse.bacc as bacc
    from concourse import mybir as _mybir
    from concourse.bass_utils import run_bass_kernel_spmd

    a = {k: np.ascontiguousarray(v) for k, v in inputs.items()}
    bf16 = np.dtype(_mybir.dt.np(BF16)) if hasattr(_mybir.dt, "np") else np.dtype("bfloat16")

    def rows(v):
        return np.broadcast_to(v.reshape(1, -1), (P, v.size))

    def blocks(w):
        return w.reshape(-1, P, w.shape[1]).transpose(1, 0, 2).reshape(P, -1)

    n = np.arange(SEQ, dtype=np.float32)
    inv_freq = (1.0 / 10000.0 ** (np.arange(0, DH, 2, dtype=np.float32) / DH)).astype(np.float32)
    freqs = n[:, None] * inv_freq[None, :]
    cos = np.cos(np.concatenate([freqs, freqs], -1))
    sin = np.sin(freqs)
    sin = np.concatenate([-sin, sin], -1)

    def by_tile(t):
        return t.reshape(SEQ_TILES, P, DH).transpose(1, 0, 2).reshape(P, -1)

    const = _pack(np, CONST, CONST_W, ident=np.eye(P), cos=by_tile(cos), sin=by_tile(sin),
                  rank=rows(np.arange(EXPERTS, 0, -1)))
    i = np.arange(P)
    hidden = -1e30
    causal = np.where(i[None, :] > i[:, None], hidden, 0)
    rot_01 = np.where(rows(i) >= CTX - P, hidden, 0)
    rot_11 = np.where((i[None, :] >= CTX - P) & (i[None, :] > i[:, None]), hidden, 0)
    masks = _pack(np, MASKS, MASKS_W, ident=np.eye(P), diag=causal, rot_01=rot_01, rot_11=rot_11,
                  diag_T=causal.T, rot_T=np.concatenate([rot_01.T, rot_11.T], 1)).astype(bf16)
    start = 2.0 ** -0.5
    slopes = np.array([start * start ** h for h in range(HEADS)], np.float32)
    bias = slopes[:, None] * n[None, :]
    parts = []
    for _ in range(3):
        part = bias.astype(bf16)
        parts.append(np.tile(part.reshape(1, -1), (1, BATCH)))
        bias = bias - part.astype(np.float32)
    ones = np.ones((3, ALL_HEADS * SEQ), bf16)
    rows_ali = np.concatenate(parts + [ones])
    rows_rot = np.concatenate([np.zeros((3, ALL_HEADS * SEQ), bf16), ones])

    qkv = a["L0_attn_b_qkv_kernel"]
    pair_v = qkv[:, 2]
    w_attn = a["L1_attn_b_w_attn"]
    arrays = {
        "x": a["L0_attn_a_x"], "const": const, "masks": masks, "rows_q": ones, "rows_rot": rows_rot,
        "rows_ali": rows_ali,
        "w_rot": _pack(np, W_ROT, W_ROT_W, qkv=np.concatenate([a["L0_attn_a_Wq"].T, a["L0_attn_a_Wkv"].T], 1),
                       out=a["L0_attn_a_Wo"].T, bo=rows(a["L0_attn_a_bo"]), ln_g=rows(a["L0_attn_a_ln_g"]),
                       ln_b=rows(a["L0_attn_a_ln_b"])),
        "w_moe": _pack(np, W_MOE, W_MOE_W, router=a["L0_ffn_router_w"].T, w1=a["L0_ffn_w1"],
                       w2=blocks(a["L0_ffn_w2"])),
        "w_pair": _pack(np, W_PAIR, W_PAIR_W, q=qkv[:, 0], k=qkv[:, 1], v=pair_v, v_T=blocks(pair_v.T),
                        out=blocks(a["L0_attn_b_out_kernel"]), ln_scale=a["L0_attn_b_ln_scale"][:, None],
                        ln_bias=a["L0_attn_b_ln_bias"][:, None]),
        "w_rec": _pack(np, W_REC, W_REC_W, **{"in": a["L1_attn_a_W_in"], "out": a["L1_attn_a_W_out"],
                                              "lower": rows(a["L1_attn_a_lower_bound"])}),
        "w_ali": _pack(np, W_ALI, W_ALI_W, q=w_attn[0:P].T, k=w_attn[P:2 * P].T, v=w_attn[2 * P:3 * P].T,
                       out=a["L1_attn_b_w_proj"].T),
        "w_lora": _pack(np, W_LORA, W_LORA_W, wi=a["L1_ffn_wi"].T, wo=blocks(a["L1_ffn_wo"].T),
                        a_gate=np.concatenate([a["L1_ffn_lora_A"].reshape(-1, P).T, a["L1_ffn_gate_w"].T], 1),
                        b=a["L1_ffn_lora_B"].transpose(0, 2, 1).reshape(P, FF),
                        bi=a["L1_ffn_bi"].reshape(FF_BLOCKS, P).T, gate_b=rows(a["L1_ffn_gate_b"]),
                        bo=rows(a["L1_ffn_bo"])),
    }
    nc = bacc.Bacc("TRN2", target_bir_lowering=False, num_devices=1)
    args, maps = [], {}
    for name, v in arrays.items():
        maps[name] = v
        args.append(nc.dram_tensor(name, v.shape, _mybir.dt.from_np(v.dtype), kind="ExternalInput").ap())
    args.append(nc.dram_tensor("y", (BATCH, SEQ, P), F32, kind="ExternalOutput").ap())
    program(nc, *args)
    r = run_bass_kernel_spmd(nc, [maps], core_ids=[0])
    return r.results[0]["y"]
```

```python
from contextlib import ExitStack

import concourse.bass as bass
from concourse import mybir

F32 = mybir.dt.float32
BF16 = mybir.dt.bfloat16
ALU = mybir.AluOpType
ACT = mybir.ActivationFunctionType
AX = mybir.AxisListType

P = 128
BATCH, SEQ = 2, 1024
SEQ_TILES = SEQ // P
TILES = BATCH * SEQ_TILES
CHUNK = 4
CHUNKS = TILES // CHUNK
CW = CHUNK * P
TOKENS = TILES * P
HEADS, DH = 16, 8
ALL_HEADS = BATCH * HEADS
CTX = 192
EXPERTS = 8

Q_PARTS = (0, 0, 1, 1, 0, 2)
K_PARTS = (0, 1, 0, 1, 2, 0)
ROW_BIAS = len(Q_PARTS) * DH
ROW_MAX = ROW_BIAS + 3
ROWS = ROW_MAX + 3
STACKED = 96
HALF = HEADS * SEQ

PAIR_HEADS, PAIR_DH = 16, 64
PAIR_W = PAIR_HEADS * PAIR_DH
PAIR_BLOCKS = PAIR_W // P

EXPERT_BLOCKS = (1, 1, 1, 1, 2, 2, 2, 2)
HIDDEN_BLOCKS = sum(EXPERT_BLOCKS)

FF = 512
FF_BLOCKS = FF // P
RANK = 16

STAGES = 8


def columns(*fields):
    at, out = 0, {}
    for name, n in fields:
        out[name] = (at, n)
        at += n
    return out, at


CONST, CONST_W = columns(("ident", P), ("cos", SEQ_TILES * DH), ("sin", SEQ_TILES * DH), ("rank", EXPERTS))
MASKS, MASKS_W = columns(("ident", P), ("rot_01", P), ("rot_11", P), ("diag", P),
                         ("rot_T", 2 * P), ("diag_T", P))
W_ROT, W_ROT_W = columns(("qkv", 2 * P), ("out", P), ("bo", P), ("ln_g", DH), ("ln_b", DH))
W_MOE, W_MOE_W = columns(("router", EXPERTS), ("w1", HIDDEN_BLOCKS * P), ("w2", HIDDEN_BLOCKS * P))
W_PAIR, W_PAIR_W = columns(("q", PAIR_W), ("k", PAIR_W), ("v", PAIR_W), ("v_T", PAIR_W), ("out", PAIR_W),
                           ("ln_scale", 1), ("ln_bias", 1))
W_REC, W_REC_W = columns(("in", 3 * P), ("out", P), ("lower", P))
W_ALI, W_ALI_W = columns(("q", P), ("k", P), ("v", P), ("out", P))
W_LORA, W_LORA_W = columns(("wi", FF), ("wo", FF), ("a_gate", P + EXPERTS), ("b", FF), ("bi", FF_BLOCKS),
                           ("gate_b", EXPERTS), ("bo", P))


class Count:

    def __init__(self, handle):
        self.sem = handle
        self.before = 0

    def at(self, n):
        return self.before + n

    def passed(self, n):
        self.before += n


class Core:

    def __init__(self, nc, ctx):
        self.nc = nc
        self.ctx = ctx
        self.counts = {}
        self.names = 0

    def name(self, name):
        self.names += 1
        return f"{name}_{self.names}"

    def sbuf(self, ctx, name, shape, dt=F32):
        return ctx.enter_context(self.nc.sbuf_tensor(self.name(name), shape, dt))

    def psum(self, ctx, name, shape, dt=F32):
        return ctx.enter_context(self.nc.psum_tensor(self.name(name), shape, dt))

    def semaphore(self, name):
        if name not in self.counts:
            self.counts[name] = Count(self.ctx.enter_context(self.nc.semaphore(name)))
        return self.counts[name]


def field(tile, places, name):
    at, n = places[name]
    return tile[:, at:at + n]


def stage_load(core, loads):
    nc = core.nc
    loaded = core.semaphore("loaded")
    with nc.Block() as block:

        @block.sync
        def _(sp):
            for dst, src in loads:
                sp.dma_start(dst, src).then_inc(loaded.sem, 16)
            sp.wait_ge(loaded.sem, loaded.at(16 * len(loads)))
    loaded.passed(16 * len(loads))


ROOT_STEPS = 5


def inverse_root(dve, done, step, root_ready, var, eps, shifted, root, out, spare, scale=1.0):
    dve.tensor_scalar(shifted, var, scale, eps, ALU.mult, ALU.add).then_inc(step.sem, 1)
    dve.wait_ge(root_ready.sem, root_ready.at(1))
    dve.reciprocal(out, root).then_inc(step.sem, 1)
    dve.wait_ge(step.sem, step.at(2))
    dve.tensor_tensor(spare, out, out, ALU.mult).then_inc(step.sem, 1)
    dve.wait_ge(step.sem, step.at(3))
    dve.tensor_tensor(spare, spare, shifted, ALU.mult).then_inc(step.sem, 1)
    dve.wait_ge(step.sem, step.at(4))
    dve.tensor_scalar(spare, spare, -0.5, 1.5, ALU.mult, ALU.add).then_inc(step.sem, 1)
    dve.wait_ge(step.sem, step.at(5))
    dve.tensor_tensor(out, out, spare, ALU.mult).then_inc(done.sem, 1)
    dve.wait_ge(done.sem, done.at(1))


def stage_norm(core, src, eps, xT=None, token_major=None, affine=None, loads=(), meanwhile=None):
    nc = core.nc
    stats_ready = core.semaphore("norm_stats_ready")
    moments_ready = core.semaphore("norm_moments_ready")
    variance_step = core.semaphore("norm_variance_step")
    root_ready = core.semaphore("norm_root_ready")
    rstd_ready = core.semaphore("norm_rstd_ready")
    tile_ready = core.semaphore("norm_chunk_ready")
    turned = core.semaphore("norm_chunk_turned")
    xT_ready = core.semaphore("norm_xT_ready")
    with ExitStack() as ctx:
        stats = core.sbuf(ctx, "stats", [P, TILES, 6], F32)
        moments = core.sbuf(ctx, "moments", [P, TILES, 2], F32)
        variance = core.sbuf(ctx, "variance", [P, TILES], F32)
        root = core.sbuf(ctx, "root", [P, TILES], F32)
        spare = core.sbuf(ctx, "spare", [P, TILES], F32)
        rstd = core.sbuf(ctx, "rstd", [P, TILES], F32)
        normed = token_major
        if token_major is None:
            normed = core.sbuf(ctx, "normed", [P, TILES, P], F32)
            turned_ps = core.psum(ctx, "turned_ps", [P, 2, CW], F32)
        loaded = core.semaphore("loaded")
        block = ctx.enter_context(nc.Block())

        if loads:
            @block.sync
            def _(sp):
                for dst, source in loads:
                    sp.dma_start(dst, source).then_inc(loaded.sem, 16)
                sp.wait_ge(loaded.sem, loaded.at(16 * len(loads)))

        if meanwhile:
            block.gpsimd(meanwhile)

        @block.vector
        def _(dve):
            for t in range(TILES):
                last = dve.bn_stats(stats[:, t, :], src[:, t, :])
            last.then_inc(stats_ready.sem, 1)
            dve.wait_ge(stats_ready.sem, stats_ready.at(1))
            for t in range(TILES):
                last = dve.bn_aggr(moments[:, t, :], stats[:, t, :])
            last.then_inc(moments_ready.sem, 1)
            dve.wait_ge(moments_ready.sem, moments_ready.at(1))
            inverse_root(dve, rstd_ready, variance_step, root_ready, moments[:, :, 1], eps, variance[:, :],
                         root[:, :], rstd[:, :], spare[:, :])
            for c in range(CHUNKS):
                for t in range(CHUNK * c, CHUNK * (c + 1)):
                    last = dve.tensor_scalar(normed[:, t, :], src[:, t, :], moments[:, t, 0:1],
                                             rstd[:, t:t + 1], ALU.subtract, ALU.mult)
                last.then_inc(tile_ready.sem, 1)

        if token_major is None:
            @block.tensor
            def _(pe):
                for c in range(CHUNKS):
                    pe.wait_ge(tile_ready.sem, tile_ready.at(c + 1))
                    if c >= 2:
                        pe.wait_ge(xT_ready.sem, xT_ready.at(c - 1))
                    for j in range(CHUNK):
                        last = pe.transpose(turned_ps[:, c % 2, j * P:(j + 1) * P],
                                            normed[:, CHUNK * c + j, :], core.ident)
                    last.then_inc(turned.sem, 1)

        @block.scalar
        def _(act):
            act.wait_ge(variance_step.sem, variance_step.at(1))
            act.activation(root[:, :], variance[:, :], ACT.Sqrt).then_inc(root_ready.sem, 1)
            if token_major is None:
                for c in range(CHUNKS):
                    act.wait_ge(turned.sem, turned.at(c + 1))
                    out = xT[:, c * CW:(c + 1) * CW]
                    if affine:
                        ins = act.activation(out, turned_ps[:, c % 2, :], ACT.Identity,
                                             bias=affine[1], scale=affine[0])
                    else:
                        ins = act.copy(out, turned_ps[:, c % 2, :])
                    ins.then_inc(xT_ready.sem, 1)

    stats_ready.passed(1)
    moments_ready.passed(1)
    variance_step.passed(ROOT_STEPS)
    root_ready.passed(1)
    rstd_ready.passed(1)
    loaded.passed(16 * len(loads))
    tile_ready.passed(CHUNKS)
    if token_major is None:
        turned.passed(CHUNKS)
        xT_ready.passed(CHUNKS)


class Stacks:

    def __init__(self, q, k, parts, q_rows, k_rows):
        self.q, self.k, self.parts, self.q_rows, self.k_rows = q, k, parts, q_rows, k_rows


STACK_LOADS = 2 + 2 * len(Q_PARTS)


def load_stacks(core, sp, b, stacks, stored):
    loaded = core.semaphore(f"op_stacks_loaded_{b}")
    cols = slice(b * HALF, (b + 1) * HALF)
    sp.dma_start(stacks.q[ROW_BIAS:ROW_MAX, cols], stacks.q_rows[:, cols]).then_inc(loaded.sem, 16)
    sp.dma_start(stacks.k[ROW_BIAS:ROWS, cols], stacks.k_rows[:, cols]).then_inc(loaded.sem, 16)
    for s in stored:
        sp.wait_ge(s.sem, s.at(16) if b == 0 else s.at(0))
    for stack, order, first in ((stacks.q, Q_PARTS, 0), (stacks.k, K_PARTS, 3)):
        for a, part in enumerate(order):
            src = stacks.parts[first + part, :, b * SEQ:(b + 1) * SEQ].rearrange("(h d) n -> d h n", d=DH)
            dst = stack[a * DH:(a + 1) * DH, cols]
            sp.dma_start(dst.rearrange("d (h n) -> d h n", h=HEADS), src).then_inc(loaded.sem, 16)


def stage_operands(core, xT, weights, rotary, scale, stacks, v_tok):
    nc = core.nc
    proj_ready = core.semaphore("op_projection_ready")
    step_done = core.semaphore("op_vector_step_done")
    middle_ready = core.semaphore("op_middle_part_ready")
    var_step = core.semaphore("op_variance_step")
    root_ready = core.semaphore("op_root_ready")
    sq_ready = core.semaphore("op_k_variance_ready")
    rstd_ready = core.semaphore("op_k_rstd_ready")
    qk_ready = core.semaphore("op_qk_token_major_ready")
    turned = core.semaphore("op_qk_turned")
    v_ready = core.semaphore("op_v_ready")
    vps_ready = core.semaphore("op_v_product_ready")
    high_ready = core.semaphore("op_high_part_ready")
    rest_ready = core.semaphore("op_rest_ready")
    low_ready = core.semaphore("op_low_parts_ready")
    stored = [core.semaphore(f"op_parts_stored_{i}") for i in range(2)]
    ones_set = core.semaphore("op_v_ones_set")
    G = CHUNK * HEADS
    with ExitStack() as ctx:
        def sb(name, shape, dt=F32):
            return core.sbuf(ctx, name, shape, dt)

        parts = sb("parts", [P, 2, 6, CW], BF16)
        rest = sb("rest", [P, 2, CW])
        turned_ps = core.psum(ctx, "turned_ps", [P, 2, 2, CW], F32)
        if rotary:
            proj_ps = core.psum(ctx, "proj_ps", [P, 2, CHUNK, 2 * P], F32)
            by_cos = sb("by_cos", [P, CHUNK, 2 * P])
            by_sin = sb("by_sin", [P, CHUNK, 2 * P])
            rotated = sb("rotated", [P, 2, CHUNK, 2 * P])
            k_tok = sb("k_tok", [P, 2, CHUNK, P])
            mean = sb("mean", [P, G])
            var = sb("var", [P, G])
            shifted = sb("shifted", [P, G])
            root = sb("root", [P, G])
            spare = sb("spare", [P, G])
            rstd = sb("rstd", [P, G])
            square = by_sin[:, :, 0:P]
        else:
            v_ps = core.psum(ctx, "v_ps", [P, 2, CW], F32)
        block = ctx.enter_context(nc.Block())

        def v_of_chunk(c):
            b, t0 = divmod(CHUNK * c, SEQ_TILES)
            return v_tok[:, b * HEADS:(b + 1) * HEADS, t0:t0 + CHUNK, 0:DH].rearrange("p h j d -> p j h d")

        @block.tensor
        def _(pe):
            def project(c):
                if rotary:
                    if c >= 2:
                        pe.wait_ge(step_done.sem, step_done.at(2 * (c - 1)))
                    for j in range(CHUNK):
                        t = CHUNK * c + j
                        last = pe.matmul(proj_ps[:, c % 2, j, :], xT[:, t * P:(t + 1) * P],
                                         field(weights, W_ROT, "qkv"), start=True, stop=True)
                    last.then_inc(proj_ready.sem, 1)
                    return
                if c >= 2:
                    pe.wait_ge(rest_ready.sem, rest_ready.at(2 * (c - 1)))
                    pe.wait_ge(high_ready.sem, high_ready.at(2 * (c - 1)))
                    pe.wait_ge(v_ready.sem, v_ready.at(c - 1))
                for i, name in enumerate("qk"):
                    last = pe.matmul(turned_ps[:, c % 2, i, :], field(weights, W_ALI, name),
                                     xT[:, c * CW:(c + 1) * CW], start=True, stop=True)
                last.then_inc(turned.sem, 1)
                for j in range(CHUNK):
                    t = CHUNK * c + j
                    last = pe.matmul(v_ps[:, c % 2, j * P:(j + 1) * P], xT[:, t * P:(t + 1) * P],
                                     field(weights, W_ALI, "v"), start=True, stop=True)
                last.then_inc(vps_ready.sem, 1)

            def turn(c):
                pe.wait_ge(qk_ready.sem, qk_ready.at(c + 1))
                if c >= 2:
                    pe.wait_ge(rest_ready.sem, rest_ready.at(2 * (c - 1)))
                    pe.wait_ge(high_ready.sem, high_ready.at(2 * (c - 1)))
                for i, tok in enumerate((rotated[:, c % 2, :, 0:P], k_tok[:, c % 2, :, :])):
                    for j in range(CHUNK):
                        last = pe.transpose(turned_ps[:, c % 2, i, j * P:(j + 1) * P], tok[:, j, :], core.ident)
                last.then_inc(turned.sem, 1)

            for c in range(CHUNKS):
                project(c)
                if rotary and c >= 1:
                    turn(c - 1)
            if rotary:
                turn(CHUNKS - 1)

        @block.vector
        def _(dve):
            dve.memset(v_tok[:, :, :, DH:DH + 1], 1.0).then_inc(ones_set.sem, 1)

            def rotate(c):
                t0 = (CHUNK * c) % SEQ_TILES
                both = proj_ps[:, c % 2, :, :].rearrange("p j (g d) -> p j g d", d=DH)
                cos = field(core.const, CONST, "cos").rearrange("p (t d) -> p t d", d=DH)[:, t0:t0 + CHUNK, :]
                sin = field(core.const, CONST, "sin").rearrange("p (t d) -> p t d", d=DH)[:, t0:t0 + CHUNK, :]
                wide = [P, CHUNK, 2 * HEADS, DH]
                half = [P, CHUNK, 2 * HEADS, DH // 2]
                dve.wait_ge(proj_ready.sem, proj_ready.at(c + 1))
                dve.tensor_tensor(by_cos[:, :, :].rearrange("p j (g d) -> p j g d", d=DH), both,
                                  cos[:, :, None, :].to_broadcast(wide), ALU.mult)
                sines = by_sin[:, :, :].rearrange("p j (g d) -> p j g d", d=DH)
                dve.tensor_tensor(sines[:, :, :, 0:4], both[:, :, :, 4:8],
                                  sin[:, :, None, 0:4].to_broadcast(half), ALU.mult)
                dve.tensor_tensor(sines[:, :, :, 4:8], both[:, :, :, 0:4],
                                  sin[:, :, None, 4:8].to_broadcast(half), ALU.mult).then_inc(step_done.sem, 1)
                dve.wait_ge(step_done.sem, step_done.at(2 * c + 1))
                if c >= 2:
                    dve.wait_ge(turned.sem, turned.at(c - 1))
                    dve.wait_ge(v_ready.sem, v_ready.at(c - 1))
                dve.tensor_tensor(rotated[:, c % 2, :, :], by_cos[:, :, :], by_sin[:, :, :],
                                  ALU.add).then_inc(step_done.sem, 1)
                dve.wait_ge(step_done.sem, step_done.at(2 * c + 2))

            def norm_k(c):
                k = rotated[:, c % 2, :, P:2 * P].rearrange("p j (g d) -> p j g d", d=DH)
                kn = k_tok[:, c % 2, :, :].rearrange("p j (g d) -> p j g d", d=DH)
                sq = square.rearrange("p j (g d) -> p j g d", d=DH)
                shape = [P, CHUNK, HEADS, DH]

                def wide(s):
                    return s[:, :].rearrange("p (j g) -> p j g", j=CHUNK)[:, :, :, None].to_broadcast(shape)

                n = 5 * c
                dve.tensor_reduce(mean[:, :].rearrange("p (j g) -> p j g", j=CHUNK), k, AX.X,
                                  ALU.add).then_inc(sq_ready.sem, 1)
                dve.wait_ge(sq_ready.sem, sq_ready.at(n + 1))
                dve.tensor_scalar(mean[:, :], mean[:, :], 1.0 / DH, None, ALU.mult).then_inc(sq_ready.sem, 1)
                dve.wait_ge(sq_ready.sem, sq_ready.at(n + 2))
                dve.tensor_tensor(kn, k, wide(mean), ALU.subtract).then_inc(sq_ready.sem, 1)
                dve.wait_ge(sq_ready.sem, sq_ready.at(n + 3))
                dve.tensor_tensor(sq, kn, kn, ALU.mult).then_inc(sq_ready.sem, 1)
                dve.wait_ge(sq_ready.sem, sq_ready.at(n + 4))
                dve.tensor_reduce(var[:, :].rearrange("p (j g) -> p j g", j=CHUNK), sq, AX.X,
                                  ALU.add).then_inc(sq_ready.sem, 1)
                dve.wait_ge(sq_ready.sem, sq_ready.at(n + 5))
                inverse_root(dve, rstd_ready, var_step, root_ready, var[:, :], 1e-5, shifted[:, :], root[:, :],
                             rstd[:, :], spare[:, :], scale=1.0 / DH)
                var_step.before += ROOT_STEPS
                root_ready.before += 1
                rstd_ready.before += 1
                g = field(weights, W_ROT, "ln_g")[:, None, None, :].to_broadcast(shape)
                b = field(weights, W_ROT, "ln_b")[:, None, None, :].to_broadcast(shape)
                dve.tensor_tensor(kn, kn, wide(rstd), ALU.mult).then_inc(qk_step.sem, 1)
                dve.wait_ge(qk_step.sem, qk_step.at(2 * c + 1))
                dve.tensor_tensor(kn, kn, g, ALU.mult).then_inc(qk_step.sem, 1)
                dve.wait_ge(qk_step.sem, qk_step.at(2 * c + 2))
                dve.tensor_tensor(kn, kn, b, ALU.add).then_inc(qk_ready.sem, 1)

            def rest_of(c):
                for i in range(2):
                    dve.wait_ge(high_ready.sem, high_ready.at(2 * c + i + 1))
                    if c >= 1:
                        dve.wait_ge(low_ready.sem, low_ready.at(2 * (c - 1) + i + 1))
                    dve.scalar_tensor_tensor(rest[:, i, :], turned_ps[:, c % 2, i, :],
                                             scale if i == 0 else 1.0, parts[:, c % 2, 3 * i, :],
                                             ALU.mult, ALU.subtract).then_inc(rest_ready.sem, 1)

            qk_step = core.semaphore("op_k_affine_step")
            at_start = var_step.before, root_ready.before, rstd_ready.before
            if rotary:
                rotate(0)
                norm_k(0)
            for c in range(CHUNKS):
                if rotary and c + 1 < CHUNKS:
                    rotate(c + 1)
                rest_of(c)
                if rotary and c + 1 < CHUNKS:
                    norm_k(c + 1)
            if not rotary:
                dve.memset(stacks.q[0:STACKED, HALF:2 * HALF], 0.0)
            if rotary:
                qk_step.passed(2 * CHUNKS)
                var_step.before, root_ready.before, rstd_ready.before = at_start

        @block.scalar
        def _(act):
            act.wait_ge(ones_set.sem, ones_set.at(1))
            for c in range(CHUNKS):
                if rotary:
                    act.wait_ge(var_step.sem, var_step.at(ROOT_STEPS * c + 1))
                    act.activation(root[:, :], shifted[:, :], ACT.Sqrt).then_inc(root_ready.sem, 1)
                    act.wait_ge(qk_ready.sem, qk_ready.at(c + 1))
                    act.copy(v_of_chunk(c), k_tok[:, c % 2, :, :].rearrange("p j (g d) -> p j g d", d=DH)
                             ).then_inc(v_ready.sem, 1)
                act.wait_ge(turned.sem, turned.at(c + 1))
                if c >= 2:
                    act.wait_ge(stored[c % 2].sem, stored[c % 2].at(16 * (c // 2)))
                for i in range(2):
                    act.mul(parts[:, c % 2, 3 * i, :], turned_ps[:, c % 2, i, :],
                            scale if i == 0 else 1.0).then_inc(high_ready.sem, 1)
                for i in range(2):
                    act.wait_ge(rest_ready.sem, rest_ready.at(2 * c + i + 1))
                    act.copy(parts[:, c % 2, 3 * i + 1, :], rest[:, i, :]).then_inc(middle_ready.sem, 1)
                if not rotary:
                    act.wait_ge(vps_ready.sem, vps_ready.at(c + 1))
                    act.copy(v_of_chunk(c), v_ps[:, c % 2, :].rearrange("p (j g d) -> p j g d", j=CHUNK, d=DH)
                             ).then_inc(v_ready.sem, 1)

        @block.gpsimd
        def _(pool):
            if rotary:
                pool.memset(stacks.q[0:STACKED, HALF:2 * HALF].bitcast(F32), 0.0)
                pool.memset(stacks.k[0:STACKED, HALF:2 * HALF].bitcast(F32), 0.0)
            for c in range(CHUNKS):
                for i in range(2):
                    pool.wait_ge(middle_ready.sem, middle_ready.at(2 * c + i + 1))
                    pool.tensor_tensor(parts[:, c % 2, 3 * i + 2, :], rest[:, i, :],
                                       parts[:, c % 2, 3 * i + 1, :], ALU.subtract).then_inc(low_ready.sem, 1)
            if not rotary:
                pool.memset(stacks.k[0:STACKED, HALF:2 * HALF].bitcast(F32), 0.0)

        @block.sync
        def _(sp):
            for c in range(CHUNKS):
                if c == CHUNKS // BATCH:
                    load_stacks(core, sp, 0, stacks, stored)
                sp.wait_ge(high_ready.sem, high_ready.at(2 * c + 2))
                sp.wait_ge(low_ready.sem, low_ready.at(2 * c + 2))
                sp.dma_start(stacks.parts[:, :, c * CW:(c + 1) * CW].rearrange("a p n -> p a n"),
                             parts[:, c % 2, :, :]).then_inc(stored[c % 2].sem, 16)

    ones_set.passed(1)
    for s in (high_ready, rest_ready, middle_ready, low_ready):
        s.passed(2 * CHUNKS)
    turned.passed(CHUNKS)
    v_ready.passed(CHUNKS)
    for s in stored:
        s.passed(16 * CHUNKS // 2)
    if rotary:
        proj_ready.passed(CHUNKS)
        step_done.passed(2 * CHUNKS)
        sq_ready.passed(5 * CHUNKS)
        rstd_ready.passed(CHUNKS)
        qk_ready.passed(CHUNKS)
        var_step.passed(ROOT_STEPS * CHUNKS)
        root_ready.passed(CHUNKS)
    else:
        vps_ready.passed(CHUNKS)


def key_tiles(qt, rotary):
    if rotary and qt == 0:
        return 2, 1, "rot_01"
    if rotary and qt == 1:
        return 2, 1, "rot_11"
    return qt + 1, qt, "diag"


GROUP = 4
GROUPS = ALL_HEADS // GROUP
AHEAD = 6
SLOT = P // GROUP
UNITS = GROUP * SEQ_TILES
RING = 3
PROBS_RING = 4


def max_units(heads, whole=0):
    out = []
    for i, head in enumerate(heads):
        merged = i < len(heads) - whole
        if merged:
            out.append((head, ((0, 0), (1, 0))))
        else:
            out += [(head, ((0, 0),)), (head, ((1, 0),))]
        for qt in range(2, SEQ_TILES):
            out.append((head, ((qt, 0),)))
            if qt >= CHUNK:
                out.append((head, ((qt, CHUNK),)))
    return out


def plan_side(heads, settle_after, rows_after, turns, whole=0):
    out = [("max", *u) for u in max_units([h for h in heads], whole)]
    if settle_after is not None:
        at = len(max_units(heads[:settle_after]))
        out[at - 1] = ("settle", *out[at - 1][1:])
        out.insert(min(at + rows_after, len(out)), ("rows",))
    if turns:
        at = min(6, len(out))
        out[at:at] = [("turn", 0)]
        at = min(9, len(out))
        out[at:at] = [("turn", 1)]
    return out


def query_spans(rotary):
    out = []
    for kt in range(SEQ_TILES):
        q0 = 0 if rotary and kt == 1 else kt * P
        out += [(kt, max(q0, s), s + CW) for s in range(0, SEQ, CW) if q0 < s + CW]
    return out


WEIGH_W = 256
SEMAPHORE_NS = 200


def interleave(side, rotary):
    spans = query_spans(rotary)
    pe = scalar = vector = 0.0
    exp_done, side_done, weighed = [], [], []
    pieces = [(i, c, min(c + WEIGH_W, b)) for i, (_, a, b) in enumerate(spans) for c in range(a, b, WEIGH_W)]
    ends = {i: b for i, (_, a, b) in enumerate(spans)}
    out, never = [], float("inf")
    while len(exp_done) < GROUP * len(spans) or pieces or len(side_done) < len(side):
        n, k = len(exp_done), len(side_done)
        i, j = divmod(n, GROUP)
        ready = {}
        if k < len(side):
            early = side[k][0] == "turn" and n < GROUP
            ready["side"] = never if early else side_done[k - RING] + SEMAPHORE_NS if k >= RING else 0.0
        if i < len(spans):
            blocked = len(weighed) < i - PROBS_RING + 1
            ready["score"] = never if blocked else exp_done[n - RING] + SEMAPHORE_NS if n >= RING else 0.0
        if pieces:
            at = GROUP * (pieces[0][0] + 1)
            ready["weigh"] = exp_done[at - 1] + SEMAPHORE_NS if n >= at else never
        what = min(ready, key=lambda kind: max(ready[kind], pe))
        pe = max(pe, ready[what])
        if what == "side":
            kind = side[k][0]
            cols = 4 * P if kind in ("turn", "rows") else sum(min(CHUNK, qt + 1 - k0) * P for qt, k0 in side[k][2])
            pe += cols * (0.6 if kind == "turn" else 0.42) + 60
            vector = max(vector, pe + SEMAPHORE_NS) + cols * 1.05 + 60 + (1300 if kind == "settle" else 0)
            side_done.append(vector)
            out.append(("side", k))
        elif what == "score":
            w = spans[i][2] - spans[i][1]
            pe += w * 0.42 + 60
            needed = weighed[i - PROBS_RING] + SEMAPHORE_NS if i >= PROBS_RING else 0.0
            scalar = max(scalar, pe + SEMAPHORE_NS, needed) + w * 0.83 + 70
            exp_done.append(scalar)
            out.append(("score", i, j))
        else:
            i, a, b = pieces.pop(0)
            pe += (b - a) * 1.79
            if b == ends[i]:
                weighed.append(pe)
            out.append(("weigh", i, a, b))
    return out


def stage_attend(core, rotary, stacks, v_tok, o_tok):
    nc = core.nc
    side_ready = core.semaphore("att_side_ready")
    side_free = core.semaphore("att_side_bank_free")
    split = core.semaphore("att_max_split_step")
    rows_stacked = core.semaphore("att_max_rows_stacked")
    scores_ready = core.semaphore("att_scores_ready")
    exp_done = core.semaphore("att_exp_done")
    weighed = core.semaphore("att_probs_used")
    v_staged = core.semaphore("att_v_staged")
    sums_copied = core.semaphore("att_sums_copied")
    inv_ready = core.semaphore("att_inverse_ready")
    pad_set = core.semaphore("att_v_pad_set")
    stacked = [core.semaphore(f"op_stacks_loaded_{b}") for b in range(BATCH)]
    stored = [core.semaphore(f"op_parts_stored_{i}") for i in range(2)]
    q_stack, k_stack = stacks.q, stacks.k

    PROLOGUE = plan_side(list(range(GROUP)), GROUP, 0, False)
    FIRST = plan_side(list(range(GROUP, GROUP + AHEAD)), GROUP, 10, False)
    STEADY = plan_side([AHEAD + i for i in range(GROUP)], 2, 10, True, whole=1)
    LATE = plan_side([AHEAD, AHEAD + 1], 2, 2, True)
    LAST = plan_side([], None, 0, True)
    SPANS = query_spans(rotary)
    SCORES = GROUP * len(SPANS)
    FIRST_HALF = max(i for i, (_, a, _) in enumerate(SPANS) if a < CW) + 1
    assert FIRST_HALF <= len(SPANS) - PROBS_RING
    assert len(STEADY) % RING == 0 and SCORES % RING == 0 and len(SPANS) % PROBS_RING == 0
    STEADY_GROUPS = (1, GROUPS - 2)
    before = {0: len(PROLOGUE)}
    before[1] = before[0] + len(FIRST)
    for g in range(2, GROUPS - 1):
        before[g] = before[g - 1] + len(STEADY)
    before[GROUPS - 1] = before[GROUPS - 2] + len(LATE)
    SIDE = before[GROUPS - 1] + 2 * len(LAST)
    SPLIT = 7
    with ExitStack() as ctx:
        def sb(name, shape, dt=F32):
            return core.sbuf(ctx, name, shape, dt)

        side_ps = core.psum(ctx, "side_ps", [P, RING, CW])
        score_ps = core.psum(ctx, "score_ps", [P, RING, CW])
        sums_ps = core.psum(ctx, "sums_ps", [P, SEQ])
        probs = sb("probs", [P, PROBS_RING, GROUP, CW])
        v_group = sb("v_group", [P, GROUP, SEQ_TILES, SLOT])
        sums = sb("sums", [P, SEQ])
        negmax = sb("negmax", [P, ALL_HEADS * (SEQ_TILES + CHUNK)])
        group_max = sb("group_max", [P, GROUP, SEQ_TILES])
        parts = sb("parts", [P, 3, UNITS], BF16)
        rows = sb("rows", [P, P], BF16)
        inverse = sb("inverse", [P, 2, CHUNK, GROUP])
        block = ctx.enter_context(nc.Block())
        COLS = SEQ_TILES + CHUNK
        eye = field(core.masks, MASKS, "ident")

        def column(qt, k0):
            return qt if k0 == 0 else SEQ_TILES + qt - CHUNK

        def seen(qt, k0):
            n, m, mask = key_tiles(qt, rotary)
            return min(n - k0, CHUNK), m, mask

        @block.tensor
        def _(pe):
            def side(work, g, n, n0, base):
                pe.wait_ge(side_free.sem, n + side_free.at(n0 + 1))
                bank = side_ps[:, (base + n0) % RING, :]
                if work[0] == "rows":
                    pe.wait_ge(split.sem, (g + 1) * SPLIT + split.at(SPLIT))
                    pe.transpose(bank.bitcast(BF16)[0:3 * UNITS, 0:P], parts[:, :, :].rearrange("p a u -> p (a u)"),
                                 eye).then_inc(side_ready.sem, 1)
                    return
                if work[0] == "turn":
                    pe.wait_ge(sums_copied.sem, (g - 1) * 2 + sums_copied.at(work[1] + 1))
                    for i in range(CHUNK):
                        t = work[1] * CHUNK + i
                        last = pe.transpose(bank[:, i * P:(i + 1) * P], sums[:, t * P:(t + 1) * P], core.ident)
                    last.then_inc(side_ready.sem, 1)
                    return
                head = g * GROUP + work[1]
                at = 0
                for qt, k0 in work[2]:
                    n_keys, m, mask = seen(qt, k0)
                    out = bank[:, at:at + n_keys * P]
                    here = k0 <= m < k0 + n_keys
                    if here:
                        pe.matmul(out[:, (m - k0) * P:(m - k0 + 1) * P], eye, field(core.masks, MASKS, mask),
                                  start=True, stop=False, skip_group_check=True)
                    last = pe.matmul(out, q_stack[0:STACKED, bass.ds(head * SEQ + qt * P, P)],
                                     k_stack[0:STACKED, bass.ds(head * SEQ + k0 * P, n_keys * P)],
                                     start=not here, stop=True, skip_group_check=here)
                    at += n_keys * P
                last.then_inc(side_ready.sem, 1)

            def score(g, i, j):
                n = i * GROUP + j
                if n == 0:
                    pe.wait_ge(rows_stacked.sem, g * 48 + rows_stacked.at(48))
                pe.wait_ge(exp_done.sem, g * SCORES + exp_done.at(n + 1))
                head = g * GROUP + j
                kt, a, b = SPANS[i]
                out = score_ps[:, n % RING, 0:b - a]
                keys = k_stack[0:STACKED, bass.ds(head * SEQ + kt * P, P)]
                queries = q_stack[0:STACKED, bass.ds(head * SEQ + a, b - a)]
                here = (i == 0 or SPANS[i - 1][0] != kt) and not (rotary and kt == 0)
                if here:
                    mask = "rot_T" if rotary and kt == 1 else "diag_T"
                    pe.matmul(out[:, 0:MASKS[mask][1]], eye, field(core.masks, MASKS, mask), start=True,
                              stop=False, skip_group_check=True)
                pe.matmul(out, keys, queries, start=not here, stop=True,
                          skip_group_check=here).then_inc(scores_ready.sem, 1)

            def weigh(g, i, a, b, first_group):
                kt, q0, q1 = SPANS[i]
                if i == 0 and a == 0:
                    pe.wait_ge(v_staged.sem, g + v_staged.at(1))
                if i < 2 and a == q0 and not first_group:
                    pe.wait_ge(sums_copied.sem, (g - 1) * 2 + sums_copied.at(i + 1))
                if a == q0:
                    pe.wait_ge(exp_done.sem, g * SCORES + exp_done.at(RING + GROUP * (i + 1)))
                for j in range(GROUP):
                    last = pe.matmul(sums_ps[j * SLOT:(j + 1) * SLOT, a:b], v_group[:, j, kt, :],
                                     probs[:, i % PROBS_RING, j, a - q0:b - q0], start=kt == 0 and a == q0,
                                     stop=kt == SEQ_TILES - 1, skip_group_check=True)
                if b == q1:
                    last.then_inc(weighed.sem, 1)

            def step(g, plan, n, base, first_group=False):
                for what in interleave(plan, rotary):
                    if what[0] == "side":
                        side(plan[what[1]], g, n, what[1], base)
                    elif what[0] == "score":
                        score(g, *what[1:])
                    else:
                        weigh(g, *what[1:], first_group)

            pe.wait_ge(stacked[0].sem, stacked[0].at(16 * STACK_LOADS))
            for i, work in enumerate(PROLOGUE):
                side(work, 0 if work[0] != "rows" else -1, 0, i, 0)
            step(0, FIRST, before[0], before[0], True)
            pe.wait_ge(stacked[1].sem, stacked[1].at(16 * STACK_LOADS))
            with pe.Fori(*STEADY_GROUPS) as g:
                step(g, STEADY, (g - 1) * len(STEADY) + before[1], before[1])
            step(GROUPS - 2, LATE, before[GROUPS - 2], before[GROUPS - 2])
            step(GROUPS - 1, LAST, before[GROUPS - 1], before[GROUPS - 1])
            for i, work in enumerate(LAST):
                n = before[GROUPS - 1] + len(LAST)
                side(work, GROUPS, n, i, n)

        @block.vector
        def _(dve):
            dve.sem_inc(side_free.sem, RING)

            def side(work, g, n, n0, base):
                dve.wait_ge(side_ready.sem, n + side_ready.at(n0 + 1))
                bank = side_ps[:, (base + n0) % RING, :]
                if work[0] == "rows":
                    dve.tensor_copy(rows[0:3 * UNITS, :], bank.bitcast(BF16)[0:3 * UNITS, 0:P]).then_inc(side_free.sem, 1)
                    return
                if work[0] == "turn":
                    tiles = bank.rearrange("p (t j d) -> p t j d", t=CHUNK, j=GROUP)
                    dve.reciprocal(inverse[:, work[1], :, :], tiles[:, :, :, DH]).then_inc(inv_ready.sem, 1)
                    dve.wait_ge(inv_ready.sem, (g - 1) * 2 + inv_ready.at(work[1] + 1))
                    out = o_tok[:, work[1] * CHUNK:(work[1] + 1) * CHUNK, bass.ds(g - 1, 1), :]
                    dve.tensor_tensor(out.rearrange("p t o (j d) -> p t (o j) d", j=GROUP), tiles[:, :, :, 0:DH],
                                      inverse[:, work[1], :, :, None].to_broadcast([P, CHUNK, GROUP, DH]),
                                      ALU.mult).then_inc(side_free.sem, 1)
                    return
                head = g * GROUP + work[1]
                at = 0
                for qt, k0 in work[2]:
                    n_keys = seen(qt, k0)[0]
                    last = dve.tensor_reduce(negmax[:, bass.ds(head * COLS + column(qt, k0), 1)],
                                             bank[:, at:at + n_keys * P], AX.X, ALU.max, negate=True)
                    at += n_keys * P
                last.then_inc(side_free.sem, 1)
                if work[0] == "settle":
                    dve.wait_ge(side_free.sem, n + side_free.at(RING + n0 + 1))
                    settle(g + 1 if base else 0)

            def settle(g):
                own = negmax[:, bass.ds(g * (GROUP * COLS), GROUP * COLS)].rearrange("p (j c) -> p j c", c=COLS)
                flat = group_max[:, :, :].rearrange("p j t -> p (j t)")
                dve.tensor_copy(group_max[:, :, 0:CHUNK], own[:, :, 0:CHUNK]).then_inc(split.sem, 1)
                dve.tensor_tensor(group_max[:, :, CHUNK:SEQ_TILES], own[:, :, CHUNK:SEQ_TILES],
                                  own[:, :, SEQ_TILES:COLS], ALU.min).then_inc(split.sem, 1)
                dve.wait_ge(split.sem, g * SPLIT + split.at(2))
                dve.tensor_copy(parts[:, 0, :], flat).then_inc(split.sem, 1)
                dve.wait_ge(split.sem, g * SPLIT + split.at(3))
                dve.tensor_tensor(flat, flat, parts[:, 0, :], ALU.subtract).then_inc(split.sem, 1)
                dve.wait_ge(split.sem, g * SPLIT + split.at(4))
                dve.tensor_copy(parts[:, 1, :], flat).then_inc(split.sem, 1)
                dve.wait_ge(split.sem, g * SPLIT + split.at(5))
                dve.tensor_tensor(flat, flat, parts[:, 1, :], ALU.subtract).then_inc(split.sem, 1)
                dve.wait_ge(split.sem, g * SPLIT + split.at(6))
                dve.tensor_copy(parts[:, 2, :], flat).then_inc(split.sem, 1)

            for i, work in enumerate(PROLOGUE):
                side(work, 0, 0, i, 0)
            for i, work in enumerate(FIRST):
                side(work, 0, before[0], i, before[0])
            with dve.Fori(*STEADY_GROUPS) as g:
                for i, work in enumerate(STEADY):
                    side(work, g, (g - 1) * len(STEADY) + before[1], i, before[1])
            for g, plan in ((GROUPS - 2, LATE), (GROUPS - 1, LAST)):
                for i, work in enumerate(plan):
                    side(work, g, before[g], i, before[g])
            n = before[GROUPS - 1] + len(LAST)
            for i, work in enumerate(LAST):
                side(work, GROUPS, n, i, n)

        @block.scalar
        def _(act):
            act.sem_inc(exp_done.sem, RING)

            def copy_sums(g, half, spans):
                act.wait_ge(weighed.sem, g * len(SPANS) + weighed.at(PROBS_RING + spans))
                cols = slice(half * CW, (half + 1) * CW)
                act.copy(sums[:, cols], sums_ps[:, cols]).then_inc(sums_copied.sem, 1)

            def group(g, first_group):
                for n in range(SCORES):
                    i, j = divmod(n, GROUP)
                    if n == 2 and not first_group:
                        copy_sums(g - 1, 1, len(SPANS))
                    if n == SCORES - GROUP:
                        copy_sums(g, 0, FIRST_HALF)
                    act.wait_ge(scores_ready.sem, g * SCORES + scores_ready.at(n + 1))
                    if j == 0:
                        act.wait_ge(weighed.sem, g * len(SPANS) + weighed.at(i + 1))
                    w = SPANS[i][2] - SPANS[i][1]
                    act.activation(probs[:, i % PROBS_RING, j, 0:w], score_ps[:, n % RING, 0:w],
                                   ACT.Exp).then_inc(exp_done.sem, 1)

            group(0, True)
            with act.Fori(1, GROUPS) as g:
                group(g, False)
            copy_sums(GROUPS - 1, 1, len(SPANS))

        @block.gpsimd
        def _(pool):
            pool.sem_inc(weighed.sem, PROBS_RING)
            pool.memset(v_group[:, :, :, :], 0.0).then_inc(pad_set.sem, 1)
            pool.wait_ge(pad_set.sem, pad_set.at(1))
            with pool.Fori(0, GROUPS) as g:
                pool.wait_ge(weighed.sem, g * len(SPANS) + weighed.at(PROBS_RING))
                pool.tensor_copy(v_group[:, :, :, 0:DH + 1], v_tok[:, bass.ds(g * GROUP, GROUP), :, :]
                                 ).then_inc(v_staged.sem, 1)

        @block.sync
        def _(sp):
            def stack(g, n):
                sp.wait_ge(side_free.sem, n)
                for a in range(3):
                    dst = q_stack[ROW_MAX + a:ROW_MAX + a + 1, bass.ds(g * GROUP * SEQ, GROUP * SEQ)]
                    sp.dma_start(dst.rearrange("o (u n) -> o u n", n=P), rows[a * UNITS:(a + 1) * UNITS, :]
                                 ).then_inc(rows_stacked.sem, 16)

            load_stacks(core, sp, 1, stacks, stored)
            stack(0, side_free.at(RING + PROLOGUE.index(("rows",)) + 1))
            stack(1, side_free.at(RING + before[0] + FIRST.index(("rows",)) + 1))
            with sp.Fori(*STEADY_GROUPS) as g:
                stack(g + 1, (g - 1) * len(STEADY) + side_free.at(RING + before[1] + STEADY.index(("rows",)) + 1))
            stack(GROUPS - 1, side_free.at(RING + before[GROUPS - 2] + LATE.index(("rows",)) + 1))
            sp.wait_ge(rows_stacked.sem, rows_stacked.at(48 * GROUPS))

    for s in stacked:
        s.passed(16 * STACK_LOADS)
    side_ready.passed(SIDE)
    side_free.passed(SIDE + RING)
    split.passed(SPLIT * GROUPS)
    rows_stacked.passed(48 * GROUPS)
    scores_ready.passed(SCORES * GROUPS)
    exp_done.passed(SCORES * GROUPS + RING)
    weighed.passed(len(SPANS) * GROUPS + PROBS_RING)
    v_staged.passed(GROUPS)
    sums_copied.passed(2 * GROUPS)
    inv_ready.passed(2 * GROUPS)
    pad_set.passed(1)


def stage_project(core, x, w_out, o_tok=None, o_all=None, bo=None, shift=0):
    nc = core.nc
    turned = core.semaphore("prj_turned")
    oT_ready = core.semaphore("prj_oT_ready")
    product = core.semaphore("prj_product_ready")
    added = core.semaphore("prj_added")

    def rows_of(t):
        if o_all is not None:
            return o_all[:, t, :]
        b, t = divmod(t, SEQ_TILES)
        own = o_tok[:, t, b * (GROUPS // BATCH):(b + 1) * (GROUPS // BATCH), :]
        return own.rearrange("p g f -> p (g f)")

    HALVES = 2
    with ExitStack() as ctx:
        oT = core.sbuf(ctx, "oT", [P, BATCH, SEQ], F32)
        turned_ps = core.psum(ctx, "turned_ps", [P, 2, CW], F32)
        prod_ps = core.psum(ctx, "prod_ps", [P, 2, CW], F32)
        block = ctx.enter_context(nc.Block())

        @block.tensor
        def _(pe):
            for c in range(CHUNKS):
                if c >= 2:
                    pe.wait_ge(oT_ready.sem, oT_ready.at(c - 1))
                for j in range(CHUNK):
                    last = pe.transpose(turned_ps[:, c % 2, j * P:(j + 1) * P], rows_of(CHUNK * c + j),
                                        core.ident)
                last.then_inc(turned.sem, 1)
                if c % HALVES != HALVES - 1:
                    continue
                b = c // HALVES
                pe.wait_ge(oT_ready.sem, oT_ready.at(c + 1))
                for half in range(HALVES):
                    if b >= 1:
                        pe.wait_ge(added.sem, added.at(HALVES * (b - 1) + half + 1))
                    for j in range(CHUNK):
                        t = half * CHUNK + j
                        out = prod_ps[:, half, j * P:(j + 1) * P]
                        last = pe.matmul(out, oT[:, b, t * P:(t + 1) * P], w_out, start=True, stop=bo is None)
                        if bo is not None:
                            last = pe.matmul(out, core.ones[0:1, :], bo[0:1, :], start=False, stop=True)
                    last.then_inc(product.sem, 1)

        @block.scalar
        def _(act):
            for c in range(CHUNKS):
                b, half = divmod(c, HALVES)
                act.wait_ge(turned.sem, turned.at(c + 1))
                first = (half * CW - shift) % SEQ
                w = min(CW, SEQ - first)
                last = act.copy(oT[:, b, first:first + w], turned_ps[:, c % 2, 0:w])
                if w < CW:
                    last = act.copy(oT[:, b, 0:CW - w], turned_ps[:, c % 2, w:CW])
                last.then_inc(oT_ready.sem, 1)

        @block.vector
        def _(dve):
            for c in range(CHUNKS):
                dve.wait_ge(product.sem, product.at(c + 1))
                xc = x[:, CHUNK * c:CHUNK * (c + 1), :].rearrange("p t d -> p (t d)")
                dve.tensor_tensor(xc, prod_ps[:, c % HALVES, :], xc, ALU.add).then_inc(added.sem, 1)

    for s in (turned, oT_ready, product, added):
        s.passed(CHUNKS)


def top_two(dve, step, scores, rank, picks, best, work):
    wide = [P, TILES, EXPERTS]
    left, equal, order = work
    n = [0]

    def then(ins, wait=True):
        ins.then_inc(step.sem, 1)
        n[0] += 1
        if wait:
            dve.wait_ge(step.sem, step.at(n[0]))

    here = scores
    for i in range(2):
        top = best[:, i, :]
        then(dve.tensor_reduce(top, here, AX.X, ALU.max))
        then(dve.tensor_tensor(equal, here, top[:, :, None].to_broadcast(wide), ALU.is_equal))
        then(dve.tensor_tensor(equal, equal, rank[:, None, :].to_broadcast(wide), ALU.mult))
        then(dve.tensor_reduce(order, equal, AX.X, ALU.max))
        then(dve.tensor_tensor(picks[:, i, :, :], equal, order[:, :, None].to_broadcast(wide), ALU.is_equal))
        if i == 0:
            then(dve.scalar_tensor_tensor(left, picks[:, 0, :, :], -4.0, scores, ALU.mult, ALU.add))
            here = left
    return n[0]


TOP_TWO_STEPS = 11


def stage_experts(core, x, xT, weights):
    nc = core.nc
    logits_ready = core.semaphore("moe_logits_ready")
    probs_ready = core.semaphore("moe_probs_ready")
    step = core.semaphore("moe_route_step")
    hidden_ready = core.semaphore("moe_hidden_ready")
    relu_ready = core.semaphore("moe_relu_ready")
    square_ready = core.semaphore("moe_square_ready")
    out_ready = core.semaphore("moe_out_ready")
    added = core.semaphore("moe_added")
    blocks_done = core.semaphore("moe_block_used")
    rank = field(core.const, CONST, "rank")
    BUF = 4
    UP_AHEAD = 2
    EXPERT_OF = [e for e, n in enumerate(EXPERT_BLOCKS) for _ in range(n)]
    firsts = [sum(EXPERT_BLOCKS[:e]) for e in range(EXPERTS)]
    with ExitStack() as ctx:
        def sb(name, shape, dt=F32):
            return core.sbuf(ctx, name, shape, dt)

        logits_ps = core.psum(ctx, "logits_ps", [P, CW], F32)
        hidden_ps = core.psum(ctx, "hidden_ps", [P, BUF, CW], F32)
        out_ps = core.psum(ctx, "out_ps", [P, 2, CW], F32)
        probs = sb("probs", [P, TILES, EXPERTS])
        left = sb("left", [P, TILES, EXPERTS])
        equal = sb("equal", [P, TILES, EXPERTS])
        order = sb("order", [P, TILES])
        picks = sb("picks", [P, 2, TILES, EXPERTS])
        best = sb("best", [P, 2, TILES])
        total = sb("total", [P, TILES])
        share = sb("share", [P, TILES, EXPERTS])
        relu = sb("relu", [P, BUF, CW])
        square = sb("square", [P, BUF, CW])
        block = ctx.enter_context(nc.Block())
        ROUTE = TOP_TWO_STEPS + 6

        @block.tensor
        def _(pe):
            for t in range(TILES):
                last = pe.matmul(logits_ps[:, t * EXPERTS:(t + 1) * EXPERTS], xT[:, t * P:(t + 1) * P],
                                 field(weights, W_MOE, "router"), start=True, stop=True)
            last.then_inc(logits_ready.sem, 1)
            w1, w2 = field(weights, W_MOE, "w1"), field(weights, W_MOE, "w2")

            def up(c, m):
                pe.wait_ge(relu_ready.sem, c * HIDDEN_BLOCKS + relu_ready.at(m + 1))
                c, m = (c, m) if m < HIDDEN_BLOCKS else (c + 1, m - HIDDEN_BLOCKS)
                pe.matmul(hidden_ps[:, m % BUF, :], w1[:, m * P:(m + 1) * P], xT[:, bass.ds(c * CW, CW)],
                          start=True, stop=True).then_inc(hidden_ready.sem, 1)

            def down(c, m):
                e = EXPERT_OF[m]
                pe.wait_ge(square_ready.sem, c * HIDDEN_BLOCKS + square_ready.at(BUF + m + 1))
                if m == firsts[e]:
                    pe.wait_ge(added.sem, c * EXPERTS + added.at(e + 1))
                for j in range(CHUNK):
                    last = pe.matmul(out_ps[:, e % 2, j * P:(j + 1) * P],
                                     square[:, m % BUF, j * P:(j + 1) * P], w2[:, m * P:(m + 1) * P],
                                     start=m == firsts[e] and j == 0, stop=m == firsts[e] + EXPERT_BLOCKS[e] - 1,
                                     skip_group_check=True)
                last.then_inc(out_ready.sem, 1)

            for m in range(UP_AHEAD):
                up(0, m)
            with pe.Fori(0, CHUNKS - 1) as c:
                for m in range(HIDDEN_BLOCKS):
                    up(c, m + UP_AHEAD)
                    down(c, m)
            for m in range(HIDDEN_BLOCKS):
                if m + UP_AHEAD < HIDDEN_BLOCKS:
                    up(CHUNKS - 1, m + UP_AHEAD)
                down(CHUNKS - 1, m)

        @block.scalar
        def _(act):
            act.wait_ge(logits_ready.sem, logits_ready.at(1))
            act.activation(probs[:, :, :].rearrange("p t e -> p (t e)"), logits_ps[:, 0:TILES * EXPERTS],
                           ACT.Sigmoid).then_inc(probs_ready.sem, 1)
            act.sem_inc(relu_ready.sem, BUF)
            act.sem_inc(square_ready.sem, BUF)

            def relu_of(c, m):
                act.wait_ge(hidden_ready.sem, c * HIDDEN_BLOCKS + hidden_ready.at(m + 1))
                act.wait_ge(square_ready.sem, c * HIDDEN_BLOCKS + square_ready.at(m + 1))
                act.activation(relu[:, m % BUF, :], hidden_ps[:, m % BUF, :], ACT.Relu).then_inc(relu_ready.sem, 1)

            def square_of(c, m, first):
                act.wait_ge(relu_ready.sem, c * HIDDEN_BLOCKS + relu_ready.at(BUF + m + 1))
                if not first or m >= BUF:
                    act.wait_ge(out_ready.sem, c * HIDDEN_BLOCKS + out_ready.at(m - BUF + 1))
                act.activation(square[:, m % BUF, :], relu[:, m % BUF, :], ACT.Square).then_inc(square_ready.sem, 1)

            def chunk(c, first):
                for m in range(HIDDEN_BLOCKS):
                    relu_of(c, m)
                    square_of(c, m, first)

            chunk(0, True)
            with act.Fori(1, CHUNKS) as c:
                chunk(c, False)

        @block.vector
        def _(dve):
            dve.sem_inc(added.sem, 2)
            dve.wait_ge(probs_ready.sem, probs_ready.at(1))
            n = top_two(dve, step, probs[:, :, :], rank, picks, best, (left[:, :, :], equal[:, :, :], order[:, :]))
            dve.tensor_tensor(total[:, :], best[:, 0, :], best[:, 1, :], ALU.add).then_inc(step.sem, 1)
            dve.wait_ge(step.sem, step.at(n + 1))
            dve.tensor_scalar(total[:, :], total[:, :], 1e-20, None, ALU.add).then_inc(step.sem, 1)
            dve.wait_ge(step.sem, step.at(n + 2))
            dve.reciprocal(total[:, :], total[:, :]).then_inc(step.sem, 1)
            dve.wait_ge(step.sem, step.at(n + 3))
            dve.tensor_tensor(share[:, :, :], picks[:, 0, :, :], picks[:, 1, :, :], ALU.add).then_inc(step.sem, 1)
            dve.wait_ge(step.sem, step.at(n + 4))
            dve.tensor_tensor(share[:, :, :], share[:, :, :], probs[:, :, :], ALU.mult).then_inc(step.sem, 1)
            dve.wait_ge(step.sem, step.at(n + 5))
            dve.tensor_tensor(share[:, :, :], share[:, :, :],
                              total[:, :, None].to_broadcast([P, TILES, EXPERTS]), ALU.mult).then_inc(step.sem, 1)
            dve.wait_ge(step.sem, step.at(n + 6))

            def add(c, e):
                dve.wait_ge(out_ready.sem, c * HIDDEN_BLOCKS + out_ready.at(firsts[e] + EXPERT_BLOCKS[e]))
                dve.wait_ge(added.sem, c * EXPERTS + added.at(e + 2))
                for j in range(CHUNK):
                    t = c * CHUNK + j
                    xt = x[:, bass.ds(t, 1), :].rearrange("p o d -> p (o d)")
                    s = share[:, bass.ds(t, 1), e]
                    last = dve.scalar_tensor_tensor(xt, out_ps[:, e % 2, j * P:(j + 1) * P], s, xt,
                                                    ALU.mult, ALU.add)
                last.then_inc(added.sem, 1)

            with dve.Fori(0, CHUNKS) as c:
                for e in range(EXPERTS):
                    add(c, e)

    logits_ready.passed(1)
    probs_ready.passed(1)
    step.passed(ROUTE)
    hidden_ready.passed(CHUNKS * HIDDEN_BLOCKS)
    for s in (relu_ready, square_ready):
        s.passed(BUF + CHUNKS * HIDDEN_BLOCKS)
    out_ready.passed(CHUNKS * HIDDEN_BLOCKS)
    added.passed(2 + CHUNKS * EXPERTS)


def stage_pair(core, x, xT, weights):
    nc = core.nc
    vo_ready = core.semaphore("pair_vo_product")
    vo_copied = core.semaphore("pair_vo_copied")
    staged = core.semaphore("pair_tiles_staged")
    step = core.semaphore("pair_stage_step")
    q_ready = core.semaphore("pair_q_ready")
    k_ready = core.semaphore("pair_k_ready")
    v_ready = core.semaphore("pair_v_ready")
    q_copied = core.semaphore("pair_q_copied")
    prod_ready = core.semaphore("pair_qk_ready")
    chain = core.semaphore("pair_softmax_step")
    exp_ready = core.semaphore("pair_exp_ready")
    ctx_ready = core.semaphore("pair_context_ready")
    turned = core.semaphore("pair_half_turned")
    copied = core.semaphore("pair_half_copied")
    out_ready = core.semaphore("pair_out_ready")
    added = core.semaphore("pair_added")
    HALF = PAIR_BLOCKS // 2
    CHAIN = 8
    with ExitStack() as ctx:
        def sb(name, shape, dt=F32):
            return core.sbuf(ctx, name, shape, dt)

        q_ps = core.psum(ctx, "q_ps", [P, PAIR_W])
        k_ps = core.psum(ctx, "k_ps", [P, PAIR_W])
        v_ps = core.psum(ctx, "v_ps", [P, PAIR_W])
        turned_ps = core.psum(ctx, "turned_ps", [P, CW])
        out_ps = core.psum(ctx, "out_ps", [P, CW])
        vo = sb("vo", [P, P])
        y0 = sb("y0", [P, 2, P])
        y1 = sb("y1", [P, 2, P])
        dy = sb("dy", [P, 2, P])
        q = sb("q", [P, PAIR_W])
        prod = sb("prod", [P, PAIR_W])
        d = sb("d", [P, PAIR_HEADS])
        top = sb("top", [P, PAIR_HEADS])
        shifted = sb("shifted", [P, 2, PAIR_HEADS])
        e = sb("e", [P, 2, PAIR_HEADS])
        total = sb("total", [P, PAIR_HEADS])
        p1 = sb("p1", [P, PAIR_HEADS])
        context = sb("context", [P, PAIR_W])
        contextT = sb("contextT", [P, PAIR_W])
        block = ctx.enter_context(nc.Block())

        @block.gpsimd
        def _(pool):
            def stage(t, buf, used):
                if used:
                    pool.wait_ge(out_ready.sem, t + out_ready.at(0))
                a0 = xT[:, bass.ds(t * P, P)]
                a1 = xT[:, bass.ds(SEQ + t * P, P)]
                pool.tensor_copy(y0[:, buf, :], a0)
                pool.tensor_copy(y1[:, buf, :], a1)
                pool.tensor_tensor(dy[:, buf, :], a1, a0, ALU.subtract).then_inc(staged.sem, 1)

            stage(0, 0, False)
            stage(1, 1, False)
            with pool.Fori(1, SEQ_TILES // 2) as i:
                for buf in range(2):
                    stage(i * 2 + buf, buf, True)

        @block.tensor
        def _(pe):
            pe.sem_inc(turned.sem, 2)
            pe.sem_inc(out_ready.sem, 1)
            for m in range(PAIR_BLOCKS):
                last = pe.matmul(out_ps[:, 0:P], field(weights, W_PAIR, "v_T")[:, m * P:(m + 1) * P],
                                 field(weights, W_PAIR, "out")[:, m * P:(m + 1) * P],
                                 start=m == 0, stop=m == PAIR_BLOCKS - 1)
            last.then_inc(vo_ready.sem, 1)
            pe.wait_ge(vo_copied.sem, vo_copied.at(1))

            def product(out, lhs, name, ready):
                for k0 in range(0, PAIR_W, CW):
                    last = pe.matmul(out[:, k0:k0 + CW], lhs, field(weights, W_PAIR, name)[:, k0:k0 + CW],
                                     start=True, stop=True)
                last.then_inc(ready.sem, 1)

            def turn(t, half):
                pe.wait_ge(ctx_ready.sem, t + ctx_ready.at(2))
                pe.wait_ge(copied.sem, t * 2 + copied.at(half + 1))
                for m in range(HALF):
                    at = (half * HALF + m) * P
                    last = pe.transpose(turned_ps[:, m * P:(m + 1) * P], context[:, at:at + P], core.ident)
                last.then_inc(turned.sem, 1)

            def out(t, buf):
                pe.wait_ge(copied.sem, t * 2 + copied.at(3))
                pe.wait_ge(added.sem, t + added.at(1))
                pe.matmul(out_ps[:, 0:P], y0[:, buf, :], vo[:, :], start=True, stop=True)
                pe.matmul(out_ps[:, P:2 * P], y0[:, buf, :], vo[:, :], start=True, stop=False)
                for m in range(PAIR_BLOCKS):
                    last = pe.matmul(out_ps[:, P:2 * P], contextT[:, m * P:(m + 1) * P],
                                     field(weights, W_PAIR, "out")[:, m * P:(m + 1) * P],
                                     start=False, stop=m == PAIR_BLOCKS - 1)
                last.then_inc(out_ready.sem, 1)

            def tile(t, buf, back):
                pe.wait_ge(staged.sem, t + staged.at(1))
                pe.wait_ge(q_copied.sem, t + q_copied.at(1))
                product(q_ps, y1[:, buf, :], "q", q_ready)
                if back:
                    turn(t - 1, 0)
                pe.wait_ge(prod_ready.sem, t + prod_ready.at(1))
                product(k_ps, dy[:, buf, :], "k", k_ready)
                if back:
                    turn(t - 1, 1)
                pe.wait_ge(ctx_ready.sem, t + ctx_ready.at(1))
                product(v_ps, dy[:, buf, :], "v", v_ready)
                if back:
                    out(t - 1, 1 - buf)

            tile(0, 0, False)
            with pe.Fori(0, SEQ_TILES // 2 - 1) as i:
                tile(i * 2 + 1, 1, True)
                tile(i * 2 + 2, 0, True)
            tile(SEQ_TILES - 1, 1, True)
            turn(SEQ_TILES - 1, 0)
            turn(SEQ_TILES - 1, 1)
            out(SEQ_TILES - 1, 1)

        @block.scalar
        def _(act):
            act.sem_inc(q_copied.sem, 1)
            act.sem_inc(copied.sem, 1)
            act.wait_ge(vo_ready.sem, vo_ready.at(1))
            act.copy(vo[:, :], out_ps[:, 0:P]).then_inc(vo_copied.sem, 1)

            def halves(t):
                for half in range(2):
                    act.wait_ge(turned.sem, t * 2 + turned.at(half + 3))
                    if half == 0:
                        act.wait_ge(out_ready.sem, t + out_ready.at(1))
                    act.copy(contextT[:, half * CW:(half + 1) * CW], turned_ps[:, :]).then_inc(copied.sem, 1)

            def tile(t, back):
                act.wait_ge(q_ready.sem, t + q_ready.at(1))
                act.wait_ge(prod_ready.sem, t + prod_ready.at(1))
                act.copy(q[:, :], q_ps[:, :]).then_inc(q_copied.sem, 1)
                if back:
                    halves(t - 1)
                act.wait_ge(chain.sem, t * CHAIN + chain.at(5))
                act.activation(e[:, :, :], shifted[:, :, :], ACT.Exp).then_inc(exp_ready.sem, 1)

            tile(0, False)
            with act.Fori(1, SEQ_TILES) as t:
                tile(t, True)
            halves(SEQ_TILES - 1)

        @block.vector
        def _(dve):
            dve.sem_inc(prod_ready.sem, 1)
            dve.sem_inc(ctx_ready.sem, 1)
            dve.sem_inc(added.sem, 1)

            def tile(t, back):
                def then(ins, n):
                    ins.then_inc(chain.sem, 1)
                    dve.wait_ge(chain.sem, t * CHAIN + chain.at(n))

                dve.wait_ge(q_copied.sem, t + q_copied.at(2))
                dve.wait_ge(k_ready.sem, t + k_ready.at(1))
                dve.tensor_tensor(prod[:, :], k_ps[:, :], q[:, :], ALU.mult).then_inc(prod_ready.sem, 1)
                dve.wait_ge(prod_ready.sem, t + prod_ready.at(2))
                then(dve.tensor_reduce(d[:, :], prod[:, :].rearrange("p (h d) -> p h d", d=PAIR_DH), AX.X, ALU.add), 1)
                then(dve.tensor_scalar(d[:, :], d[:, :], PAIR_DH ** -0.5, None, ALU.mult), 2)
                then(dve.tensor_scalar(top[:, :], d[:, :], 0.0, None, ALU.max), 3)
                then(dve.tensor_scalar(shifted[:, 0, :], top[:, :], -1.0, None, ALU.mult), 4)
                dve.tensor_tensor(shifted[:, 1, :], d[:, :], top[:, :], ALU.subtract).then_inc(chain.sem, 1)
                dve.wait_ge(exp_ready.sem, t + exp_ready.at(1))
                then(dve.tensor_tensor(total[:, :], e[:, 0, :], e[:, 1, :], ALU.add), 6)
                then(dve.reciprocal(total[:, :], total[:, :]), 7)
                then(dve.tensor_tensor(p1[:, :], e[:, 1, :], total[:, :], ALU.mult), 8)
                dve.wait_ge(v_ready.sem, t + v_ready.at(1))
                dve.wait_ge(turned.sem, t * 2 + turned.at(2))
                dve.tensor_tensor(context[:, :].rearrange("p (h d) -> p h d", d=PAIR_DH),
                                  v_ps[:, :].rearrange("p (h d) -> p h d", d=PAIR_DH),
                                  p1[:, :, None].to_broadcast([P, PAIR_HEADS, PAIR_DH]),
                                  ALU.mult).then_inc(ctx_ready.sem, 1)
                if back:
                    add(t - 1)

            def add(t):
                dve.wait_ge(out_ready.sem, t + out_ready.at(2))
                for b in range(BATCH):
                    xt = x[:, bass.ds(b * SEQ_TILES + t, 1), :].rearrange("p o d -> p (o d)")
                    last = dve.tensor_tensor(xt, out_ps[:, b * P:(b + 1) * P], xt, ALU.add)
                last.then_inc(added.sem, 1)

            tile(0, False)
            with dve.Fori(1, SEQ_TILES) as t:
                tile(t, True)
            add(SEQ_TILES - 1)

    for s in (vo_ready, vo_copied):
        s.passed(1)
    for s in (staged, q_ready, k_ready, v_ready, exp_ready):
        s.passed(SEQ_TILES)
    for s in (q_copied, prod_ready, ctx_ready, added, out_ready):
        s.passed(SEQ_TILES + 1)
    chain.passed(CHAIN * SEQ_TILES)
    turned.passed(2 * SEQ_TILES + 2)
    copied.passed(2 * SEQ_TILES + 1)


def stage_recurrence(core, xT, weights, o_all):
    nc = core.nc
    feat_ready = core.semaphore("rec_features_ready")
    vq_ready = core.semaphore("rec_gelu_ready")
    f_copied = core.semaphore("rec_gates_copied")
    f_ready = core.semaphore("rec_sigmoid_ready")
    chain = core.semaphore("rec_step")
    BANKS = 8
    E = 2
    with ExitStack() as ctx:
        def sb(name, shape, dt=F32):
            return core.sbuf(ctx, name, shape, dt)

        feat_ps = core.psum(ctx, "feat_ps", [P, BANKS, CW])
        vq = sb("vq", [P, TILES, 2 * P])
        gates = sb("gates", [P, TILES, P])
        keys = sb("keys", [P, TILES, P])
        spare = sb("spare", [P, SEQ_TILES, P])
        dots = sb("dots", [P, 3, SEQ_TILES, P // E])
        rest = sb("rest", [P, P])
        block = ctx.enter_context(nc.Block())
        lower = field(weights, W_REC, "lower")
        N0, N1 = slice(0, SEQ_TILES), slice(SEQ_TILES, TILES)

        @block.tensor
        def _(pe):
            for t in range(TILES):
                if t >= BANKS:
                    pe.wait_ge(vq_ready.sem, vq_ready.at(t - BANKS + 1))
                pe.matmul(feat_ps[:, t % BANKS, 0:3 * P], xT[:, t * P:(t + 1) * P], field(weights, W_REC, "in"),
                          start=True, stop=True).then_inc(feat_ready.sem, 1)

        @block.scalar
        def _(act):
            for t in range(TILES):
                act.wait_ge(f_copied.sem, f_copied.at(t + 1))
                act.activation(vq[:, t, :], feat_ps[:, t % BANKS, 0:2 * P], ACT.Gelu).then_inc(vq_ready.sem, 1)
            for half in (N0, N1):
                act.wait_ge(f_copied.sem, f_copied.at(half.stop))
                act.activation(gates[:, half, :], gates[:, half, :], ACT.Sigmoid).then_inc(f_ready.sem, 1)

        @block.vector
        def _(dve):
            wide = [P, SEQ_TILES, P]
            n = [0]

            def then(ins):
                ins.then_inc(chain.sem, 1)
                n[0] += 1

            def settle():
                dve.wait_ge(chain.sem, chain.at(n[0]))

            then(dve.tensor_scalar(rest[:, :], lower, -1.0, 1.0, ALU.mult, ALU.add))
            for t in range(TILES):
                dve.wait_ge(feat_ready.sem, feat_ready.at(t + 1))
                dve.tensor_copy(gates[:, t, :], feat_ps[:, t % BANKS, 2 * P:3 * P]).then_inc(f_copied.sem, 1)
            settle()
            for i, half in enumerate((N0, N1)):
                dve.wait_ge(f_ready.sem, f_ready.at(i + 1))
                then(dve.tensor_tensor(gates[:, half, :], gates[:, half, :],
                                       rest[:, None, :].to_broadcast(wide), ALU.mult))
                settle()
                then(dve.tensor_tensor(gates[:, half, :], gates[:, half, :],
                                       lower[:, None, :].to_broadcast(wide), ALU.add))
                settle()
                then(dve.tensor_scalar(keys[:, half, :], gates[:, half, :], -1.0, 1.0, ALU.mult, ALU.add))
                settle()
            dve.wait_ge(vq_ready.sem, vq_ready.at(TILES))

            def dot(i, qn, k):
                then(dve.tensor_tensor(k, k, vq[:, qn, P:2 * P], ALU.mult))
                settle()
                pairs = k.rearrange("p t (h e) -> p t h e", e=E)
                then(dve.tensor_tensor(dots[:, i, :, :], pairs[:, :, :, 0], pairs[:, :, :, 1], ALU.add))
                settle()

            then(dve.tensor_tensor(spare[:, :, :], keys[:, N0, :], gates[:, N1, :], ALU.mult))
            settle()
            dot(1, N1, spare[:, :, :])
            dot(0, N0, keys[:, N0, :])
            dot(2, N1, keys[:, N1, :])
            four = [P, SEQ_TILES, P // E, E]

            def values(half):
                return vq[:, half, 0:P].rearrange("p t (h e) -> p t h e", e=E)

            def times(i):
                return dots[:, i, :, :, None].to_broadcast(four)

            def heads(tile, half):
                return tile[:, half, :].rearrange("p t (h e) -> p t h e", e=E)

            then(dve.tensor_tensor(heads(o_all, N0), values(N0), times(0), ALU.mult))
            then(dve.tensor_tensor(heads(spare, slice(0, SEQ_TILES)), values(N0), times(1), ALU.mult))
            then(dve.tensor_tensor(heads(o_all, N1), values(N1), times(2), ALU.mult))
            settle()
            then(dve.tensor_tensor(o_all[:, N1, :], o_all[:, N1, :], spare[:, :, :], ALU.add))
            settle()

    for s in (feat_ready, vq_ready, f_copied):
        s.passed(TILES)
    f_ready.passed(2)
    chain.passed(1 + 2 * 3 + 1 + 3 * 2 + 4)


def stage_lora_route(core, xT, weights, lowT, picksT, gate):
    nc = core.nc
    low_ready = core.semaphore("lora_low_rank_ready")
    low_copied = core.semaphore("lora_low_rank_copied")
    products_ready = core.semaphore("lora_gate_products_ready")
    logits_ready = core.semaphore("lora_logits_ready")
    step = core.semaphore("lora_route_step")
    exp_ready = core.semaphore("lora_exp_ready")
    picked = core.semaphore("lora_picked")
    turned = core.semaphore("lora_picks_turned")
    copied = core.semaphore("lora_picks_copied")
    rank = field(core.const, CONST, "rank")
    with ExitStack() as ctx:
        def sb(name, shape, dt=F32):
            return core.sbuf(ctx, name, shape, dt)

        logits_ps = core.psum(ctx, "logits_ps", [P, CW])
        low_ps = core.psum(ctx, "low_ps", [P, CHUNKS, CW])
        turned_ps = core.psum(ctx, "turned_ps", [P, CW])
        scores = sb("scores", [P, TILES, EXPERTS])
        top = sb("top", [P, TILES])
        left = sb("left", [P, TILES, EXPERTS])
        equal = sb("equal", [P, TILES, EXPERTS])
        order = sb("order", [P, TILES])
        picks = sb("picks", [P, 2, TILES, EXPERTS])
        moves = sb("moves", [P, 2, TILES * EXPERTS], BF16)
        best = sb("best", [P, 2, TILES])
        block = ctx.enter_context(nc.Block())
        wide = [P, TILES, EXPERTS]
        a_gate = field(weights, W_LORA, "a_gate")

        @block.tensor
        def _(pe):
            for t in range(TILES):
                last = pe.matmul(logits_ps[:, t * EXPERTS:(t + 1) * EXPERTS], xT[:, t * P:(t + 1) * P],
                                 a_gate[:, P:P + EXPERTS], start=True, stop=True)
            last.then_inc(products_ready.sem, 1)
            for c in range(CHUNKS):
                pe.matmul(low_ps[:, c, :], a_gate[:, 0:P], xT[:, c * CW:(c + 1) * CW],
                          start=True, stop=True).then_inc(low_ready.sem, 1)
            pe.wait_ge(picked.sem, picked.at(1))
            out = turned_ps[:, 0:P].bitcast(BF16)
            for i in range(2):
                last = pe.transpose(out[:, i * P:(i + 1) * P], moves[:, i, :], field(core.masks, MASKS, "ident"))
            last.then_inc(turned.sem, 1)

        @block.scalar
        def _(act):
            act.wait_ge(logits_ready.sem, logits_ready.at(1))
            act.activation(scores[:, :, :], scores[:, :, :], ACT.Exp).then_inc(exp_ready.sem, 1)
            for c in range(CHUNKS):
                act.wait_ge(low_ready.sem, low_ready.at(c + 1))
                act.copy(lowT[:, c * CW:(c + 1) * CW], low_ps[:, c, :]).then_inc(low_copied.sem, 1)
            act.wait_ge(turned.sem, turned.at(1))
            act.copy(picksT[:, :, :].rearrange("p i n -> p (i n)"),
                     turned_ps[:, 0:P].bitcast(BF16)).then_inc(copied.sem, 1)

        @block.vector
        def _(dve):
            n = [0]

            def then(ins):
                ins.then_inc(step.sem, 1)
                n[0] += 1
                dve.wait_ge(step.sem, step.at(n[0]))

            dve.wait_ge(products_ready.sem, products_ready.at(1))
            then(dve.tensor_tensor(scores[:, :, :],
                                   logits_ps[:, 0:TILES * EXPERTS].rearrange("p (t e) -> p t e", e=EXPERTS),
                                   field(weights, W_LORA, "gate_b")[:, None, :].to_broadcast(wide), ALU.add))
            then(dve.tensor_reduce(top[:, :], scores[:, :, :], AX.X, ALU.max))
            dve.tensor_tensor(scores[:, :, :], scores[:, :, :], top[:, :, None].to_broadcast(wide),
                              ALU.subtract).then_inc(logits_ready.sem, 1)
            dve.wait_ge(exp_ready.sem, exp_ready.at(1))
            then(dve.tensor_reduce(top[:, :], scores[:, :, :], AX.X, ALU.add))
            then(dve.reciprocal(top[:, :], top[:, :]))
            then(dve.tensor_tensor(scores[:, :, :], scores[:, :, :], top[:, :, None].to_broadcast(wide), ALU.mult))
            step.before += n[0]
            top_two(dve, step, scores[:, :, :], rank, picks, best, (left[:, :, :], equal[:, :, :], order[:, :]))
            step.before -= n[0]
            first = picks[:, 0, :, :].rearrange("p t e -> p (t e)")
            dve.tensor_copy(moves[:, 0, :], first)
            dve.tensor_tensor(moves[:, 1, :], picks[:, 1, :, :].rearrange("p t e -> p (t e)"), first,
                              ALU.subtract).then_inc(picked.sem, 1)
            dve.tensor_tensor(gate[:, :], best[:, 0, :], best[:, 1, :], ALU.add)

    low_ready.passed(CHUNKS)
    low_copied.passed(CHUNKS)
    step.passed(5 + TOP_TWO_STEPS)
    for s in (products_ready, logits_ready, exp_ready, picked, turned, copied):
        s.passed(1)


def stage_lora(core, x, xT, weights, lowT, picksT, spread, gate):
    nc = core.nc
    spread_ready = core.semaphore("lora_spread_picks_ready")
    chosen_ready = core.semaphore("lora_chosen_rows_ready")
    first_ready = core.semaphore("lora_first_hidden_ready")
    first_relu = core.semaphore("lora_first_relu_ready")
    second_ready = core.semaphore("lora_second_hidden_ready")
    second_relu = core.semaphore("lora_second_relu_ready")
    sum_ready = core.semaphore("lora_relu_sum_ready")
    out_ready = core.semaphore("lora_out_ready")
    added = core.semaphore("lora_added")
    F = FF_BLOCKS
    LAST = CHUNKS - 1
    with ExitStack() as ctx:
        hidden_ps = core.psum(ctx, "hidden_ps", [P, F, CW])
        out_ps = core.psum(ctx, "out_ps", [P, CW])
        spread_ps = core.psum(ctx, "spread_ps", [P, 2, CW])
        chosen = core.sbuf(ctx, "chosen", [P, 2, TOKENS])
        relu = core.sbuf(ctx, "relu", [P, 2, 2, CW])
        both = core.sbuf(ctx, "both", [P, 2, CW])
        block = ctx.enter_context(nc.Block())

        @block.tensor
        def _(pe):
            def choose(c, first=False):
                if not first:
                    pe.wait_ge(chosen_ready.sem, c + chosen_ready.at(0))
                for i in range(2):
                    for j in range(CHUNK):
                        last = pe.matmul(spread_ps[:, i, j * P:(j + 1) * P],
                                         spread[:, bass.ds((c * CHUNK + j) * P, P)], picksT[:, i, :],
                                         start=True, stop=True)
                last.then_inc(spread_ready.sem, 1)

            def up_first(c, m):
                c, m = (c, m) if m < F else (c + 1, m - F)
                pe.wait_ge(second_relu.sem, c * F + second_relu.at(m + 1))
                pe.matmul(hidden_ps[:, m, :], field(weights, W_LORA, "wi")[:, m * P:(m + 1) * P],
                          xT[:, bass.ds(c * CW, CW)], start=True, stop=False)
                if m == 0:
                    pe.wait_ge(chosen_ready.sem, c + chosen_ready.at(1))
                pe.matmul(hidden_ps[:, m, :], field(weights, W_LORA, "b")[:, m * P:(m + 1) * P],
                          chosen[:, 0, bass.ds(c * CW, CW)], start=False, stop=True).then_inc(first_ready.sem, 1)

            def up_second(c, m):
                c, m = (c, m) if m < F else (c + 1, m - F)
                pe.wait_ge(first_relu.sem, c * F + first_relu.at(m + 1))
                pe.matmul(hidden_ps[:, m, :], field(weights, W_LORA, "b")[:, m * P:(m + 1) * P],
                          chosen[:, 1, bass.ds(c * CW, CW)], start=False, stop=True,
                          skip_group_check=True).then_inc(second_ready.sem, 1)

            def down(c, m):
                pe.wait_ge(sum_ready.sem, c * F + sum_ready.at(m + 3))
                if m == 0:
                    pe.wait_ge(added.sem, c + added.at(1))
                    pe.matmul(out_ps[:, :], core.twos[0:1, :],
                              field(weights, W_LORA, "bo")[0:1, None, :].to_broadcast([1, CHUNK, P]),
                              start=True, stop=False, skip_group_check=True)
                for j in range(CHUNK):
                    last = pe.matmul(out_ps[:, j * P:(j + 1) * P], both[:, m % 2, j * P:(j + 1) * P],
                                     field(weights, W_LORA, "wo")[:, m * P:(m + 1) * P],
                                     start=False, stop=m == F - 1, skip_group_check=True)
                last.then_inc(out_ready.sem, 1)

            def chunk(c, last=False):
                for m in range(F):
                    if m == 0 and not last:
                        choose(c + 1)
                    if m + 2 < F or not last:
                        up_first(c, m + 2)
                    if m + 1 < F or not last:
                        up_second(c, m + 1)
                    down(c, m)

            choose(0, True)
            up_first(0, 0)
            up_first(0, 1)
            up_second(0, 0)
            with pe.Fori(0, LAST) as c:
                chunk(c)
            chunk(LAST, True)

        @block.scalar
        def _(act):
            act.sem_inc(second_relu.sem, F)

            def relu_first(c, m):
                act.wait_ge(first_ready.sem, c * F + first_ready.at(m + 1))
                act.wait_ge(sum_ready.sem, c * F + sum_ready.at(m + 1))
                act.activation(relu[:, m % 2, 0, :], hidden_ps[:, m % F, :], ACT.Relu,
                               bias=field(weights, W_LORA, "bi")[:, m % F:m % F + 1]).then_inc(first_relu.sem, 1)

            def relu_second(c, m):
                act.wait_ge(second_ready.sem, c * F + second_ready.at(m + 1))
                act.activation(relu[:, m % 2, 1, :], hidden_ps[:, m % F, :], ACT.Relu,
                               bias=field(weights, W_LORA, "bi")[:, m % F:m % F + 1]).then_inc(second_relu.sem, 1)

            relu_first(0, 0)
            relu_first(0, 1)
            relu_second(0, 0)
            with act.Fori(0, LAST) as c:
                for m in range(F):
                    relu_first(c, m + 2)
                    relu_second(c, m + 1)
            for m in range(F):
                if m + 2 < F:
                    relu_first(LAST, m + 2)
                if m + 1 < F:
                    relu_second(LAST, m + 1)

        @block.vector
        def _(dve):
            dve.sem_inc(sum_ready.sem, 2)
            dve.sem_inc(added.sem, 1)

            def choose(c):
                dve.wait_ge(spread_ready.sem, c + spread_ready.at(1))
                for i in range(2):
                    last = dve.tensor_tensor(chosen[:, i, bass.ds(c * CW, CW)], spread_ps[:, i, :], lowT[:, bass.ds(c * CW, CW)],
                                             ALU.mult)
                last.then_inc(chosen_ready.sem, 1)

            def sum_of(c, m, first=False):
                dve.wait_ge(second_relu.sem, c * F + second_relu.at(F + m + 1))
                if not first:
                    dve.wait_ge(out_ready.sem, c * F + out_ready.at(m - 1))
                dve.tensor_tensor(both[:, m % 2, :], relu[:, m % 2, 0, :], relu[:, m % 2, 1, :],
                                  ALU.add).then_inc(sum_ready.sem, 1)

            def add(c):
                dve.wait_ge(out_ready.sem, c * F + out_ready.at(F))
                for j in range(CHUNK):
                    t = c * CHUNK + j
                    xt = x[:, bass.ds(t, 1), :].rearrange("p o d -> p (o d)")
                    last = dve.scalar_tensor_tensor(xt, out_ps[:, j * P:(j + 1) * P],
                                                    gate[:, bass.ds(t, 1)], xt, ALU.mult, ALU.add)
                last.then_inc(added.sem, 1)

            def chunk(c, first=False, last=False):
                sum_of(c, 0, first)
                if not first:
                    add(c - 1)
                if not last:
                    choose(c + 1)
                sum_of(c, 1, first)
                for m in range(2, F):
                    sum_of(c, m)

            choose(0)
            chunk(0, first=True)
            with dve.Fori(1, LAST) as c:
                chunk(c)
            chunk(LAST, last=True)
            add(LAST)

    for s in (spread_ready, chosen_ready):
        s.passed(CHUNKS)
    for s in (first_ready, first_relu, second_ready, out_ready):
        s.passed(CHUNKS * F)
    second_relu.passed(F + CHUNKS * F)
    sum_ready.passed(2 + CHUNKS * F)
    added.passed(1 + CHUNKS)


def program(nc, x_in, const_in, masks_in, rows_q, rows_rot, rows_ali, w_rot, w_moe, w_pair, w_rec, w_ali,
            w_lora, out):
    with ExitStack() as ctx:
        core = Core(nc, ctx)

        def sb(name, shape, dt=F32):
            return core.sbuf(ctx, name, shape, dt)

        x = sb("x", [P, TILES, P])
        core.const = sb("const", [P, CONST_W])
        core.masks = sb("masks", [P, MASKS_W], BF16)
        core.ident = field(core.const, CONST, "ident")
        core.ones = sb("ones", [P, P])
        core.twos = sb("twos", [P, P])
        x_view = x_in.rearrange("b (t p) d -> p (b t) d", p=P)
        out_view = out.rearrange("b (t p) d -> p (b t) d", p=P)

        def long_attention(weights, places, rotary, scale, k_rows, bo, shift, loads=()):
            with ExitStack() as outer:
                xT = core.sbuf(outer, "xT", [P, TOKENS])
                o_tok = xT[:, :].rearrange("p (t g f) -> p t g f", g=GROUPS, t=SEQ_TILES)
                with ExitStack() as inner:
                    q_stack = core.sbuf(inner, "q_stack", [P, ALL_HEADS * SEQ], BF16)
                    k_stack = core.sbuf(inner, "k_stack", [P, ALL_HEADS * SEQ], BF16)
                    parts = nc.dram_tensor("parts_rot" if rotary else "parts_ali", [6, P, TOKENS], BF16,
                                           kind="Internal")
                    stacks = Stacks(q_stack, k_stack, parts, rows_q, k_rows)
                    v_tok = core.sbuf(inner, "v_tok", [P, ALL_HEADS, SEQ_TILES, DH + 1])

                    def zero_first_half(pool):
                        for stack in (q_stack, k_stack):
                            pool.memset(stack[0:STACKED, 0:HALF].bitcast(F32), 0.0)

                    stage_norm(core, x, 1e-5, xT=xT, loads=loads, meanwhile=zero_first_half)
                    stage_operands(core, xT, weights, rotary, scale, stacks, v_tok)
                    stage_attend(core, rotary, stacks, v_tok, o_tok)
                stage_project(core, x, field(weights, places, "out"), o_tok=o_tok, bo=bo, shift=shift)

        def experts():
            with ExitStack() as inner:
                moe = core.sbuf(inner, "moe", [P, W_MOE_W])
                xT = core.sbuf(inner, "xT", [P, TOKENS])
                stage_norm(core, x, 1e-5, xT=xT, loads=[(moe[:, :], w_moe)])
                stage_experts(core, x, xT, moe)

        def pair():
            with ExitStack() as inner:
                weights = core.sbuf(inner, "w_pair", [P, W_PAIR_W])
                once = core.sbuf(inner, "normed_once", [P, TILES, P])
                xT = core.sbuf(inner, "xT", [P, TOKENS])
                stage_norm(core, x, 1e-5, token_major=once, loads=[(weights[:, :], w_pair)])
                stage_norm(core, once, 1e-6, xT=xT, affine=(field(weights, W_PAIR, "ln_scale"),
                                                            field(weights, W_PAIR, "ln_bias")))
                stage_pair(core, x, xT, weights)

        def recurrence():
            with ExitStack() as inner:
                xT = core.sbuf(inner, "xT", [P, TOKENS])
                o_all = core.sbuf(inner, "o_all", [P, TILES, P])
                rec = core.sbuf(inner, "rec", [P, W_REC_W])
                stage_norm(core, x, 1e-5, xT=xT, loads=[(rec[:, :], w_rec)])
                stage_recurrence(core, xT, rec, o_all)
                stage_project(core, x, field(rec, W_REC, "out"), o_all=o_all)

        def lora():
            with ExitStack() as inner:
                weights = core.sbuf(inner, "w_lora", [P, W_LORA_W])
                xT = core.sbuf(inner, "xT", [P, TOKENS])
                lowT = core.sbuf(inner, "lowT", [P, TOKENS])
                picksT = core.sbuf(inner, "picksT", [P, 2, P], BF16)
                spread = core.sbuf(inner, "spread", [P, TILES * P], BF16)
                gate = core.sbuf(inner, "gate", [P, TILES])

                def spread_ident(pool):
                    pool.tensor_copy(spread[:, :].rearrange("p (q r) -> p q r", r=RANK),
                                     field(core.masks, MASKS, "ident")[:, :, None].to_broadcast([P, P, RANK]))

                stage_norm(core, x, 1e-5, xT=xT, loads=[(weights[:, :], w_lora)], meanwhile=spread_ident)
                stage_lora_route(core, xT, weights, lowT, picksT, gate)
                stage_lora(core, x, xT, weights, lowT, picksT, spread, gate)

        with ExitStack() as first:
            rot = core.sbuf(first, "rot", [P, W_ROT_W])
            stage_load(core, [(x[:, :, :], x_view), (core.const[:, :], const_in), (core.masks[:, :], masks_in),
                              (rot[:, :], w_rot)])
            ones_set = core.semaphore("ones_set")
            with nc.Block() as block:
                @block.vector
                def _(dve):
                    dve.memset(core.ones[:, :], 1.0)
                    dve.memset(core.twos[:, :], 2.0).then_inc(ones_set.sem, 1)
            if STAGES >= 1:
                long_attention(rot, W_ROT, True, DH ** -0.5, rows_rot, field(rot, W_ROT, "bo"), CTX)
        if STAGES >= 2:
            experts()
        if STAGES >= 3:
            pair()
        if STAGES >= 4:
            experts()
        if STAGES >= 5:
            recurrence()
        if STAGES >= 6:
            lora()
        if STAGES >= 7:
            with ExitStack() as inner:
                ali = core.sbuf(inner, "ali", [P, W_ALI_W])
                long_attention(ali, W_ALI, False, DH ** -0.5, rows_ali, None, 0, loads=[(ali[:, :], w_ali)])
        if STAGES >= 8:
            lora()
        stored = core.semaphore("x_stored")
        with nc.Block() as block:
            @block.sync
            def _(sp):
                sp.dma_start(out_view, x[:, :, :]).then_inc(stored.sem, 16)
                sp.wait_ge(stored.sem, 16)



def _pack(np, places, width, **arrays):
    out = np.zeros((P, width), np.float32)
    for name, a in arrays.items():
        at, n = places[name]
        out[:, at:at + n] = a
    return out


def kernel(**inputs):
    import numpy as np
    import concourse.bacc as bacc
    from concourse import mybir as _mybir
    from concourse.bass_utils import run_bass_kernel_spmd

    a = {k: np.ascontiguousarray(v) for k, v in inputs.items()}
    bf16 = np.dtype(_mybir.dt.np(BF16)) if hasattr(_mybir.dt, "np") else np.dtype("bfloat16")

    def rows(v):
        return np.broadcast_to(v.reshape(1, -1), (P, v.size))

    def blocks(w):
        return w.reshape(-1, P, w.shape[1]).transpose(1, 0, 2).reshape(P, -1)

    n = np.arange(SEQ, dtype=np.float32)
    inv_freq = (1.0 / 10000.0 ** (np.arange(0, DH, 2, dtype=np.float32) / DH)).astype(np.float32)
    freqs = n[:, None] * inv_freq[None, :]
    cos = np.cos(np.concatenate([freqs, freqs], -1))
    sin = np.sin(freqs)
    sin = np.concatenate([-sin, sin], -1)

    def by_tile(t):
        return t.reshape(SEQ_TILES, P, DH).transpose(1, 0, 2).reshape(P, -1)

    const = _pack(np, CONST, CONST_W, ident=np.eye(P), cos=by_tile(cos), sin=by_tile(sin),
                  rank=rows(np.arange(EXPERTS, 0, -1)))
    i = np.arange(P)
    hidden = -1e30
    causal = np.where(i[None, :] > i[:, None], hidden, 0)
    rot_01 = np.where(rows(i) >= CTX - P, hidden, 0)
    rot_11 = np.where((i[None, :] >= CTX - P) & (i[None, :] > i[:, None]), hidden, 0)
    masks = _pack(np, MASKS, MASKS_W, ident=np.eye(P), diag=causal, rot_01=rot_01, rot_11=rot_11,
                  diag_T=causal.T, rot_T=np.concatenate([rot_01.T, rot_11.T], 1)).astype(bf16)
    start = 2.0 ** -0.5
    slopes = np.array([start * start ** h for h in range(HEADS)], np.float32)
    bias = slopes[:, None] * n[None, :]
    parts = []
    for _ in range(3):
        part = bias.astype(bf16)
        parts.append(np.tile(part.reshape(1, -1), (1, BATCH)))
        bias = bias - part.astype(np.float32)
    ones = np.ones((3, ALL_HEADS * SEQ), bf16)
    rows_ali = np.concatenate(parts + [ones])
    rows_rot = np.concatenate([np.zeros((3, ALL_HEADS * SEQ), bf16), ones])

    qkv = a["L0_attn_b_qkv_kernel"]
    pair_v = qkv[:, 2]
    w_attn = a["L1_attn_b_w_attn"]
    arrays = {
        "x": a["L0_attn_a_x"], "const": const, "masks": masks, "rows_q": ones, "rows_rot": rows_rot,
        "rows_ali": rows_ali,
        "w_rot": _pack(np, W_ROT, W_ROT_W, qkv=np.concatenate([a["L0_attn_a_Wq"].T, a["L0_attn_a_Wkv"].T], 1),
                       out=a["L0_attn_a_Wo"].T, bo=rows(a["L0_attn_a_bo"]), ln_g=rows(a["L0_attn_a_ln_g"]),
                       ln_b=rows(a["L0_attn_a_ln_b"])),
        "w_moe": _pack(np, W_MOE, W_MOE_W, router=a["L0_ffn_router_w"].T, w1=a["L0_ffn_w1"],
                       w2=blocks(a["L0_ffn_w2"])),
        "w_pair": _pack(np, W_PAIR, W_PAIR_W, q=qkv[:, 0], k=qkv[:, 1], v=pair_v, v_T=blocks(pair_v.T),
                        out=blocks(a["L0_attn_b_out_kernel"]), ln_scale=a["L0_attn_b_ln_scale"][:, None],
                        ln_bias=a["L0_attn_b_ln_bias"][:, None]),
        "w_rec": _pack(np, W_REC, W_REC_W, **{"in": a["L1_attn_a_W_in"], "out": a["L1_attn_a_W_out"],
                                              "lower": rows(a["L1_attn_a_lower_bound"])}),
        "w_ali": _pack(np, W_ALI, W_ALI_W, q=w_attn[0:P].T, k=w_attn[P:2 * P].T, v=w_attn[2 * P:3 * P].T,
                       out=a["L1_attn_b_w_proj"].T),
        "w_lora": _pack(np, W_LORA, W_LORA_W, wi=a["L1_ffn_wi"].T, wo=blocks(a["L1_ffn_wo"].T),
                        a_gate=np.concatenate([a["L1_ffn_lora_A"].reshape(-1, P).T, a["L1_ffn_gate_w"].T], 1),
                        b=a["L1_ffn_lora_B"].transpose(0, 2, 1).reshape(P, FF),
                        bi=a["L1_ffn_bi"].reshape(FF_BLOCKS, P).T, gate_b=rows(a["L1_ffn_gate_b"]),
                        bo=rows(a["L1_ffn_bo"])),
    }
    nc = bacc.Bacc("TRN2", target_bir_lowering=False, num_devices=1)
    args, maps = [], {}
    for name, v in arrays.items():
        maps[name] = v
        args.append(nc.dram_tensor(name, v.shape, _mybir.dt.from_np(v.dtype), kind="ExternalInput").ap())
    args.append(nc.dram_tensor("y", (BATCH, SEQ, P), F32, kind="ExternalOutput").ap())
    program(nc, *args)
    r = run_bass_kernel_spmd(nc, [maps], core_ids=[0])
    return r.results[0]["y"]
```
